# Optimizing a Trainium2 kernel written in Bass

```python
import numpy as np
import jax
import jax.numpy as jnp

def _softmax(x, axis=-1):
    return jax.nn.softmax(x, axis=axis)

def _gelu(x):
    return jax.nn.gelu(x, approximate=True)

def _silu(x):
    return jax.nn.silu(x)

def _sigmoid(x):
    return jax.nn.sigmoid(x)

def _layernorm(x, axis=-1, eps=1e-05):
    m = jnp.mean(x, axis=axis, keepdims=True)
    v = jnp.var(x, axis=axis, keepdims=True)
    return (x - m) / jnp.sqrt(v + eps)

def _scatter_add(tgt, idx, src, axis=0):
    return tgt.at[idx].add(src)

def _segment_sum(src, seg, n):
    return jax.ops.segment_sum(src, seg, n)
kernel_name = 'mk_sandwich_d1_jaxref_r8_f3b1ac'

def setup_inputs(seed: int=0):
    np.random.seed(seed)
    _w = jnp.asarray

    def _L0_attn_setup():
        import jax, jax.numpy as jnp
        import numpy as np
        from jax import lax
        H = 64
        P = 64
        N = 128
        G = 8
        K = 4
        D_MODEL = 512
        I = H * P
        GN = G * N
        CONV_DIM = I + 2 * GN
        PROJ = I + CONV_DIM + H
        EPS = 1e-05
        GROUP_SIZE = I // G

        def _reference_tuple_inner(hidden_states, in_proj_w, conv_weight, conv_bias, dt_bias, A_log, D, norm_weight, out_proj_w):
            B, L, _ = hidden_states.shape
            proj = jnp.einsum('bld,pd->blp', hidden_states, in_proj_w)
            gate = proj[..., :I]
            hbc = proj[..., I:I + CONV_DIM]
            dt = proj[..., -H:]
            pad = jnp.pad(hbc, ((0, 0), (K - 1, 0), (0, 0)))
            conv = conv_bias
            for k in range(K):
                conv = conv + pad[:, k:k + L, :] * conv_weight[:, k]
            xBC = jax.nn.silu(conv)
            x = xBC[..., :I].reshape(B, L, H, P)
            Bm = xBC[..., I:I + GN].reshape(B, L, G, N)
            Cm = xBC[..., I + GN:].reshape(B, L, G, N)
            hpg = H // G
            B_h = jnp.repeat(Bm, hpg, axis=2)
            C_h = jnp.repeat(Cm, hpg, axis=2)
            dt_p = jax.nn.softplus(dt + dt_bias)
            A = -jnp.exp(A_log)
            dA = jnp.exp(dt_p * A)
            dtx = dt_p[..., None] * x

            def step(state, inp):
                dA_t, dtx_t, B_t, C_t = inp
                state = state * dA_t[..., None, None] + dtx_t[..., None] * B_t[:, :, None, :]
                y_t = jnp.einsum('bhpn,bhn->bhp', state, C_t)
                return (state, y_t)
            xs = (jnp.moveaxis(dA, 1, 0), jnp.moveaxis(dtx, 1, 0), jnp.moveaxis(B_h, 1, 0), jnp.moveaxis(C_h, 1, 0))
            state0 = jnp.zeros((B, H, P, N), jnp.float32)
            final_state, ys = lax.scan(step, state0, xs)
            y = jnp.moveaxis(ys, 0, 1) + x * D[None, None, :, None]
            y = y.reshape(B, L, I)
            yg = y.reshape(B, L, G, GROUP_SIZE)
            var = jnp.mean(yg * yg, axis=-1, keepdims=True)
            yn = (yg * lax.rsqrt(var + EPS)).reshape(B, L, I) * norm_weight
            yn = yn * jax.nn.silu(gate)
            out = jnp.einsum('bli,di->bld', yn, out_proj_w)
            conv_state_new = jnp.moveaxis(hbc[:, L - (K - 1):, :], 1, 2)
            return (out, conv_state_new, final_state)
        key = jax.random.key(seed)
        ks = jax.random.split(key, 6)
        B, L = (2, 256)
        s = 0.02
        return {'hidden_states': jax.random.normal(ks[0], (B, L, D_MODEL), jnp.float32), 'in_proj_w': jax.random.normal(ks[1], (PROJ, D_MODEL), jnp.float32) * s, 'conv_weight': jax.random.normal(ks[2], (CONV_DIM, K), jnp.float32) * s, 'conv_bias': jnp.zeros((CONV_DIM,), jnp.float32), 'dt_bias': jnp.ones((H,), jnp.float32), 'A_log': jnp.log(jnp.arange(1, H + 1, dtype=jnp.float32)), 'D': jnp.ones((H,), jnp.float32), 'norm_weight': jnp.ones((I,), jnp.float32), 'out_proj_w': jax.random.normal(ks[3], (D_MODEL, I), jnp.float32) * s}
    _L0_attn_in = _L0_attn_setup()

    def _L0_ffn_setup():
        import jax, jax.numpy as jnp
        import numpy as np
        H = 512
        I = 1792
        G = 128

        def dequant(q, s, g=G):
            O, In = q.shape
            return (q.reshape(O, In // g, g).astype(s.dtype) * s[:, :, None]).reshape(O, In)
        key = jax.random.key(seed)
        ks = jax.random.split(key, 7)
        x = jax.random.normal(ks[0], (2, 256, H), dtype=jnp.float32)

        def mk_qlinear(kq, ksc, out_d, in_d):
            q = jax.random.randint(kq, (out_d, in_d), -8, 8, dtype=jnp.int32)
            s = jax.random.uniform(ksc, (out_d, in_d // G), dtype=jnp.float32, minval=0.005, maxval=0.02)
            return (q, s)
        gate_q, gate_s = mk_qlinear(ks[1], ks[2], I, H)
        up_q, up_s = mk_qlinear(ks[3], ks[4], I, H)
        down_q, down_s = mk_qlinear(ks[5], ks[6], H, I)
        return {'x': x, 'gate_q': gate_q, 'gate_s': gate_s, 'up_q': up_q, 'up_s': up_s, 'down_q': down_q, 'down_s': down_s}
    _L0_ffn_in = _L0_ffn_setup()
    _d = {'L0_attn_hidden_states': _L0_attn_in['hidden_states'], 'L0_attn_in_proj_w': _L0_attn_in['in_proj_w'], 'L0_attn_conv_weight': _L0_attn_in['conv_weight'], 'L0_attn_conv_bias': _L0_attn_in['conv_bias'], 'L0_attn_dt_bias': _L0_attn_in['dt_bias'], 'L0_attn_A_log': _L0_attn_in['A_log'], 'L0_attn_D': _L0_attn_in['D'], 'L0_attn_norm_weight': _L0_attn_in['norm_weight'], 'L0_attn_out_proj_w': _L0_attn_in['out_proj_w'], 'L0_ffn_gate_q': _L0_ffn_in['gate_q'], 'L0_ffn_gate_s': _L0_ffn_in['gate_s'], 'L0_ffn_up_q': _L0_ffn_in['up_q'], 'L0_ffn_up_s': _L0_ffn_in['up_s'], 'L0_ffn_down_q': _L0_ffn_in['down_q'], 'L0_ffn_down_s': _L0_ffn_in['down_s']}
    _x0 = _d['L0_attn_hidden_states']
    _d['L0_attn_hidden_states'] = jax.random.normal(jax.random.fold_in(jax.random.key(seed), 1), (2, 512, 512), dtype=_x0.dtype)
    del _x0
    return _d

def reference(L0_attn_hidden_states, L0_attn_in_proj_w, L0_attn_conv_weight, L0_attn_conv_bias, L0_attn_dt_bias, L0_attn_A_log, L0_attn_D, L0_attn_norm_weight, L0_attn_out_proj_w, L0_ffn_gate_q, L0_ffn_gate_s, L0_ffn_up_q, L0_ffn_up_s, L0_ffn_down_q, L0_ffn_down_s):

    def _L0_attn_ref(hidden_states, in_proj_w, conv_weight, conv_bias, dt_bias, A_log, D, norm_weight, out_proj_w):
        import jax, jax.numpy as jnp
        import numpy as np
        from jax import lax
        H = 64
        P = 64
        N = 128
        G = 8
        K = 4
        D_MODEL = 512
        I = H * P
        GN = G * N
        CONV_DIM = I + 2 * GN
        PROJ = I + CONV_DIM + H
        EPS = 1e-05
        GROUP_SIZE = I // G

        def _reference_tuple_inner(hidden_states, in_proj_w, conv_weight, conv_bias, dt_bias, A_log, D, norm_weight, out_proj_w):
            B, L, _ = hidden_states.shape
            proj = jnp.einsum('bld,pd->blp', hidden_states, in_proj_w)
            gate = proj[..., :I]
            hbc = proj[..., I:I + CONV_DIM]
            dt = proj[..., -H:]
            pad = jnp.pad(hbc, ((0, 0), (K - 1, 0), (0, 0)))
            conv = conv_bias
            for k in range(K):
                conv = conv + pad[:, k:k + L, :] * conv_weight[:, k]
            xBC = jax.nn.silu(conv)
            x = xBC[..., :I].reshape(B, L, H, P)
            Bm = xBC[..., I:I + GN].reshape(B, L, G, N)
            Cm = xBC[..., I + GN:].reshape(B, L, G, N)
            hpg = H // G
            B_h = jnp.repeat(Bm, hpg, axis=2)
            C_h = jnp.repeat(Cm, hpg, axis=2)
            dt_p = jax.nn.softplus(dt + dt_bias)
            A = -jnp.exp(A_log)
            dA = jnp.exp(dt_p * A)
            dtx = dt_p[..., None] * x

            def step(state, inp):
                dA_t, dtx_t, B_t, C_t = inp
                state = state * dA_t[..., None, None] + dtx_t[..., None] * B_t[:, :, None, :]
                y_t = jnp.einsum('bhpn,bhn->bhp', state, C_t)
                return (state, y_t)
            xs = (jnp.moveaxis(dA, 1, 0), jnp.moveaxis(dtx, 1, 0), jnp.moveaxis(B_h, 1, 0), jnp.moveaxis(C_h, 1, 0))
            state0 = jnp.zeros((B, H, P, N), jnp.float32)
            final_state, ys = lax.scan(step, state0, xs)
            y = jnp.moveaxis(ys, 0, 1) + x * D[None, None, :, None]
            y = y.reshape(B, L, I)
            yg = y.reshape(B, L, G, GROUP_SIZE)
            var = jnp.mean(yg * yg, axis=-1, keepdims=True)
            yn = (yg * lax.rsqrt(var + EPS)).reshape(B, L, I) * norm_weight
            yn = yn * jax.nn.silu(gate)
            out = jnp.einsum('bli,di->bld', yn, out_proj_w)
            conv_state_new = jnp.moveaxis(hbc[:, L - (K - 1):, :], 1, 2)
            return (out, conv_state_new, final_state)
        return _reference_tuple_inner(hidden_states, in_proj_w, conv_weight, conv_bias, dt_bias, A_log, D, norm_weight, out_proj_w)[0]

    def _L0_ffn_ref(x, gate_q, gate_s, up_q, up_s, down_q, down_s):
        import jax, jax.numpy as jnp
        import numpy as np
        H = 512
        I = 1792
        G = 128

        def dequant(q, s, g=G):
            O, In = q.shape
            return (q.reshape(O, In // g, g).astype(s.dtype) * s[:, :, None]).reshape(O, In)
        Wg = dequant(gate_q, gate_s)
        Wu = dequant(up_q, up_s)
        Wd = dequant(down_q, down_s)
        gate_score = jax.nn.silu(jnp.einsum('bsh,ih->bsi', x, Wg))
        intermediate = gate_score * jnp.einsum('bsh,ih->bsi', x, Wu)
        return jnp.einsum('bsi,hi->bsh', intermediate, Wd)
    x = L0_attn_hidden_states
    x = x + _layernorm(_L0_attn_ref(_layernorm(x, axis=-1), L0_attn_in_proj_w, L0_attn_conv_weight, L0_attn_conv_bias, L0_attn_dt_bias, L0_attn_A_log, L0_attn_D, L0_attn_norm_weight, L0_attn_out_proj_w), axis=-1)
    x = x + _layernorm(_L0_ffn_ref(_layernorm(x, axis=-1), L0_ffn_gate_q, L0_ffn_gate_s, L0_ffn_up_q, L0_ffn_up_s, L0_ffn_down_q, L0_ffn_down_s), axis=-1)
    return x

_drawn_inputs = setup_inputs


def setup_inputs(seed=0):
    import zlib

    import numpy as np

    out = dict(_drawn_inputs(seed))
    spreads = {'L0_attn_conv_bias': (0.0, 0.1),
     'L0_attn_dt_bias': (1.0, 0.2),
     'L0_attn_D': (1.0, 0.2),
     'L0_attn_norm_weight': (1.0, 0.2)}
    factors = {}
    for name, (base, spread) in spreads.items():
        noise = np.random.default_rng([zlib.crc32(name.encode()), seed]).standard_normal(out[name].shape)
        drawn = base * np.exp(spread * noise) if base else spread * noise
        out[name] = jnp.asarray(drawn.astype(out[name].dtype))
    for name, factor in factors.items():
        out[name] = (out[name] * factor).astype(out[name].dtype)
    return out
```

```python
from contextlib import ExitStack

import concourse.bass as bass
from concourse import mybir

F32 = mybir.dt.float32
F32R = mybir.dt.float32r
I32 = mybir.dt.int32
ALU = mybir.AluOpType
ACT = mybir.ActivationFunctionType

P = 128
DM = 512
NB, L = 2, 512
T = NB * L
NH, HD, NS = 64, 64, 128
NG = 8
HG = NH // NG
Q = 128
NC = L // Q
NT = T // Q
KT = DM // P
GW = HG * HD
CT = GW // P
NTILE = 2 + 2 * CT
NCONV = 2 + CT
TAPS = 4
NPAR = NCONV * (TAPS + 1) + 2 * CT
PD, PNW = NCONV * (TAPS + 1), NCONV * (TAPS + 1) + CT
FI = 1792
FT = FI // P
EPS = 1e-5
NU = NB * NG
DT, WE, CUM, DEC = range(4)

SLOTS = [([0], [1]), ([2], [3, 4]), ([5], [6, 7]), ([8], [9])]
SPLIT_AT = [2, 2, 3, 3, 3, 4, 4, 4, 5, 5]


def mixer_and_ffn(nc, x, win, wdt, wo, parg, hpar, consts, gu_q, gu_s, dn_q, dn_s, out):
    cum_dram = nc.dram_tensor("cum_dram", [NG, NT, HG * Q], F32, kind="Internal").ap()
    ecum_dram = nc.dram_tensor("ecum_dram", [NG, NT, 2, CT * Q], F32, kind="Internal").ap()

    with ExitStack() as ctx:
        def sem(name):
            return ctx.enter_context(nc.semaphore(name))

        def sb(name, shape, dt, scope=ctx):
            return scope.enter_context(nc.sbuf_tensor(name, shape, dt))

        xT_hi = sb("xT_hi", [P, KT, T], F32R)
        xT_lo = sb("xT_lo", [P, KT, T], F32R)
        oacc = sb("oacc", [P, NT, DM], F32)
        con = sb("con", [P, 4, P], F32)
        ln_st = sb("ln_st", [P, 32, 6], F32)
        ln_mv = sb("ln_mv", [P, 32, 2], F32)
        ln_ve = sb("ln_ve", [P, 32], F32)
        ln_rs = sb("ln_rs", [P, 32], F32)
        mhalf = sb("mhalf", [P, 1], F32)
        ident, tri, mask4, ones = (con[:, i, :] for i in range(4))
        mix = ExitStack()
        w_hi = sb("w_hi", [P, NTILE, KT, P], F32R, mix)
        w_lo = sb("w_lo", [P, NTILE, KT, P], F32R, mix)
        wo_hi = sb("wo_hi", [P, CT, DM], F32R, mix)
        wo_lo = sb("wo_lo", [P, CT, DM], F32R, mix)
        w_raw = sb("w_raw", [P, 2, KT * P], F32, mix)
        wo_raw = sb("wo_raw", [P, 2, DM], F32, mix)
        xc = sb("xc", [P, NB, NCONV, L], F32, mix)
        gate = sb("gate", [P, NB, CT, L], F32, mix)
        acc = sb("acc", [P, 2, L], F32, mix)
        th = sb("th", [P, L], F32, mix)
        cumb = sb("cumb", [P, 2, HG, Q], F32, mix)
        ecum = sb("ecum", [P, 2, CT, Q], F32, mix)
        em = sb("em", [P, HG, Q], F32, mix)
        smask = sb("smask", [P, Q], F32, mix)
        btok = sb("btok", [P, NS], F32, mix)
        xdt = sb("xdt", [P, HG, HD], F32, mix)
        xw = sb("xw", [P, HG, HD], F32, mix)
        ybuf = sb("ybuf", [P, CT, Q], F32, mix)
        ysq = sb("ysq", [P, CT * Q], F32, mix)
        zbuf = sb("zbuf", [P, CT, Q], F32, mix)
        z_hi = sb("z_hi", [P, CT, Q], F32R, mix)
        z_lo = sb("z_lo", [P, CT, Q], F32R, mix)
        hst = sb("hst", [P, HG, HD], F32, mix)
        hdec = sb("hdec", [P, HG, HD], F32, mix)
        tab = sb("tab", [P, NU, 4, NC, HG], F32, mix)
        cur = sb("cur", [P, NB, 4, NC, HG], F32, mix)
        par = sb("par", [P, NG, NPAR], F32, mix)
        cpar = sb("cpar", [P, NB, NPAR], F32, mix)
        hp = sb("hp", [NH, 4], F32, mix)
        rms = sb("rms", [P, 2], F32, mix)
        mix.close()
        ffn = ExitStack()
        h_hi = sb("h_hi", [P, FT, T], F32R, ffn)
        h_lo = sb("h_lo", [P, FT, T], F32R, ffn)
        f_q = sb("f_q", [P, 2 * DM], I32, ffn)
        f_s = sb("f_s", [P, 2 * DM], F32, ffn)
        f_hi = sb("f_hi", [P, 2, 2 * DM], F32R, ffn)
        f_lo = sb("f_lo", [P, 2, 2 * DM], F32R, ffn)
        f_th = sb("f_th", [P, 2 * NB, L], F32, ffn)
        xin = sb("xin", [P, 2, DM], F32, ffn)
        ffn.close()

        bank = [ctx.enter_context(nc.psum_tensor(f"bank{i}", [P, DM], F32)) for i in range(8)]
        B_OP, B_DH, B_XT, B_S, B_YD, B_YO = bank[2:8]

        s_x = [sem(f"s_x{t}") for t in range(NT)]
        s_con, s_par, s_hp, s_wdt = (sem(n) for n in ("s_con", "s_par", "s_hp", "s_wdt"))
        s_raw = [sem(f"s_raw{i}") for i in range(2)]
        s_woraw = [sem(f"s_woraw{i}") for i in range(2)]
        s_cumb = [sem(f"s_cumb{i}") for i in range(2)]
        s_ecum = [sem(f"s_ecum{i}") for i in range(2)]
        s_scr = sem("s_scr")
        stats, aggr, var_eps, rstd = (sem(n) for n in ("stats", "aggr", "var_eps", "rstd"))
        const_set = sem("const_set")
        normed, xtp, xt_hi_done, xt_lo_done = (sem(n) for n in ("normed", "xtp", "xt_hi_done", "xt_lo_done"))
        wdt_split, dt_mm, pre_pe, pre_act, pre_dve = (
            sem(n) for n in ("wdt_split", "dt_mm", "pre_pe", "pre_act", "pre_dve"))
        ip_done, tap0, taps, th_done, xc_done = (sem(n) for n in ("ip_done", "tap0", "taps", "th_done", "xc_done"))
        tap_step, pre_step = sem("tap_step"), sem("pre_step")
        w_hi_done, w_lo_done, wo_hi_done, wo_lo_done = (
            sem(n) for n in ("w_hi_done", "w_lo_done", "wo_hi_done", "wo_lo_done"))
        cpar_done, cur_done = sem("cpar_done"), sem("cur_done")
        st_done, xt_done, yd_done, yo_done, dh_done, ssq_done, op_done = (
            sem(n) for n in ("st_done", "xt_done", "yd_done", "yo_done", "dh_done", "ssq_done", "op_done"))
        diff_done, e_done, sq_done, z_hi_done = sem("diff_done"), sem("e_done"), sem("sq_done"), sem("z_hi_done")
        sm_done, bt_done, xdt_done, m_done, yl_done, t1_done, y_done, h_done, z_lo_done = (
            sem(n) for n in ("sm_done", "bt_done", "xdt_done", "m_done", "yl_done", "t1_done", "y_done",
                             "h_done", "z_lo_done"))
        ms_done, oacc_done = sem("ms_done"), sem("oacc_done")
        dx_done, xw_done, hd_done, z_done, ysum_half, ysum, r_done = (
            sem(n) for n in ("dx_done", "xw_done", "hd_done", "z_done", "ysum_half", "ysum", "r_done"))
        s_xin = [sem(f"s_xin{i}") for i in range(2)]
        ln1, x2_done, x2n_done, x2tp = (sem(n) for n in ("ln1", "x2_done", "x2n_done", "x2tp"))
        s_fq, s_fs = sem("s_fq"), sem("s_fs")
        f_w, f_hi_done, f_lo_done = sem("f_w"), sem("f_hi_done"), sem("f_lo_done")
        g_mm, u_mm, g_th, g_silu, hbuf_done, h_hi_done, h_lo_done, dn_mm, y_out = (
            sem(n) for n in ("g_mm", "u_mm", "g_th", "g_silu", "hbuf_done", "h_hi_done", "h_lo_done", "dn_mm", "y_out"))
        fin_n, s_out = sem("fin_n"), sem("s_out")

        def wait(eng, s, n):
            if not isinstance(n, int) or n > 0:
                eng.wait_ge(s, n)

        def groups(eng, body):
            body(0)
            with eng.Fori(1, NG - 1) as g:
                body(g)
            body(NG - 1)

        def pairs(eng, body):
            body(0)
            with eng.Fori(1, FT // 2 - 1) as j:
                body(j)
            body(FT // 2 - 1)

        def following(b, c, u, more):
            return (b, c + 1, u) if c < NC - 1 else (1 - b, 0, u + 1) if more else None

        def last_group(g):
            return isinstance(g, int) and g == NG - 1

        def steps(g):
            for b in range(NB):
                for c in range(NC):
                    more = not (b == NB - 1 and last_group(g))
                    yield b, c, g * NB + b, (g * NB + b) * NC + c, more, (g + b), 1 - b

        def cumb_loads(u, c):
            return u * (NC // 2) + c // 2 + 1

        def ecum_loads(u, c):
            return u + 1 if c == 2 else u * 2 + (c + 1) // 2

        def wait_y(eng, u, q, c):
            if c == 0:
                eng.wait_ge(yl_done, q + 1)
            else:
                eng.wait_ge(y_done, u * (NC - 1) + c)

        cumf = cumb[:].rearrange("p s h i -> p (s h i)")
        dt_raw, dt_abs = cumf[0:NH, 0:T], cumf[0:NH, T:2 * T]
        dt_e1 = ecum[:].rearrange("p s k i -> p (s k i)")[0:NH, :]
        dt_ln = em[:].rearrange("p h i -> p (h i)")[0:NH, :]
        dt_h, a_h, cum_h, ecum_h = dt_e1, dt_abs, dt_raw, dt_ln
        a_tok, cum_tok = (v[:].rearrange("p h d -> p (h d)") for v in (xdt, xw))
        diff_tok, w_tok = ysq[:], zbuf[:].rearrange("p k i -> p (k i)")

        block = ctx.enter_context(nc.Block())

        @block.sync
        def _(sp):
            for t in range(NT):
                sp.dma_start(oacc[:, t, :], x[t * P:(t + 1) * P, :]).then_inc(s_x[t], 16)
            sp.dma_start(con[:], consts).then_inc(s_con, 16)
            sp.dma_start(em[:, 0:KT, :], wdt).then_inc(s_wdt, 16)
            sp.dma_start(hp[:, 0:2], hpar).then_inc(s_hp, 16)
            sp.dma_start(par[:], parg).then_inc(s_par, 16)

            def load_w(g, n):
                wait(sp, w_hi_done, g * NTILE + n - 1)
                wait(sp, w_lo_done, g * NTILE + n - 1)
                sp.dma_start(w_raw[:, n % 2, :], win[g, :, n, :]).then_inc(s_raw[n % 2], 16)

            def load_wo(g, k):
                wait(sp, wo_hi_done, g * CT + k - 1)
                wait(sp, wo_lo_done, g * CT + k - 1)
                sp.dma_start(wo_raw[:, k % 2, :], wo[g, :, k, :]).then_inc(s_woraw[k % 2], 16)

            def load_chunk(g, b, c, u, q):
                t = b * NC + c
                wait(sp, e_done, q - 1)
                sp.dma_start(cumb[:, c % 2, :, :].rearrange("p h i -> p (h i)"),
                             cum_dram[g, t, :].unsqueeze(0).broadcast_to([P, HG * Q])).then_inc(s_cumb[c % 2], 16)
                if c > 0:
                    wait(sp, y_done, u * (NC - 1) + (0, 0, -1, 1)[c])
                    for par_ in range(2):
                        sp.dma_start(ecum[par_ * HD:(par_ + 1) * HD, c % 2, :, :].rearrange("p h i -> p (h i)"),
                                     ecum_dram[g, t, par_, :].unsqueeze(0).broadcast_to([HD, CT * Q])
                                     ).then_inc(s_ecum[c % 2], 16)

            for n in range(NTILE):
                load_w(0, n)
            for k in range(2):
                load_wo(0, k)
            sp.wait_ge(pre_dve, 15)
            for g in range(NG):
                sp.dma_start(cum_dram[g].rearrange("t (h i) -> h t i", h=HG),
                             cum_h[g * HG:(g + 1) * HG, :].rearrange("h (t i) -> h t i", t=NT)).then_inc(s_scr, 16)
                for hh in range(2):
                    sp.dma_start(ecum_dram[g, :, hh, :].rearrange("t (h i) -> h t i", h=CT),
                                 ecum_h[g * HG + hh:(g + 1) * HG:2, :].rearrange("h (t i) -> h t i", t=NT)
                                 ).then_inc(s_scr, 16)
            sp.wait_ge(s_scr, 16 * 3 * NG)
            load_chunk(0, 0, 0, 0, 0)
            load_chunk(0, 0, 1, 0, 1)

            def body(g):
                for b, c, u, q, more, gn, bn in steps(g):
                    if c < NC - 2:
                        load_chunk(g, b, c + 2, u, q + 2)
                    elif more:
                        load_chunk(gn, bn, c + 2 - NC, u + 1, q + 2)
                    st = b * NC + c
                    if st == 0:
                        for k in range(2, CT):
                            load_wo(g, k)
                    if not last_group(g):
                        for n in range(NTILE):
                            if SPLIT_AT[n] == st + 1:
                                load_w(g + 1, n)
                        if st == NB * NC - 1:
                            for k in range(2):
                                load_wo(g + 1, k)

            groups(sp, body)

            sp.wait_ge(oacc_done, NU * NC)

            def load_f(k, w, q_src, s_src):
                wait(sp, f_lo_done, k)
                sp.dma_start(f_q[:, 0:w], q_src).then_inc(s_fq, 16)
                sp.dma_start(f_s[:, 0:w], s_src.unsqueeze(0).broadcast_to([P, w])).then_inc(s_fs, 16)

            load_f(0, 2 * DM, gu_q[0], gu_s[0])
            for t in range(NT):
                wait(sp, x2tp, t - 1)
                sp.dma_start(xin[:, t % 2, :], x[t * P:(t + 1) * P, :]).then_inc(s_xin[t % 2], 16)
            with sp.Fori(1, FT) as i:
                load_f(i, 2 * DM, gu_q[i], gu_s[i])
            for i in range(FT):
                load_f(FT + i, DM, dn_q[i], dn_s[i])
            for t in range(NT):
                sp.wait_ge(y_out, t + 1)
                sp.dma_start(out[t * P:(t + 1) * P, :], oacc[:, t, :]).then_inc(s_out, 16)
            sp.wait_ge(s_out, 16 * NT)

        @block.tensor
        def _(pe):
            pe.wait_ge(s_con, 16)
            for t in range(NT):
                pe.wait_ge(normed, t + 1)
                wait(pe, xt_lo_done, t - 1)
                for k in range(KT):
                    last = nc.tensor.transpose(bank[t % 2][:, k * P:(k + 1) * P], oacc[:, t, k * P:(k + 1) * P], ident)
                last.then_inc(xtp, 1)

            def split_product(o, l_hi, l_lo, r_hi, r_lo, first, final):
                nc.tensor.matmul(o, l_hi, r_hi, start=first, stop=False)
                nc.tensor.matmul(o, l_hi, r_lo, start=False, stop=False)
                return nc.tensor.matmul(o, l_lo, r_hi, start=False, stop=final)

            pe.wait_ge(wdt_split, 2)
            pe.wait_ge(xt_lo_done, NT)
            for b in range(NB):
                s = slice(b * L, (b + 1) * L)
                for k in range(KT):
                    last = split_product(bank[2 + b][:], z_hi[:, k, :], z_lo[:, k, :], xT_hi[:, k, s], xT_lo[:, k, s],
                                         k == 0, k == KT - 1)
                last.then_inc(dt_mm, 1)

            def project(g, b, n, u):
                k0 = u * NTILE + n
                wait(pe, w_hi_done, g * NTILE + n + 1)
                wait(pe, w_lo_done, g * NTILE + n + 1)
                if n < 2:
                    wait(pe, xc_done, k0 - 1)
                elif n - 2 < NCONV:
                    wait(pe, taps, u * NCONV + n - 1)
                else:
                    wait(pe, xc_done, k0 - 1)
                s = slice(b * L, (b + 1) * L)
                for k in range(KT):
                    last = split_product(bank[n % 2][:], w_hi[:, n, k, :], w_lo[:, n, k, :],
                                         xT_hi[:, k, s], xT_lo[:, k, s], k == 0, k == KT - 1)
                last.then_inc(ip_done, 1)

            for n in range(2):
                project(0, 0, n, 0)
            pe.wait_ge(pre_dve, 6)
            for src, o in ((dt_h, bank[4]), (a_h, bank[5])):
                for t in range(NT):
                    last = nc.tensor.transpose(o[:, t * NH:(t + 1) * NH], src[:, t * P:(t + 1) * P], ident[0:NH, 0:NH])
                last.then_inc(pre_pe, 1)
            project(0, 0, 2, 0)
            pe.wait_ge(pre_dve, 8)
            nc.tensor.matmul(bank[6][:], tri, a_tok, start=True, stop=True).then_inc(pre_pe, 1)
            nc.tensor.matmul(bank[7][:], ones, a_tok, start=True, stop=True).then_inc(pre_pe, 1)
            project(0, 0, 3, 0)
            pe.wait_ge(pre_dve, 9)
            for t in range(NT):
                last = nc.tensor.transpose(bank[4 + t // 4][0:NH, (t % 4) * P:(t % 4 + 1) * P],
                                           cum_tok[:, t * NH:(t + 1) * NH], ident)
            last.then_inc(pre_pe, 1)
            for n in range(4, NTILE):
                project(0, 0, n, 0)

            def sum_squares(q):
                pe.wait_ge(ysum, q + 1)
                now = q + 1 if isinstance(q, int) and q == NU * NC - 1 else q + 2
                pe.wait_ge(sm_done, now)
                pe.wait_ge(bt_done, now)
                nc.tensor.matmul(B_S[:, 2 * Q:2 * Q + 1], ysq[:, 0:Q], ones[:, 0:1], start=True, stop=True
                                 ).then_inc(ssq_done, 1)

            def out_project(g, q):
                pe.wait_ge(z_hi_done, q + 1)
                pe.wait_ge(z_lo_done, q + 1)
                pe.wait_ge(wo_hi_done, (g + 1) * CT)
                pe.wait_ge(wo_lo_done, (g + 1) * CT)
                wait(pe, oacc_done, q)
                for k in range(CT):
                    last = split_product(B_OP[:], z_hi[:, k, :], z_lo[:, k, :], wo_hi[:, k, :], wo_lo[:, k, :],
                                         k == 0, k == CT - 1)
                last.then_inc(op_done, 1)

            def by_token(b, c, u, q):
                s = slice(c * Q, (c + 1) * Q)
                pe.wait_ge(xc_done, u * NTILE + NCONV)
                wait(pe, ms_done, q - 1)
                nc.tensor.matmul(B_S[:, 0:Q], xc[:, b, 0, s], xc[:, b, 1, s], start=True, stop=True)
                nc.tensor.transpose(B_S[:, Q:2 * Q], xc[:, b, 0, s], ident).then_inc(st_done, 1)
                wait(pe, xdt_done, q)
                for k in range(CT):
                    last = nc.tensor.transpose(B_XT[:, k * P:(k + 1) * P], xc[:, b, 2 + k, s], ident)
                last.then_inc(xt_done, 1)

            by_token(0, 0, 0, 0)

            def body(g):
                for b, c, u, q, more, gn, bn in steps(g):
                    first = isinstance(q, int) and q == 0
                    if not first:
                        sum_squares(q - 1)
                    pe.wait_ge(m_done, q + 1)
                    pe.wait_ge(xdt_done, q + 1)
                    wait(pe, yl_done, q)
                    for h in range(HG):
                        last = nc.tensor.matmul(B_YD[(h % 2) * HD:(h % 2 + 1) * HD, (h // 2) * Q:(h // 2 + 1) * Q],
                                                xdt[:, h, :], em[:, h, :], start=True, stop=True)
                    last.then_inc(yd_done, 1)
                    nd = u * (NC - 1) + c
                    if c > 0:
                        pe.wait_ge(h_done, nd)
                        wait(pe, t1_done, nd - 1)
                        for k in range(CT):
                            last = nc.tensor.matmul(B_YO[:, k * Q:(k + 1) * Q],
                                                    hst[:, 2 * k:2 * k + 2, :].rearrange("p h d -> p (h d)"),
                                                    xc[:, b, 1, c * Q:(c + 1) * Q], start=True, stop=True)
                        last.then_inc(yo_done, 1)
                    if c < NC - 1:
                        pe.wait_ge(xw_done, nd + 1)
                        pe.wait_ge(bt_done, q + 1)
                        wait(pe, h_done, nd)
                        nc.tensor.matmul(B_DH[:], btok[:], xw[:].rearrange("p h d -> p (h d)"),
                                         start=True, stop=True).then_inc(dh_done, 1)
                    if nxt := following(b, c, u, more):
                        by_token(*nxt, q + 1)
                    for n in SLOTS[c][0] if more else []:
                        project(gn, bn, n, u + 1)
                    if not first:
                        out_project(g if b or c else g - 1, q - 1)
                    for n in SLOTS[c][1] if more else []:
                        project(gn, bn, n, u + 1)

            groups(pe, body)
            sum_squares(NU * NC - 1)
            out_project(NG - 1, NU * NC - 1)

            for t in range(NT):
                pe.wait_ge(x2n_done, t + 1)
                wait(pe, xt_lo_done, NT + t - 1)
                for k in range(KT):
                    last = nc.tensor.transpose(bank[t % 2][:, k * P:(k + 1) * P], xin[:, t % 2, k * P:(k + 1) * P],
                                               ident)
                last.then_inc(x2tp, 1)
            pe.wait_ge(xt_hi_done, 2 * NT)
            pe.wait_ge(xt_lo_done, 2 * NT)

            def pair(j):
                for r in range(2):
                    i = j * 2 + r
                    pe.wait_ge(f_hi_done, i + 1)
                    pe.wait_ge(f_lo_done, i + 1)
                    for b in range(NB):
                        wait(pe, hbuf_done, (i - 2) * NB + b + 1)
                        s = slice(b * L, (b + 1) * L)
                        for m, s_mm in ((0, g_mm), (1, u_mm)):
                            for k in range(KT):
                                w = slice(m * DM + k * P, m * DM + (k + 1) * P)
                                last = split_product(bank[4 * r + 2 * b + m][:], f_hi[:, r, w], f_lo[:, r, w],
                                                     xT_hi[:, k, s], xT_lo[:, k, s], k == 0, k == KT - 1)
                            last.then_inc(s_mm, 1)

            pairs(pe, pair)
            pe.wait_ge(hbuf_done, FT * NB)
            pe.wait_ge(h_hi_done, FT * NB)
            pe.wait_ge(h_lo_done, FT * NB)
            for i in range(FT):
                pe.wait_ge(f_hi_done, FT + i + 1)
                pe.wait_ge(f_lo_done, FT + i + 1)
                for t in range(NT):
                    s = slice(t * P, (t + 1) * P)
                    last = split_product(bank[t][:], h_hi[:, i, s], h_lo[:, i, s], f_hi[:, i % 2, 0:DM],
                                         f_lo[:, i % 2, 0:DM], i == 0, i == FT - 1)
                    if i == FT - 1 or t == NT - 1:
                        last.then_inc(dn_mm, 1)

        @block.scalar
        def _(act):
            act.wait_ge(s_wdt, 16)
            nc.scalar.activation(z_hi[:], em[:, 0:KT, :], ACT.Copy).then_inc(wdt_split, 1)

            def split_w(g, n):
                act.wait_ge(s_raw[n % 2], (g * (NTILE // 2) + n // 2 + 1) * 16)
                wait(act, ip_done, ((g - 1) * NB + 1) * NTILE + n + 1)
                nc.scalar.activation(w_hi[:, n, :, :].rearrange("p k c -> p (k c)"), w_raw[:, n % 2, :], ACT.Copy
                                     ).then_inc(w_hi_done, 1)

            for t in range(NT):
                act.wait_ge(xtp, t + 1)
                nc.scalar.activation(xT_hi[:, :, t * P:(t + 1) * P], bank[t % 2][:].rearrange("p (k i) -> p k i", k=KT),
                                     ACT.Copy).then_inc(xt_hi_done, 1)
            for n in range(2):
                split_w(0, n)
            act.wait_ge(s_hp, 16)
            nc.scalar.activation(hp[:, 2:3], hp[:, 1:2], ACT.Exp).then_inc(pre_act, 1)
            act.wait_ge(wdt_split, 2)
            act.wait_ge(pre_dve, 2)
            nc.scalar.activation(dt_abs, dt_abs, ACT.Exp, scale=-1.0).then_inc(pre_act, 1)
            act.wait_ge(pre_dve, 3)
            nc.scalar.activation(dt_ln, dt_e1, ACT.Ln).then_inc(pre_act, 1)
            for n in range(2, NTILE):
                split_w(0, n)

            def first_pass(n, b, u):
                k0 = u * NTILE + n
                act.wait_ge(ip_done, k0 + 1)
                if n < NCONV:
                    act.wait_ge(cpar_done, u + 1)
                    wait(act, xc_done, k0 - 1 if n > 1 else (u - 1) * NTILE + NCONV)
                    p0 = n * (TAPS + 1)
                    nc.scalar.activation(acc[:, n % 2, :], bank[n % 2][:], ACT.Identity,
                                         scale=cpar[:, b, p0 + TAPS - 1:p0 + TAPS], bias=cpar[:, b, p0 + TAPS:p0 + TAPS + 1]
                                         ).then_inc(tap0, 1)
                else:
                    wait(act, xc_done, k0)
                    nc.scalar.activation(th[:], bank[n % 2][:], ACT.Tanh, scale=0.5).then_inc(th_done, 1)

            def second_pass(n, u):
                k0 = u * NTILE + n
                act.wait_ge(taps, u * NCONV + n + 1)
                wait(act, xc_done, k0)
                nc.scalar.activation(th[:], acc[:, n % 2, :], ACT.Tanh, scale=0.5).then_inc(th_done, 1)

            def slot(tiles, b, u):
                for n in tiles:
                    if 0 < n <= NCONV:
                        second_pass(n - 1, u)
                    first_pass(n, b, u)

            slot(range(4), 0, 0)
            act.wait_ge(pre_pe, 4)
            act.wait_ge(pre_dve, 10)
            nc.scalar.activation(w_tok, diff_tok, ACT.Exp).then_inc(pre_act, 1)
            for b in range(NB):
                o = tab[:, b::NB, DEC, :, :].rearrange("p g c h -> p c g h")
                i_ = bank[7][:, b * (DM // 2):(b + 1) * (DM // 2)].rearrange("p (c g h) -> p c g h", c=NC, h=HG)
                nc.scalar.activation(o, i_, ACT.Exp).then_inc(pre_act, 1)
            slot([4], 0, 0)
            act.wait_ge(pre_dve, 13)
            nc.scalar.activation(ecum_h, cum_h, ACT.Exp).then_inc(pre_act, 1)
            slot(range(5, NTILE), 0, 0)

            def decays(b, c, u, q):
                act.wait_ge(s_cumb[c % 2], cumb_loads(u, c) * 16)
                act.wait_ge(cur_done, u + 1)
                wait(act, yd_done, q)
                for h in range(HG):
                    last = nc.scalar.activation(em[:, h, :], cumb[:, c % 2, h, :], ACT.Relu, scale=-1.0,
                                                bias=cur[:, b, CUM, c, h:h + 1])
                last.then_inc(diff_done, 1)
                act.wait_ge(diff_done, q + 1)
                nc.scalar.activation(em[:], em[:], ACT.Exp, scale=-1.0).then_inc(e_done, 1)

            act.wait_ge(wdt_split, 2)
            act.wait_ge(dt_mm, NB)
            decays(0, 0, 0, 0)

            def body(g):
                for b, c, u, q, more, gn, bn in steps(g):
                    if nxt := following(b, c, u, more):
                        decays(*nxt, q + 1)
                    slot(SLOTS[c][0] if more else [], bn, u + 1)
                    wait_y(act, u, q, c)
                    wait(act, ssq_done, q)
                    nc.scalar.activation(ysq[:], ybuf[:].rearrange("p k i -> p (k i)"), ACT.Square).then_inc(sq_done, 1)
                    if not last_group(g):
                        for n in range(NTILE):
                            if SPLIT_AT[n] == b * NC + c:
                                split_w(g + 1, n)
                    act.wait_ge(z_done, q + 1)
                    wait(act, op_done, q)
                    nc.scalar.activation(z_hi[:], zbuf[:], ACT.Copy).then_inc(z_hi_done, 1)
                    slot(SLOTS[c][1] if more else [], bn, u + 1)
                    if b == 0 and c == 0:
                        act.wait_ge(cpar_done, u + 1)
                        wait(act, op_done, q)
                        for k in range(CT):
                            act.wait_ge(s_woraw[k % 2], (g * (CT // 2) + k // 2 + 1) * 16)
                            nc.scalar.activation(wo_hi[:, k, :], wo_raw[:, k % 2, :], ACT.Copy,
                                                 scale=cpar[:, b, PNW + k:PNW + k + 1]).then_inc(wo_hi_done, 1)

            groups(act, body)

            for t in range(NT):
                act.wait_ge(x2tp, t + 1)
                nc.scalar.activation(xT_hi[:, :, t * P:(t + 1) * P], bank[t % 2][:].rearrange("p (k i) -> p k i", k=KT),
                                     ACT.Copy).then_inc(xt_hi_done, 1)

            def split_f(k, slot_, w):
                act.wait_ge(f_w, k + 1)
                if isinstance(k, int) and k > FT + 1:
                    act.wait_ge(dn_mm, k - FT - 1)
                else:
                    wait(act, u_mm, (k - 1) * NB)
                nc.scalar.activation(f_hi[:, slot_, 0:w], f_s[:, 0:w], ACT.Copy).then_inc(f_hi_done, 1)

            split_f(0, 0, 2 * DM)

            def pair(j):
                for r in range(2):
                    i = j * 2 + r
                    split_f(i + 1, 1 - r, DM if isinstance(i, int) and i == FT - 1 else 2 * DM)
                    for b in range(NB):
                        act.wait_ge(g_mm, i * NB + b + 1)
                        wait(act, g_silu, (i - 1) * NB + b + 1)
                        nc.scalar.activation(f_th[:, b, :], bank[4 * r + 2 * b][:], ACT.Tanh, scale=0.5).then_inc(g_th, 1)
                    for b in range(NB):
                        act.wait_ge(hbuf_done, i * NB + b + 1)
                        nc.scalar.activation(h_hi[:, i, b * L:(b + 1) * L], f_th[:, 2 + b, :], ACT.Copy
                                             ).then_inc(h_hi_done, 1)

            pairs(act, pair)
            for i in range(1, FT):
                split_f(FT + i, i % 2, DM)

        @block.gpsimd
        def _(pool):
            nc.gpsimd.memset(mhalf[:], -0.5).then_inc(const_set, 1)
            pool.wait_ge(const_set, 1)

            def power(k):
                pool.wait_ge(var_eps, k + 1)
                nc.gpsimd.tensor_tensor(ln_rs[:, k:k + 1], ln_ve[:, k:k + 1], mhalf[:], ALU.pow).then_inc(rstd, 1)

            def split_w(g, n):
                pool.wait_ge(w_hi_done, g * NTILE + n + 1)
                nc.gpsimd.tensor_tensor(w_lo[:, n, :, :].rearrange("p k c -> p (k c)"), w_raw[:, n % 2, :],
                                        w_hi[:, n, :, :].rearrange("p k c -> p (k c)").bitcast(F32), ALU.subtract
                                        ).then_inc(w_lo_done, 1)

            for t in range(NT):
                power(t)
            pool.wait_ge(wdt_split, 1)
            nc.gpsimd.tensor_tensor(z_lo[:], em[:, 0:KT, :], z_hi[:].bitcast(F32), ALU.subtract).then_inc(wdt_split, 1)
            for n in range(NTILE):
                split_w(0, n)

            def over(table, b, c):
                return cur[:, b, table, c, :].unsqueeze(2).broadcast_to([P, HG, HD])

            def skip_term(b, c, u, q):
                pool.wait_ge(xc_done, u * NTILE + NCONV)
                pool.wait_ge(cpar_done, u + 1)
                wait(pool, sq_done, q)
                wait(pool, z_done, q)
                nc.gpsimd.tensor_tensor(ybuf[:], xc[:, b, 2:2 + CT, c * Q:(c + 1) * Q],
                                        cpar[:, b, PD:PD + CT].unsqueeze(2).broadcast_to([P, CT, Q]), ALU.mult
                                        ).then_inc(dx_done, 1)

            def state_terms(b, c, u, q):
                nd = u * (NC - 1) + c
                pool.wait_ge(cur_done, u + 1)
                if c < NC - 1:
                    pool.wait_ge(xdt_done, q + 1)
                    wait(pool, dh_done, nd)
                    nc.gpsimd.tensor_tensor(xw[:], xdt[:], over(WE, b, c), ALU.mult).then_inc(xw_done, 1)
                    if c > 0:
                        pool.wait_ge(h_done, nd)
                        nc.gpsimd.tensor_tensor(hdec[:], hst[:], over(DEC, b, c), ALU.mult).then_inc(hd_done, 1)

            def root(q):
                pool.wait_ge(ms_done, q + 1)
                wait(pool, oacc_done, q)
                nc.gpsimd.tensor_tensor(rms[:, 1:2], rms[:, 0:1], mhalf[:], ALU.pow).then_inc(r_done, 1)

            state_terms(0, 0, 0, 0)
            skip_term(0, 0, 0, 0)

            def body(g):
                for b, c, u, q, more, gn, bn in steps(g):
                    if not (isinstance(q, int) and q == 0):
                        root(q - 1)
                    wait_y(pool, u, q, c)
                    pool.wait_ge(xc_done, (u + 1) * NTILE)
                    wait(pool, z_hi_done, q)
                    wait(pool, z_lo_done, q)
                    nc.gpsimd.tensor_tensor(zbuf[:], ybuf[:], gate[:, b, :, c * Q:(c + 1) * Q], ALU.mult
                                            ).then_inc(z_done, 1)
                    nxt = following(b, c, u, more)
                    if nxt:
                        state_terms(*nxt, q + 1)
                    pool.wait_ge(sq_done, q + 1)
                    nc.gpsimd.tensor_tensor(ysq[:, 0:2 * Q], ysq[:, 0:2 * Q], ysq[:, 2 * Q:4 * Q], ALU.add
                                            ).then_inc(ysum_half, 1)
                    pool.wait_ge(ysum_half, q + 1)
                    nc.gpsimd.tensor_tensor(ysq[:, 0:Q], ysq[:, 0:Q], ysq[:, Q:2 * Q], ALU.add).then_inc(ysum, 1)
                    if nxt:
                        skip_term(*nxt, q + 1)
                    if not last_group(g):
                        for n in range(NTILE):
                            if SPLIT_AT[n] == b * NC + c:
                                split_w(g + 1, n)

            groups(pool, body)
            root(NU * NC - 1)

            for k in range(2 * NT):
                power(NT + k)

            def split_f(k, slot_, w):
                pool.wait_ge(f_hi_done, k + 1)
                nc.gpsimd.tensor_tensor(f_lo[:, slot_, 0:w], f_s[:, 0:w], f_hi[:, slot_, 0:w].bitcast(F32), ALU.subtract
                                        ).then_inc(f_lo_done, 1)

            with pool.Fori(0, FT // 2) as j:
                for r in range(2):
                    split_f(j * 2 + r, r, 2 * DM)
            for i in range(FT):
                split_f(FT + i, i % 2, DM)
            for t in range(NT):
                power(3 * NT + t)

        @block.vector
        def _(dve):
            def moments(k, src):
                nc.vector.bn_stats(ln_st[:, k, :], src).then_inc(stats, 1)
                dve.wait_ge(stats, k + 1)
                nc.vector.bn_aggr(ln_mv[:, k, :], ln_st[:, k, :]).then_inc(aggr, 1)
                dve.wait_ge(aggr, k + 1)
                nc.vector.tensor_scalar(ln_ve[:, k:k + 1], ln_mv[:, k, 1:2], EPS, None, ALU.add).then_inc(var_eps, 1)

            def normalize(k, dst, src):
                dve.wait_ge(rstd, k + 1)
                return nc.vector.tensor_scalar(dst, src, ln_mv[:, k, 0:1], ln_rs[:, k:k + 1], ALU.subtract, ALU.mult)

            for t in range(NT + 1):
                if t < NT:
                    dve.wait_ge(s_x[t], 16)
                    moments(t, oacc[:, t, :])
                if t > 0:
                    normalize(t - 1, oacc[:, t - 1, :], oacc[:, t - 1, :]).then_inc(normed, 1)

            def copy_params(g, b, u):
                if not (isinstance(u, int) and u < 2):
                    q0 = (u - 1) * NC
                    dve.wait_ge(dx_done, q0)
                    dve.wait_ge(e_done, q0)
                    dve.wait_ge(xw_done, (u - 1) * (NC - 1))
                    dve.wait_ge(hd_done, (u - 1) * (NC - 2))
                    if b == 0:
                        dve.wait_ge(wo_hi_done, g * CT)
                if not (isinstance(u, int) and u == 0):
                    nc.vector.tensor_copy(cpar[:, b, :], par[:, g, :]).then_inc(cpar_done, 1)
                nc.vector.tensor_copy(cur[:, b, :, :, :].rearrange("p k c h -> p (k c h)"),
                                      tab[:, u, :, :, :].rearrange("p k c h -> p (k c h)")).then_inc(cur_done, 1)

            for t in range(NT):
                dve.wait_ge(xt_hi_done, t + 1)
                sl = slice(t * P, (t + 1) * P)
                nc.vector.tensor_tensor(xT_lo[:, :, sl], bank[t % 2][:].rearrange("p (k i) -> p k i", k=KT),
                                        xT_hi[:, :, sl].bitcast(F32), ALU.subtract).then_inc(xt_lo_done, 1)
            def first_use(n, b, u):
                k0 = u * NTILE + n
                if n < NCONV:
                    dve.wait_ge(tap0, u * NCONV + n + 1)
                    dve.wait_ge(cpar_done, u + 1)
                    p0 = n * (TAPS + 1)
                    for d in range(1, TAPS):
                        last = nc.vector.scalar_tensor_tensor(
                            out=acc[:, n % 2, d:L], in0=bank[n % 2][:, 0:L - d],
                            scalar=cpar[:, b, p0 + TAPS - 1 - d:p0 + TAPS - d], in1=acc[:, n % 2, d:L],
                            op0=ALU.mult, op1=ALU.add)
                        if d < TAPS - 1:
                            last.then_inc(tap_step, 1)
                            dve.wait_ge(tap_step, (u * NCONV + n) * (TAPS - 2) + d)
                    last.then_inc(taps, 1)
                else:
                    dve.wait_ge(th_done, k0 + 1)
                    wait(dve, z_done, (u - 1) * NC)
                    nc.vector.scalar_tensor_tensor(out=gate[:, b, n - NCONV, :], in0=th[:], scalar=1.0,
                                                   in1=bank[n % 2][:], op0=ALU.add, op1=ALU.mult).then_inc(xc_done, 1)

            def second_use(n, b, u):
                dve.wait_ge(th_done, u * NTILE + n + 1)
                wait(dve, dx_done, (u - 1) * NC)
                wait(dve, yd_done, (u - 1) * NC)
                wait(dve, yo_done, (u - 1) * (NC - 1))
                nc.vector.scalar_tensor_tensor(out=xc[:, b, n, :], in0=th[:], scalar=1.0, in1=acc[:, n % 2, :],
                                               op0=ALU.add, op1=ALU.mult).then_inc(xc_done, 1)

            def slot(tiles, b, u):
                for n in tiles:
                    if 0 < n <= NCONV:
                        second_use(n - 1, b, u)
                    first_use(n, b, u)

            dve.wait_ge(s_par, 16)
            nc.vector.tensor_scalar(par[:, :, PD:PD + 2 * CT], par[:, :, PD:PD + 2 * CT], 0.5, None, ALU.mult
                                    ).then_inc(pre_dve, 1)
            dve.wait_ge(pre_dve, 1)
            nc.vector.tensor_copy(cpar[:, 0, :], par[:, 0, :]).then_inc(cpar_done, 1)
            dve.wait_ge(s_hp, 16)
            dve.wait_ge(dt_mm, NB)
            for b in range(NB):
                last = nc.vector.tensor_scalar(dt_raw[:, b * L:(b + 1) * L], bank[2 + b][0:NH, :], hp[:, 0:1], None, ALU.add)
            last.then_inc(pre_step, 1)
            dve.wait_ge(pre_step, 1)
            nc.vector.scalar_tensor_tensor(out=dt_abs, in0=dt_raw, scalar=-1.0, in1=dt_raw, op0=ALU.mult, op1=ALU.max
                                           ).then_inc(pre_dve, 1)
            dve.wait_ge(pre_act, 2)
            nc.vector.tensor_scalar(dt_e1, dt_abs, 1.0, None, ALU.add).then_inc(pre_dve, 1)
            dve.wait_ge(pre_dve, 3)
            nc.vector.scalar_tensor_tensor(out=dt_abs, in0=dt_e1, scalar=-1.0, in1=dt_abs, op0=ALU.add, op1=ALU.subtract
                                           ).then_inc(pre_step, 1)
            dve.wait_ge(pre_step, 2)
            dve.wait_ge(pre_act, 3)
            nc.vector.tensor_tensor(dt_ln, dt_ln, dt_abs, ALU.subtract).then_inc(pre_step, 1)
            nc.vector.tensor_scalar(hp[:, 3:4], hp[:, 2:3], -1.0, None, ALU.mult).then_inc(pre_dve, 1)
            dve.wait_ge(pre_step, 3)
            dve.wait_ge(pre_dve, 4)
            nc.vector.scalar_tensor_tensor(out=dt_h, in0=dt_raw, scalar=0.0, in1=dt_ln, op0=ALU.max, op1=ALU.add
                                           ).then_inc(pre_dve, 1)
            dve.wait_ge(pre_dve, 5)
            nc.vector.tensor_scalar(a_h, dt_h, hp[:, 3:4], None, ALU.mult).then_inc(pre_dve, 1)

            def by_unit(table, b):
                return tab[:, b::NB, table, :, :].rearrange("p g c h -> p c g h")

            def by_token(flat, b):
                return flat[:, b * (DM // 2):(b + 1) * (DM // 2)].rearrange("p (c g h) -> p c g h", c=NC, h=HG)

            slot([0], 0, 0)
            dve.wait_ge(pre_pe, 1)
            for b in range(NB):
                last = nc.vector.tensor_scalar(by_unit(DT, b), by_token(bank[4][:], b), 0.5, None, ALU.mult)
            last.then_inc(pre_dve, 1)
            dve.wait_ge(pre_pe, 2)
            nc.vector.tensor_copy(a_tok, bank[5][:]).then_inc(pre_dve, 1)
            slot([1], 0, 0)
            dve.wait_ge(pre_pe, 3)
            nc.vector.tensor_copy(cum_tok, bank[6][:]).then_inc(pre_dve, 1)
            dve.wait_ge(pre_pe, 4)
            dve.wait_ge(pre_dve, 9)
            nc.vector.tensor_tensor(diff_tok, bank[7][:], cum_tok, ALU.subtract).then_inc(pre_dve, 1)
            for b in range(NB):
                last = nc.vector.tensor_copy(by_unit(CUM, b), by_token(cum_tok, b))
            last.then_inc(pre_dve, 1)
            slot([2, 3], 0, 0)
            dve.wait_ge(pre_pe, 5)
            for k in range(2):
                nc.vector.tensor_copy(cum_h[:, k * 4 * P:(k + 1) * 4 * P], bank[4 + k][0:NH, :]).then_inc(pre_dve, 1)
            dve.wait_ge(pre_act, 4)
            for b in range(NB):
                last = nc.vector.tensor_scalar(by_unit(WE, b), by_token(w_tok, b), 0.5, None, ALU.mult)
            last.then_inc(pre_dve, 1)
            slot([4], 0, 0)
            dve.wait_ge(pre_act, 7)
            nc.vector.tensor_scalar(ecum_h, ecum_h, 0.5, None, ALU.mult).then_inc(pre_dve, 1)
            dve.wait_ge(pre_dve, 15)
            copy_params(0, 0, 0)
            nc.vector.memset(oacc[:, NT - 1, :], 0.0).then_inc(pre_step, 1)
            slot(range(5, NTILE), 0, 0)
            dve.wait_ge(pre_step, 4)

            def mean_square(q):
                dve.wait_ge(ssq_done, q + 1)
                wait(dve, r_done, q)
                nc.vector.tensor_scalar(rms[:, 0:1], B_S[:, 2 * Q:2 * Q + 1], 1.0 / GW, EPS, ALU.mult, ALU.add
                                        ).then_inc(ms_done, 1)

            def gather_out(g, t, q):
                dve.wait_ge(op_done, q + 1)
                dve.wait_ge(r_done, q + 1)
                if isinstance(g, int) and g == 0:
                    nc.vector.tensor_scalar(oacc[:, t, :], B_OP[:], rms[:, 1:2], None, ALU.mult).then_inc(oacc_done, 1)
                else:
                    nc.vector.scalar_tensor_tensor(out=oacc[:, t, :], in0=B_OP[:], scalar=rms[:, 1:2], in1=oacc[:, t, :],
                                                   op0=ALU.mult, op1=ALU.add).then_inc(oacc_done, 1)

            def matrix(b, c, u, q):
                nd = u * (NC - 1) + c
                dve.wait_ge(st_done, q + 1)
                wait(dve, dh_done, nd)
                nc.vector.tensor_tensor(smask[:], B_S[:, 0:Q], mask4, ALU.mult).then_inc(sm_done, 1)
                nc.vector.tensor_copy(btok[:], B_S[:, Q:2 * Q]).then_inc(bt_done, 1)
                dve.wait_ge(xt_done, q + 1)
                wait(dve, yd_done, q)
                wait(dve, xw_done, nd)
                dve.wait_ge(cur_done, u + 1)
                nc.vector.tensor_tensor(xdt[:], B_XT[:].rearrange("p (h d) -> p h d", h=HG),
                                        cur[:, b, DT, c, :].unsqueeze(2).broadcast_to([P, HG, HD]), ALU.mult
                                        ).then_inc(xdt_done, 1)
                dve.wait_ge(e_done, q + 1)
                dve.wait_ge(sm_done, q + 1)
                nc.vector.tensor_tensor(em[:], em[:], smask[:].unsqueeze(1).broadcast_to([P, HG, Q]), ALU.mult
                                        ).then_inc(m_done, 1)

            matrix(0, 0, 0, 0)

            def body(g):
                for b, c, u, q, more, gn, bn in steps(g):
                    first = isinstance(q, int) and q == 0
                    nd = u * (NC - 1) + c
                    if not first:
                        mean_square(q - 1)
                    dve.wait_ge(yd_done, q + 1)
                    dve.wait_ge(dx_done, q + 1)
                    nc.vector.tensor_tensor(ybuf[:], B_YD[:].rearrange("p (k i) -> p k i", k=CT), ybuf[:], ALU.add
                                            ).then_inc(yl_done, 1)
                    if c > 0:
                        dve.wait_ge(yo_done, nd)
                        dve.wait_ge(s_ecum[c % 2], ecum_loads(u, c) * 32)
                        nc.vector.tensor_tensor(ecum[:, c % 2, :, :], B_YO[:].rearrange("p (k i) -> p k i", k=CT),
                                                ecum[:, c % 2, :, :], ALU.mult).then_inc(t1_done, 1)
                        dve.wait_ge(yl_done, q + 1)
                        dve.wait_ge(t1_done, nd)
                        nc.vector.tensor_tensor(ybuf[:], ybuf[:], ecum[:, c % 2, :, :], ALU.add).then_inc(y_done, 1)
                    if c < NC - 1:
                        dve.wait_ge(dh_done, nd + 1)
                        hflat = hst[:].rearrange("p h d -> p (h d)")
                        if c == 0:
                            wait(dve, yo_done, u * (NC - 1))
                            nc.vector.tensor_copy(hflat, B_DH[:]).then_inc(h_done, 1)
                        else:
                            dve.wait_ge(hd_done, u * (NC - 2) + c)
                            nc.vector.tensor_tensor(hflat, B_DH[:], hdec[:].rearrange("p h d -> p (h d)"), ALU.add
                                                    ).then_inc(h_done, 1)
                    if nxt := following(b, c, u, more):
                        matrix(*nxt, q + 1)
                    if c == 0 and more:
                        copy_params(gn, bn, u + 1)
                    slot(SLOTS[c][0] if more else [], bn, u + 1)
                    if not first:
                        gather_out(g if b or c else g - 1, (b * NC + c - 1) % NT, q - 1)
                    dve.wait_ge(z_hi_done, q + 1)
                    nc.vector.tensor_tensor(z_lo[:], zbuf[:], z_hi[:].bitcast(F32), ALU.subtract).then_inc(z_lo_done, 1)
                    slot(SLOTS[c][1] if more else [], bn, u + 1)
                    if b == 0 and c == 0:
                        for k in range(CT):
                            dve.wait_ge(wo_hi_done, g * CT + k + 1)
                            nc.vector.scalar_tensor_tensor(out=wo_lo[:, k, :], in0=wo_raw[:, k % 2, :],
                                                           scalar=cpar[:, b, PNW + k:PNW + k + 1],
                                                           in1=wo_hi[:, k, :].bitcast(F32), op0=ALU.mult,
                                                           op1=ALU.subtract).then_inc(wo_lo_done, 1)

            groups(dve, body)
            mean_square(NU * NC - 1)
            gather_out(NG - 1, NT - 1, NU * NC - 1)

            for t in range(NT):
                dve.wait_ge(oacc_done, NU * NC)
                k = NT + 2 * t
                moments(k, oacc[:, t, :])
                normalize(k, oacc[:, t, :], oacc[:, t, :]).then_inc(ln1, 1)
                dve.wait_ge(ln1, t + 1)
                dve.wait_ge(s_xin[t % 2], (t // 2 + 1) * 16)
                nc.vector.tensor_tensor(oacc[:, t, :], oacc[:, t, :], xin[:, t % 2, :], ALU.add).then_inc(x2_done, 1)
                dve.wait_ge(x2_done, t + 1)
                moments(k + 1, oacc[:, t, :])
                normalize(k + 1, xin[:, t % 2, :], oacc[:, t, :]).then_inc(x2n_done, 1)
                dve.wait_ge(xt_hi_done, NT + t + 1)
                sl = slice(t * P, (t + 1) * P)
                nc.vector.tensor_tensor(xT_lo[:, :, sl], bank[t % 2][:].rearrange("p (k i) -> p k i", k=KT),
                                        xT_hi[:, :, sl].bitcast(F32), ALU.subtract).then_inc(xt_lo_done, 1)

            def dequant(k, w, factor):
                dve.wait_ge(s_fq, (k + 1) * 16)
                dve.wait_ge(s_fs, (k + 1) * 16)
                nc.vector.scalar_tensor_tensor(out=f_s[:, 0:w], in0=f_q[:, 0:w], scalar=factor, in1=f_s[:, 0:w],
                                               op0=ALU.mult, op1=ALU.mult).then_inc(f_w, 1)

            dequant(0, 2 * DM, 1.0)

            def pair(j):
                for r in range(2):
                    i = j * 2 + r
                    if isinstance(i, int) and i == FT - 1:
                        dequant(FT, DM, 0.5)
                    else:
                        dequant(i + 1, 2 * DM, 1.0)
                    for b in range(NB):
                        n = i * NB + b
                        hb = f_th[:, 2 + b, :]
                        dve.wait_ge(g_th, n + 1)
                        wait(dve, h_hi_done, (i - 1) * NB + b + 1)
                        wait(dve, h_lo_done, (i - 1) * NB + b + 1)
                        nc.vector.scalar_tensor_tensor(out=hb, in0=f_th[:, b, :], scalar=1.0,
                                                       in1=bank[4 * r + 2 * b][:], op0=ALU.add, op1=ALU.mult
                                                       ).then_inc(g_silu, 1)
                        dve.wait_ge(u_mm, n + 1)
                        dve.wait_ge(g_silu, n + 1)
                        nc.vector.tensor_tensor(hb, bank[4 * r + 2 * b + 1][:], hb, ALU.mult).then_inc(hbuf_done, 1)
                        dve.wait_ge(h_hi_done, n + 1)
                        hs = (slice(None), i, slice(b * L, (b + 1) * L))
                        nc.vector.tensor_tensor(h_lo[hs], hb, h_hi[hs].bitcast(F32), ALU.subtract).then_inc(h_lo_done, 1)

            pairs(dve, pair)
            for i in range(1, FT):
                dequant(FT + i, DM, 0.5)

            def last_moments(t):
                dve.wait_ge(dn_mm, FT - 1 + t + 1)
                moments(3 * NT + t, bank[t][:])

            last_moments(0)
            for t in range(NT):
                if t + 1 < NT:
                    last_moments(t + 1)
                normalize(3 * NT + t, f_th[:, t % 2, :], bank[t][:]).then_inc(fin_n, 1)
                dve.wait_ge(fin_n, t + 1)
                nc.vector.tensor_tensor(oacc[:, t, :], oacc[:, t, :], f_th[:, t % 2, :], ALU.add).then_inc(y_out, 1)


def lay_out(a):
    import numpy as np

    w = a["L0_attn_in_proj_w"]
    gate_rows, x_rows = w[:NG * GW], w[NG * GW:2 * NG * GW]
    b_rows, c_rows = w[2 * NG * GW:2 * NG * GW + NG * NS], w[2 * NG * GW + NG * NS:2 * NG * (GW + NS)]
    dt_rows = w[-NH:]

    def tiles(rows, n):
        return rows.reshape(NG, n, P, KT, P).transpose(0, 4, 1, 3, 2)

    win = np.concatenate([tiles(b_rows, 1), tiles(c_rows, 1), tiles(x_rows, CT), tiles(gate_rows, CT)], axis=2)
    wdt = np.zeros((P, KT, P), np.float32)
    wdt[:, :, :NH] = dt_rows.reshape(NH, KT, P).transpose(2, 1, 0)
    wo = a["L0_attn_out_proj_w"].reshape(DM, NG, CT, P).transpose(1, 3, 2, 0)

    cw, cb = a["L0_attn_conv_weight"], a["L0_attn_conv_bias"]
    conv = np.concatenate([cw, cb[:, None]], axis=1)
    cx, cB, cC = conv[:NG * GW], conv[NG * GW:NG * (GW + NS)], conv[NG * (GW + NS):]

    def by_partition(v, n):
        return v.reshape(NG, n, P, -1).transpose(2, 0, 1, 3).reshape(P, NG, -1)

    skip = np.repeat(a["L0_attn_D"], HD)
    parg = np.concatenate([by_partition(cB, 1), by_partition(cC, 1), by_partition(cx, CT), by_partition(skip, CT),
                           by_partition(a["L0_attn_norm_weight"], CT)], axis=2)
    hpar = np.stack([a["L0_attn_dt_bias"], a["L0_attn_A_log"]], axis=1)
    i = np.arange(P)
    tri = (i[:, None] <= i[None, :]).astype(np.float32)
    consts = np.stack([np.eye(P, dtype=np.float32), tri, tri * np.float32(0.25), np.ones((P, P), np.float32)], axis=1)

    gq, uq = (a[f"L0_ffn_{n}_q"].reshape(FT, P, KT, P).transpose(0, 3, 2, 1) for n in ("gate", "up"))
    gs, us = (a[f"L0_ffn_{n}_s"].reshape(FT, P, KT).transpose(0, 2, 1) for n in ("gate", "up"))
    return {
        "x": a["L0_attn_hidden_states"].reshape(T, DM),
        "win": win.reshape(NG, P, NTILE, KT * P),
        "wdt": wdt,
        "wo": wo,
        "parg": parg,
        "hpar": hpar,
        "consts": consts,
        "gu_q": np.stack([gq, uq], axis=2).reshape(FT, P, 2 * DM),
        "gu_s": np.stack([gs, us], axis=1).reshape(FT, 2 * DM),
        "dn_q": a["L0_ffn_down_q"].reshape(DM, FT, P).transpose(1, 2, 0),
        "dn_s": a["L0_ffn_down_s"].T,
    }


def kernel(**inputs):
    import numpy as np
    import concourse.bacc as bacc
    from concourse.bass_utils import run_bass_kernel_spmd

    nc = bacc.Bacc("TRN2", target_bir_lowering=False, num_devices=1)
    arrays, args = {}, {}
    for name, v in lay_out({k: np.asarray(v) for k, v in inputs.items()}).items():
        v = np.ascontiguousarray(v)
        arrays[f"in_{name}"] = v
        args[name] = nc.dram_tensor(f"in_{name}", v.shape, mybir.dt.from_np(v.dtype), kind="ExternalInput").ap()
    out = nc.dram_tensor("out_0", (T, DM), F32, kind="ExternalOutput").ap()
    mixer_and_ffn(nc, out=out, **args)
    got = run_bass_kernel_spmd(nc, [arrays], core_ids=[0]).results[0]["out_0"]
    return got.reshape(NB, L, DM)
```

```python
from contextlib import ExitStack

import concourse.bass as bass
from concourse import mybir

F32 = mybir.dt.float32
F32R = mybir.dt.float32r
I32 = mybir.dt.int32
ALU = mybir.AluOpType
ACT = mybir.ActivationFunctionType

P = 128
DM = 512
NB, L = 2, 512
T = NB * L
NH, HD, NS = 64, 64, 128
NG = 8
HG = NH // NG
Q = 128
NC = L // Q
NT = T // Q
KT = DM // P
GW = HG * HD
CT = GW // P
NTILE = 2 + 2 * CT
NCONV = 2 + CT
TAPS = 4
NPAR = NCONV * (TAPS + 1) + 2 * CT
PD, PNW = NCONV * (TAPS + 1), NCONV * (TAPS + 1) + CT
FI = 1792
FT = FI // P
EPS = 1e-5
NU = NB * NG
DT, WE, CUM, DEC = range(4)

TILES = [(True, 0), (True, 1), (True, 2), (False, 0), (True, 3), (True, 4), (True, 5), (False, 1), (False, 2), (False, 3)]
BANKS = [0, 1, 2, 0, 1, 2, 0, 1, 2, 1]
ACC_SLOTS = [k % 2 if conv else None for conv, k in TILES]
ALL_CONV = 7
SLOTS = [([0], [1]), ([2, 3], [4]), ([5], [6, 7]), ([8], [9])]
SPLIT_AT = [1, 1, 2, 2, 3, 3, 4, 4, 5, 5]


ROUNDS = [[0, 1, 2], [3], [4], [5, 6]]
ROUND_AFTER = 6


def parts_of(rounds, after=False):
    for r in rounds:
        for p in (3, 2, 1, 0):
            if 0 <= r - p < NT and (r < ROUND_AFTER or (r > ROUND_AFTER or p == 3) == after):
                yield p, r - p


def tiles_up_to(n, conv):
    return sum(k == conv for k, _ in TILES[:n])


def last_user(n, same):
    back = [m for m in range(n) if same[m] == same[n]]
    return (back[-1], 0) if back else (max(m for m in range(NTILE) if same[m] == same[n]), 1)


def mixer_and_ffn(nc, x, win, wdt, wo, parg, hpar, consts, gu_q, gu_s, dn_q, dn_s, out):
    cum_dram = nc.dram_tensor("cum_dram", [NG, NT, HG * Q], F32, kind="Internal").ap()
    ecum_dram = nc.dram_tensor("ecum_dram", [NG, NT, 2, CT * Q], F32, kind="Internal").ap()

    with ExitStack() as ctx:
        def sem(name):
            return ctx.enter_context(nc.semaphore(name))

        def sb(name, shape, dt, scope=ctx):
            return scope.enter_context(nc.sbuf_tensor(name, shape, dt))

        xT_hi = sb("xT_hi", [P, KT, T], F32R)
        xT_lo = sb("xT_lo", [P, KT, T], F32R)
        oacc = sb("oacc", [P, NT, DM], F32)
        con = sb("con", [P, 4, P], F32)
        ln_st = sb("ln_st", [P, 32, 6], F32)
        ln_mv = sb("ln_mv", [P, 32, 2], F32)
        ln_ve = sb("ln_ve", [P, 32], F32)
        ln_rs = sb("ln_rs", [P, 32], F32)
        ln_sh = sb("ln_sh", [P, NT], F32)
        mhalf = sb("mhalf", [P, 1], F32)
        ident, tri, mask4, ones = (con[:, i, :] for i in range(4))
        mix = ExitStack()
        w_hi = sb("w_hi", [P, NTILE, KT, P], F32R, mix)
        w_lo = sb("w_lo", [P, NTILE, KT, P], F32R, mix)
        wo_hi = sb("wo_hi", [P, CT, DM], F32R, mix)
        wo_lo = sb("wo_lo", [P, CT, DM], F32R, mix)
        w_raw = sb("w_raw", [P, 2, KT * P], F32, mix)
        wo_raw = sb("wo_raw", [P, CT, DM], F32, mix)
        xc = sb("xc", [P, NB, NCONV, L], F32, mix)
        gate = sb("gate", [P, NB, CT, L], F32, mix)
        acc = sb("acc", [P, 2, L], F32, mix)
        th = sb("th", [P, L], F32, mix)
        cumb = sb("cumb", [P, 2, HG, Q], F32, mix)
        ecum = sb("ecum", [P, 2, CT, Q], F32, mix)
        smask = sb("smask", [P, Q], F32, mix)
        btok = sb("btok", [P, NS], F32, mix)
        xdt = sb("xdt", [P, HG, HD], F32, mix)
        xw = sb("xw", [P, HG, HD], F32, mix)
        ybuf = sb("ybuf", [P, CT, Q], F32, mix)
        ysq = sb("ysq", [P, CT * Q], F32, mix)
        zbuf = sb("zbuf", [P, CT, Q], F32, mix)
        z_hi = sb("z_hi", [P, CT, Q], F32R, mix)
        z_lo = sb("z_lo", [P, CT, Q], F32R, mix)
        hst = sb("hst", [P, HG, HD], F32, mix)
        hdec = sb("hdec", [P, HG, HD], F32, mix)
        tab = sb("tab", [P, NU, 4, NC, HG], F32, mix)
        cur = sb("cur", [P, NB, 4, NC, HG], F32, mix)
        par = sb("par", [P, NG, NPAR], F32, mix)
        cpar = sb("cpar", [P, NB, NPAR], F32, mix)
        hp = sb("hp", [NH, 4], F32, mix)
        rms = sb("rms", [P, 2], F32, mix)
        mix.close()
        ffn = ExitStack()
        f_q = sb("f_q", [P, 2 * DM], I32, ffn)
        f_s = sb("f_s", [P, 2 * DM], F32, ffn)
        f_hi = sb("f_hi", [P, 2, 2 * DM], F32R, ffn)
        f_lo = sb("f_lo", [P, 2, 2 * DM], F32R, ffn)
        f_th = sb("f_th", [P, 2 * NB, L], F32, ffn)
        xin = sb("xin", [P, 4, DM], F32, ffn)
        h_hi = sb("h_hi", [P, FT, T], F32R, ffn)
        h_lo = sb("h_lo", [P, FT, T], F32R, ffn)
        ffn.close()

        bank = [ctx.enter_context(nc.psum_tensor(f"bank{i}", [P, DM], F32)) for i in range(8)]
        B_OP, B_XT, B_S, B_YD, B_YO = bank[3:8]

        s_x = [sem(f"s_x{t}") for t in range(NT)]
        s_con, s_par, s_hp, s_wdt = (sem(n) for n in ("s_con", "s_par", "s_hp", "s_wdt"))
        s_raw = [sem(f"s_raw{i}") for i in range(2)]
        s_woraw = sem("s_woraw")
        s_cumb = [sem(f"s_cumb{i}") for i in range(2)]
        s_ecum = [sem(f"s_ecum{i}") for i in range(2)]
        s_scr = sem("s_scr")
        stats, aggr, var_eps, rstd = (sem(n) for n in ("stats", "aggr", "var_eps", "rstd"))
        const_set = sem("const_set")
        normed, xtp, xt_hi_done, xt_lo_done = (sem(n) for n in ("normed", "xtp", "xt_hi_done", "xt_lo_done"))
        wdt_split, dt_mm, pre_pe, pre_act, pre_dve = (
            sem(n) for n in ("wdt_split", "dt_mm", "pre_pe", "pre_act", "pre_dve"))
        ip_done, tap0, taps, th_done, xc_done = (sem(n) for n in ("ip_done", "tap0", "taps", "th_done", "xc_done"))
        tap_step, pre_step = sem("tap_step"), sem("pre_step")
        w_hi_done, w_lo_done, wo_hi_done, wo_lo_done = (
            sem(n) for n in ("w_hi_done", "w_lo_done", "wo_hi_done", "wo_lo_done"))
        cpar_done, cur_done = sem("cpar_done"), sem("cur_done")
        st_done, xt_done, yd_done, yo_done, dh_done, ssq_done, op_done = (
            sem(n) for n in ("st_done", "xt_done", "yd_done", "yo_done", "dh_done", "ssq_done", "op_done"))
        diff_done, e_done, sq_done, z_hi_done = sem("diff_done"), sem("e_done"), sem("sq_done"), sem("z_hi_done")
        sm_done, bt_done, xdt_done, m_done, yl_done, t1_done, y_done, h_done, z_lo_done = (
            sem(n) for n in ("sm_done", "bt_done", "xdt_done", "m_done", "yl_done", "t1_done", "y_done",
                             "h_done", "z_lo_done"))
        ms_done, oacc_done = sem("ms_done"), sem("oacc_done")
        dx_done, xw_done, hd_done, z_done, ysum_half, ysum, r_done = (
            sem(n) for n in ("dx_done", "xw_done", "hd_done", "z_done", "ysum_half", "ysum", "r_done"))
        s_xin = [sem(f"s_xin{i}") for i in range(4)]
        ln1, x2_done, x2n_done, x2tp = (sem(n) for n in ("ln1", "x2_done", "x2n_done", "x2tp"))
        s_fq, s_fs = sem("s_fq"), sem("s_fs")
        s_down = [sem(f"s_down{i}") for i in range(2)]
        f_w, f_hi_done, f_lo_done = sem("f_w"), sem("f_hi_done"), sem("f_lo_done")
        g_mm, u_mm, g_th, g_silu, hbuf_done, h_hi_done, h_lo_done, dn_mm, shift_done = (
            sem(n) for n in ("g_mm", "u_mm", "g_th", "g_silu", "hbuf_done", "h_hi_done", "h_lo_done", "dn_mm", "shift_done"))
        y_out = [sem(f"y_out{i}") for i in range(2)]
        fin_n, s_out = sem("fin_n"), sem("s_out")

        def wait(eng, s, n):
            if not isinstance(n, int) or n > 0:
                eng.wait_ge(s, n)

        def groups(eng, body):
            body(0)
            with eng.Fori(1, NG - 1) as g:
                body(g)
            body(NG - 1)

        def pairs(eng, body):
            body(0)
            with eng.Fori(1, FT // 2 - 1) as j:
                body(j)
            body(FT // 2 - 1)

        def following(b, c, u, more):
            return (b, c + 1, u) if c < NC - 1 else (1 - b, 0, u + 1) if more else None

        def half(i):
            return slice(i % 2 * DM, (i % 2 + 1) * DM)

        def x2_bank(t):
            return bank[t % 2 + t // NC * 6]

        def last_group(g):
            return isinstance(g, int) and g == NG - 1

        def steps(g):
            for b in range(NB):
                for c in range(NC):
                    more = not (b == NB - 1 and last_group(g))
                    yield b, c, g * NB + b, (g * NB + b) * NC + c, more, (g + b), 1 - b

        def wait_tile_read(eng, n, u):
            if TILES[n][0]:
                wait(eng, taps, u * NCONV + tiles_up_to(n + 1, True))
            else:
                wait(eng, xc_done, u * NTILE + n + 1)

        def cumb_loads(u, c):
            return u * (NC // 2) + c // 2 + 1

        def ecum_loads(u, c):
            return u + 1 if c == 2 else u * 2 + (c + 1) // 2

        def wait_y(eng, u, q, c):
            if c == 0:
                eng.wait_ge(yl_done, q + 1)
            else:
                eng.wait_ge(y_done, u * (NC - 1) + c)

        cumf = cumb[:].rearrange("p s h i -> p (s h i)")
        dt_raw, dt_abs = cumf[0:NH, 0:T], cumf[0:NH, T:2 * T]
        dt_e1 = ecum[:].rearrange("p s k i -> p (s k i)")[0:NH, :]
        dt_ln = xc[:, 1, 0:2, :].rearrange("p k i -> p (k i)")[0:NH, :]
        wdt_raw = xc[:, 1, 2, :].rearrange("p (k i) -> p k i", k=KT)
        dt_h, a_h, cum_h, ecum_h = dt_e1, dt_abs, dt_raw, dt_ln
        a_tok, cum_tok = (v[:].rearrange("p h d -> p (h d)") for v in (xdt, xw))
        diff_tok, w_tok = ysq[:], zbuf[:].rearrange("p k i -> p (k i)")

        block = ctx.enter_context(nc.Block())

        @block.sync
        def _(sp):
            for t in range(NT):
                sp.dma_start(oacc[:, t, :], x[t * P:(t + 1) * P, :]).then_inc(s_x[t], 16)
            sp.dma_start(con[:], consts).then_inc(s_con, 16)
            sp.dma_start(wdt_raw, wdt).then_inc(s_wdt, 16)
            sp.dma_start(hp[:, 0:2], hpar).then_inc(s_hp, 16)
            sp.dma_start(par[:], parg).then_inc(s_par, 16)

            def load_w(g, n):
                wait(sp, w_hi_done, g * NTILE + n - 1)
                wait(sp, w_lo_done, g * NTILE + n - 1)
                sp.dma_start(w_raw[:, n % 2, :], win[g, :, n, :]).then_inc(s_raw[n % 2], 16)

            def load_wo(g):
                wait(sp, wo_lo_done, g * CT)
                sp.dma_start(wo_raw[:], wo[g]).then_inc(s_woraw, 16)

            def load_chunk(g, b, c, u, q):
                t = b * NC + c
                wait(sp, yd_done, q - 1)
                sp.dma_start(cumb[:, c % 2, :, :].rearrange("p h i -> p (h i)"),
                             cum_dram[g, t, :].unsqueeze(0).broadcast_to([P, HG * Q])).then_inc(s_cumb[c % 2], 16)
                if c > 0:
                    wait(sp, y_done, u * (NC - 1) + (0, 0, -1, 1)[c])
                    for par_ in range(2):
                        sp.dma_start(ecum[par_ * HD:(par_ + 1) * HD, c % 2, :, :].rearrange("p h i -> p (h i)"),
                                     ecum_dram[g, t, par_, :].unsqueeze(0).broadcast_to([HD, CT * Q])
                                     ).then_inc(s_ecum[c % 2], 16)

            for n in range(NTILE):
                load_w(0, n)
            load_wo(0)
            sp.wait_ge(pre_dve, 15)
            for g in range(NG):
                sp.dma_start(cum_dram[g].rearrange("t (h i) -> h t i", h=HG),
                             cum_h[g * HG:(g + 1) * HG, :].rearrange("h (t i) -> h t i", t=NT)).then_inc(s_scr, 16)
                for hh in range(2):
                    sp.dma_start(ecum_dram[g, :, hh, :].rearrange("t (h i) -> h t i", h=CT),
                                 ecum_h[g * HG + hh:(g + 1) * HG:2, :].rearrange("h (t i) -> h t i", t=NT)
                                 ).then_inc(s_scr, 16)
            sp.wait_ge(s_scr, 16 * 3 * NG)
            load_chunk(0, 0, 0, 0, 0)
            load_chunk(0, 0, 1, 0, 1)

            def body(g):
                for b, c, u, q, more, gn, bn in steps(g):
                    if c < NC - 2:
                        load_chunk(g, b, c + 2, u, q + 2)
                    elif more:
                        load_chunk(gn, bn, c + 2 - NC, u + 1, q + 2)
                    st = b * NC + c
                    if not last_group(g):
                        for n in range(NTILE):
                            if SPLIT_AT[n] == st + 1:
                                load_w(g + 1, n)
                        if st == 1:
                            load_wo(g + 1)
                    if not more and c == 0:
                        sp.wait_ge(ip_done, NU * NTILE)
                        for t in range(NB * 2):
                            load_x(t)
                        load_f(0)

            def load_x(t):
                wait(sp, x2tp, t - 3)
                sp.dma_start(xin[:, t % 4, :], x[t * P:(t + 1) * P, :]).then_inc(s_xin[t % 4], 16)

            def load_f(i):
                wait(sp, f_lo_done, i)
                sp.dma_start(f_q[:], gu_q[i]).then_inc(s_fq, 16)
                sp.dma_start(f_s[:], gu_s[i].unsqueeze(0).broadcast_to([P, 2 * DM])).then_inc(s_fs, 16)

            def load_down(i):
                wait(sp, f_lo_done, FT + max(i - 1, 0))
                w = half(i)
                sp.dma_start(f_q[:, w], dn_q[i]).then_inc(s_down[i % 2], 16)
                sp.dma_start(f_s[:, w], dn_s[i].unsqueeze(0).broadcast_to([P, DM])).then_inc(s_down[i % 2], 16)

            groups(sp, body)
            for t in range(4, NT):
                load_x(t)
            with sp.Fori(1, FT) as i:
                load_f(i)
            for i in range(FT):
                load_down(i)
            for t in range(NT):
                sp.wait_ge(y_out[t % 2], t // 2 + 1)
                sp.dma_start(out[t * P:(t + 1) * P, :], oacc[:, t, :]).then_inc(s_out, 16)
            sp.wait_ge(s_out, 16 * NT)

        @block.tensor
        def _(pe):
            pe.wait_ge(s_con, 16)
            for t in range(NT):
                pe.wait_ge(normed, t + 1)
                wait(pe, xt_lo_done, t - 1)
                for k in range(KT):
                    last = nc.tensor.transpose(bank[t % 2][:, k * P:(k + 1) * P], oacc[:, t, k * P:(k + 1) * P], ident)
                last.then_inc(xtp, 1)

            def split_product(o, l_hi, l_lo, r_hi, r_lo, first, final):
                nc.tensor.matmul(o, l_hi, r_hi, start=first, stop=False)
                nc.tensor.matmul(o, l_hi, r_lo, start=False, stop=False)
                return nc.tensor.matmul(o, l_lo, r_hi, start=False, stop=final)

            pe.wait_ge(wdt_split, 2)
            pe.wait_ge(xt_lo_done, NT)
            for b in range(NB):
                s = slice(b * L, (b + 1) * L)
                for k in range(KT):
                    last = split_product(bank[2 + b][:], z_hi[:, k, :], z_lo[:, k, :], xT_hi[:, k, s], xT_lo[:, k, s],
                                         k == 0, k == KT - 1)
                last.then_inc(dt_mm, 1)

            def project(g, b, n, u):
                k0 = u * NTILE + n
                wait(pe, w_hi_done, g * NTILE + n + 1)
                wait(pe, w_lo_done, g * NTILE + n + 1)
                m, back = last_user(n, BANKS)
                wait_tile_read(pe, m, u - back)
                s = slice(b * L, (b + 1) * L)
                for k in range(KT):
                    last = split_product(bank[BANKS[n]][:], w_hi[:, n, k, :], w_lo[:, n, k, :],
                                         xT_hi[:, k, s], xT_lo[:, k, s], k == 0, k == KT - 1)
                last.then_inc(ip_done, 1)

            for n in range(2):
                project(0, 0, n, 0)
            pe.wait_ge(pre_dve, 6)
            for src, o in ((dt_h, bank[4]), (a_h, bank[5])):
                for t in range(NT):
                    last = nc.tensor.transpose(o[:, t * NH:(t + 1) * NH], src[:, t * P:(t + 1) * P], ident[0:NH, 0:NH])
                last.then_inc(pre_pe, 1)
            project(0, 0, 2, 0)
            pe.wait_ge(pre_dve, 8)
            nc.tensor.matmul(bank[6][:], tri, a_tok, start=True, stop=True).then_inc(pre_pe, 1)
            nc.tensor.matmul(bank[7][:], ones, a_tok, start=True, stop=True).then_inc(pre_pe, 1)
            project(0, 0, 3, 0)
            pe.wait_ge(pre_dve, 9)
            for t in range(NT):
                last = nc.tensor.transpose(bank[4 + t // 4][0:NH, (t % 4) * P:(t % 4 + 1) * P],
                                           cum_tok[:, t * NH:(t + 1) * NH], ident)
            last.then_inc(pre_pe, 1)
            for n in range(4, NTILE):
                project(0, 0, n, 0)

            def sum_squares(q):
                pe.wait_ge(ysum, q + 1)
                wait(pe, oacc_done, q)
                nc.tensor.matmul(B_OP[:, 0:1], ysq[:, 0:Q], ones[:, 0:1], start=True, stop=True).then_inc(ssq_done, 1)

            def out_project(g, q, changes):
                pe.wait_ge(z_hi_done, q + 1)
                pe.wait_ge(z_lo_done, q + 1)
                pe.wait_ge(wo_hi_done, (g + 1) * CT)
                pe.wait_ge(wo_lo_done, (g + 1) * CT)
                pe.wait_ge(h_done, changes)
                for k in range(CT):
                    last = split_product(B_OP[:], z_hi[:, k, :], z_lo[:, k, :], wo_hi[:, k, :], wo_lo[:, k, :],
                                         k == 0, k == CT - 1)
                last.then_inc(op_done, 1)

            def by_token(b, c, u, q):
                s = slice(c * Q, (c + 1) * Q)
                pe.wait_ge(xc_done, u * NTILE + ALL_CONV)
                wait(pe, sm_done, q)
                wait(pe, bt_done, q)
                nc.tensor.matmul(B_S[:, 0:Q], xc[:, b, 0, s], xc[:, b, 1, s], start=True, stop=True)
                nc.tensor.transpose(B_S[:, Q:2 * Q], xc[:, b, 0, s], ident).then_inc(st_done, 1)
                wait(pe, xdt_done, q)
                for k in range(CT):
                    last = nc.tensor.transpose(B_XT[:, k * P:(k + 1) * P], xc[:, b, 2 + k, s], ident)
                last.then_inc(xt_done, 1)

            by_token(0, 0, 0, 0)

            def body(g):
                for b, c, u, q, more, gn, bn in steps(g):
                    first = isinstance(q, int) and q == 0
                    if not first:
                        sum_squares(q - 1)
                    pe.wait_ge(m_done, q + 1)
                    pe.wait_ge(xdt_done, q + 1)
                    wait(pe, yl_done, q)
                    for h in range(HG):
                        last = nc.tensor.matmul(B_YD[(h % 2) * HD:(h % 2 + 1) * HD, (h // 2) * Q:(h // 2 + 1) * Q],
                                                xdt[:, h, :], cumb[:, c % 2, h, :], start=True, stop=True)
                    last.then_inc(yd_done, 1)
                    nd = u * (NC - 1) + c
                    if c > 0:
                        pe.wait_ge(h_done, nd)
                        wait(pe, t1_done, nd - 1)
                        for k in range(CT):
                            last = nc.tensor.matmul(B_YO[:, k * Q:(k + 1) * Q],
                                                    hst[:, 2 * k:2 * k + 2, :].rearrange("p h d -> p (h d)"),
                                                    xc[:, b, 1, c * Q:(c + 1) * Q], start=True, stop=True)
                        last.then_inc(yo_done, 1)
                    if c < NC - 1:
                        pe.wait_ge(xw_done, nd + 1)
                        pe.wait_ge(bt_done, q + 1)
                        wait(pe, ms_done, q)
                        nc.tensor.matmul(B_OP[:], btok[:], xw[:].rearrange("p h d -> p (h d)"),
                                         start=True, stop=True).then_inc(dh_done, 1)
                    if nxt := following(b, c, u, more):
                        by_token(*nxt, q + 1)
                    for n in SLOTS[c][0] if more else []:
                        project(gn, bn, n, u + 1)
                    if not first:
                        if c == NC - 1:
                            pe.wait_ge(ms_done, q)
                        out_project(g if b or c else g - 1, q - 1, u * (NC - 1) + min(c + 1, NC - 1))
                    for n in SLOTS[c][1] if more else []:
                        project(gn, bn, n, u + 1)
                    if not more:
                        for p, t in parts_of(ROUNDS[c]):
                            if p == 3:
                                transpose_x2(t)

            def transpose_x2(t):
                pe.wait_ge(x2n_done, t + 1)
                wait(pe, xt_lo_done, NT + t - 1)
                for k in range(KT):
                    last = nc.tensor.transpose(x2_bank(t)[:, k * P:(k + 1) * P], xin[:, t % 4, k * P:(k + 1) * P],
                                               ident)
                last.then_inc(x2tp, 1)

            groups(pe, body)
            sum_squares(NU * NC - 1)
            pe.wait_ge(ms_done, NU * NC)
            out_project(NG - 1, NU * NC - 1, NU * (NC - 1))

            def rest_of_x2(stop):
                for p, t in parts_of(range(ROUND_AFTER, NT + 3), True):
                    if p == 3 and stop - NC <= t < stop:
                        transpose_x2(t)
                pe.wait_ge(xt_lo_done, NT + stop)

            rest_of_x2(NC)

            def pair(j):
                for r in range(2):
                    i = j * 2 + r
                    pe.wait_ge(f_hi_done, i + 1)
                    pe.wait_ge(f_lo_done, i + 1)
                    for b in range(NB):
                        if isinstance(i, int) and i == 0 and b == 1:
                            rest_of_x2(NT)
                        wait(pe, hbuf_done, (i - 2) * NB + b + 1)
                        s = slice(b * L, (b + 1) * L)
                        for m, s_mm in ((0, g_mm), (1, u_mm)):
                            for k in range(KT):
                                w = slice(m * DM + k * P, m * DM + (k + 1) * P)
                                last = split_product(bank[4 * r + 2 * b + m][:], f_hi[:, r, w], f_lo[:, r, w],
                                                     xT_hi[:, k, s], xT_lo[:, k, s], k == 0, k == KT - 1)
                            last.then_inc(s_mm, 1)

            pairs(pe, pair)
            def down(i, t):
                tok = slice(t * P, (t + 1) * P)
                return split_product(bank[t][:], h_hi[:, i, tok], h_lo[:, i, tok], f_hi[:, i % 2, 0:DM],
                                     f_lo[:, i % 2, 0:DM], i == 0, i == FT - 1)

            def wait_down(i):
                pe.wait_ge(h_hi_done, (i + 1) * NB)
                pe.wait_ge(h_lo_done, (i + 1) * NB)
                pe.wait_ge(f_hi_done, FT + i + 1)
                pe.wait_ge(f_lo_done, FT + i + 1)

            for i in range(FT - 2):
                wait_down(i)
                for t in range(NT):
                    if i == 0 and t % 2 == 0:
                        pe.wait_ge(hbuf_done, (FT - 1) * NB + max(t // 2 - 1, 0))
                    last = down(i, t)
                last.then_inc(dn_mm, 1)
            wait_down(FT - 2)
            wait_down(FT - 1)
            for t in range(NT):
                down(FT - 2, t)
                down(FT - 1, t).then_inc(dn_mm, 1)

        @block.scalar
        def _(act):
            act.wait_ge(s_wdt, 16)
            nc.scalar.activation(z_hi[:], wdt_raw, ACT.Copy).then_inc(wdt_split, 1)

            def split_w(g, n):
                act.wait_ge(s_raw[n % 2], (g * (NTILE // 2) + n // 2 + 1) * 16)
                wait(act, ip_done, ((g - 1) * NB + 1) * NTILE + n + 1)
                nc.scalar.activation(w_hi[:, n, :, :].rearrange("p k c -> p (k c)"), w_raw[:, n % 2, :], ACT.Copy
                                     ).then_inc(w_hi_done, 1)

            for t in range(NT):
                act.wait_ge(xtp, t + 1)
                nc.scalar.activation(xT_hi[:, :, t * P:(t + 1) * P], bank[t % 2][:].rearrange("p (k i) -> p k i", k=KT),
                                     ACT.Copy).then_inc(xt_hi_done, 1)
            for n in range(2):
                split_w(0, n)
            act.wait_ge(s_hp, 16)
            nc.scalar.activation(hp[:, 2:3], hp[:, 1:2], ACT.Exp).then_inc(pre_act, 1)
            act.wait_ge(pre_dve, 2)
            nc.scalar.activation(dt_abs, dt_abs, ACT.Exp, scale=-1.0).then_inc(pre_act, 1)
            act.wait_ge(pre_dve, 3)
            nc.scalar.activation(dt_ln, dt_e1, ACT.Ln).then_inc(pre_act, 1)
            for n in range(2, NTILE):
                split_w(0, n)

            def first_pass(n, b, u):
                conv, k = TILES[n]
                act.wait_ge(ip_done, u * NTILE + n + 1)
                if conv:
                    act.wait_ge(cpar_done, u + 1)
                    m, back = last_user(n, ACC_SLOTS)
                    wait(act, xc_done, (u - back) * NTILE + m + 1)
                    p0 = k * (TAPS + 1)
                    nc.scalar.activation(acc[:, k % 2, :], bank[BANKS[n]][:], ACT.Identity,
                                         scale=cpar[:, b, p0 + TAPS - 1:p0 + TAPS], bias=cpar[:, b, p0 + TAPS:p0 + TAPS + 1]
                                         ).then_inc(tap0, 1)
                else:
                    wait(act, xc_done, u * NTILE + n)
                    nc.scalar.activation(th[:], bank[BANKS[n]][:], ACT.Tanh, scale=0.5).then_inc(th_done, 1)

            def second_pass(n, u):
                if TILES[n][0]:
                    act.wait_ge(taps, u * NCONV + tiles_up_to(n + 1, True))
                    wait(act, xc_done, u * NTILE + n)
                    nc.scalar.activation(th[:], acc[:, TILES[n][1] % 2, :], ACT.Tanh, scale=0.5).then_inc(th_done, 1)

            def slot(tiles, b, u):
                for n in tiles:
                    if n > 0:
                        second_pass(n - 1, u)
                    first_pass(n, b, u)

            slot(range(4), 0, 0)
            act.wait_ge(pre_pe, 4)
            act.wait_ge(pre_dve, 10)
            nc.scalar.activation(w_tok, diff_tok, ACT.Exp).then_inc(pre_act, 1)
            for b in range(NB):
                o = tab[:, b::NB, DEC, :, :].rearrange("p g c h -> p c g h")
                i_ = bank[7][:, b * (DM // 2):(b + 1) * (DM // 2)].rearrange("p (c g h) -> p c g h", c=NC, h=HG)
                nc.scalar.activation(o, i_, ACT.Exp).then_inc(pre_act, 1)
            slot([4], 0, 0)
            act.wait_ge(pre_dve, 13)
            nc.scalar.activation(ecum_h, cum_h, ACT.Exp).then_inc(pre_act, 1)
            slot(range(5, NTILE), 0, 0)

            def decays(b, c, u, q):
                act.wait_ge(s_cumb[c % 2], cumb_loads(u, c) * 16)
                act.wait_ge(cur_done, u + 1)
                for h in range(HG):
                    last = nc.scalar.activation(cumb[:, c % 2, h, :], cumb[:, c % 2, h, :], ACT.Relu, scale=-1.0,
                                                bias=cur[:, b, CUM, c, h:h + 1])
                last.then_inc(diff_done, 1)
                act.wait_ge(diff_done, q + 1)
                nc.scalar.activation(cumb[:, c % 2, :, :], cumb[:, c % 2, :, :], ACT.Exp, scale=-1.0).then_inc(e_done, 1)

            act.wait_ge(wdt_split, 2)
            act.wait_ge(dt_mm, NB)
            decays(0, 0, 0, 0)

            def body(g):
                for b, c, u, q, more, gn, bn in steps(g):
                    if nxt := following(b, c, u, more):
                        decays(*nxt, q + 1)
                    slot(SLOTS[c][0] if more else [], bn, u + 1)
                    wait_y(act, u, q, c)
                    wait(act, ssq_done, q)
                    nc.scalar.activation(ysq[:], ybuf[:].rearrange("p k i -> p (k i)"), ACT.Square).then_inc(sq_done, 1)
                    if not last_group(g):
                        for n in range(NTILE):
                            if SPLIT_AT[n] == b * NC + c:
                                split_w(g + 1, n)
                    act.wait_ge(z_done, q + 1)
                    wait(act, op_done, q)
                    nc.scalar.activation(z_hi[:], zbuf[:], ACT.Copy).then_inc(z_hi_done, 1)
                    slot(SLOTS[c][1] if more else [], bn, u + 1)
                    if b == 0 and c == 0:
                        act.wait_ge(cpar_done, u + 1)
                        wait(act, op_done, q)
                        act.wait_ge(s_woraw, (g + 1) * 16)
                        for k in range(CT):
                            nc.scalar.activation(wo_hi[:, k, :], wo_raw[:, k, :], ACT.Copy,
                                                 scale=cpar[:, b, PNW + k:PNW + k + 1]).then_inc(wo_hi_done, 1)
                    if not more:
                        for p, t in parts_of(ROUNDS[c]):
                            if p == 3:
                                copy_x2(t)
                        if c == 1:
                            split_f(0, 0)

            def copy_x2(t):
                act.wait_ge(x2tp, t + 1)
                nc.scalar.activation(xT_hi[:, :, t * P:(t + 1) * P], x2_bank(t)[:].rearrange("p (k i) -> p k i", k=KT),
                                     ACT.Copy).then_inc(xt_hi_done, 1)

            def split_f(i, slot_):
                act.wait_ge(f_w, i + 1)
                wait(act, u_mm, (i - 1) * NB)
                nc.scalar.activation(f_hi[:, slot_, :], f_s[:], ACT.Copy).then_inc(f_hi_done, 1)

            def split_down(i):
                act.wait_ge(f_w, FT + i + 1)
                if i > 1:
                    act.wait_ge(dn_mm, i - 1)
                else:
                    act.wait_ge(u_mm, (FT + i - 1) * NB)
                nc.scalar.activation(f_hi[:, i % 2, 0:DM], f_s[:, half(i)], ACT.Copy).then_inc(f_hi_done, 1)

            groups(act, body)
            for p, t in parts_of(range(ROUND_AFTER, NT + 3), True):
                if p == 3:
                    copy_x2(t)

            def pair(j):
                for r in range(2):
                    i = j * 2 + r
                    if isinstance(i, int) and i == FT - 1:
                        split_down(0)
                    else:
                        split_f(i + 1, 1 - r)
                    for b in range(NB):
                        act.wait_ge(g_mm, i * NB + b + 1)
                        wait(act, g_silu, (i - 1) * NB + b + 1)
                        nc.scalar.activation(f_th[:, b, :], bank[4 * r + 2 * b][:], ACT.Tanh, scale=0.5).then_inc(g_th, 1)
                    for b in range(NB):
                        act.wait_ge(hbuf_done, i * NB + b + 1)
                        nc.scalar.activation(h_hi[:, i, b * L:(b + 1) * L], f_th[:, 2 + b, :], ACT.Copy
                                             ).then_inc(h_hi_done, 1)

            pairs(act, pair)
            for i in range(1, FT):
                split_down(i)
            for t in range(NT):
                act.wait_ge(shift_done, t + 1)
                wait(act, y_out[t % 2], t // 2)
                nc.scalar.activation(f_th[:, t % 2, :], bank[t][:], ACT.Identity, scale=ln_rs[:, 3 * NT + t:3 * NT + t + 1],
                                     bias=ln_sh[:, t:t + 1]).then_inc(fin_n, 1)

        @block.gpsimd
        def _(pool):
            nc.gpsimd.memset(mhalf[:], -0.5).then_inc(const_set, 1)
            pool.wait_ge(const_set, 1)

            def power(k):
                pool.wait_ge(var_eps, k + 1)
                nc.gpsimd.tensor_tensor(ln_rs[:, k:k + 1], ln_ve[:, k:k + 1], mhalf[:], ALU.pow).then_inc(rstd, 1)

            def split_w(g, n):
                pool.wait_ge(w_hi_done, g * NTILE + n + 1)
                nc.gpsimd.tensor_tensor(w_lo[:, n, :, :].rearrange("p k c -> p (k c)"), w_raw[:, n % 2, :],
                                        w_hi[:, n, :, :].rearrange("p k c -> p (k c)").bitcast(F32), ALU.subtract
                                        ).then_inc(w_lo_done, 1)

            for t in range(NT):
                power(t)
            pool.wait_ge(wdt_split, 1)
            nc.gpsimd.tensor_tensor(z_lo[:], wdt_raw, z_hi[:].bitcast(F32), ALU.subtract).then_inc(wdt_split, 1)
            for n in range(NTILE):
                split_w(0, n)

            def over(table, b, c):
                return cur[:, b, table, c, :].unsqueeze(2).broadcast_to([P, HG, HD])

            def skip_term(b, c, u, q):
                pool.wait_ge(xc_done, u * NTILE + ALL_CONV)
                pool.wait_ge(cpar_done, u + 1)
                wait(pool, sq_done, q)
                wait(pool, z_done, q)
                nc.gpsimd.tensor_tensor(ybuf[:], xc[:, b, 2:2 + CT, c * Q:(c + 1) * Q],
                                        cpar[:, b, PD:PD + CT].unsqueeze(2).broadcast_to([P, CT, Q]), ALU.mult
                                        ).then_inc(dx_done, 1)

            def state_terms(b, c, u, q):
                nd = u * (NC - 1) + c
                pool.wait_ge(cur_done, u + 1)
                if c < NC - 1:
                    pool.wait_ge(xdt_done, q + 1)
                    wait(pool, dh_done, nd)
                    nc.gpsimd.tensor_tensor(xw[:], xdt[:], over(WE, b, c), ALU.mult).then_inc(xw_done, 1)
                    if c > 0:
                        pool.wait_ge(h_done, nd)
                        nc.gpsimd.tensor_tensor(hdec[:], hst[:], over(DEC, b, c), ALU.mult).then_inc(hd_done, 1)

            def root(q):
                pool.wait_ge(ms_done, q + 1)
                wait(pool, oacc_done, q)
                nc.gpsimd.tensor_tensor(rms[:, 1:2], rms[:, 0:1], mhalf[:], ALU.pow).then_inc(r_done, 1)

            state_terms(0, 0, 0, 0)
            skip_term(0, 0, 0, 0)

            def body(g):
                for b, c, u, q, more, gn, bn in steps(g):
                    if not (isinstance(q, int) and q == 0):
                        root(q - 1)
                    wait_y(pool, u, q, c)
                    pool.wait_ge(xc_done, (u + 1) * NTILE)
                    wait(pool, z_hi_done, q)
                    wait(pool, z_lo_done, q)
                    nc.gpsimd.tensor_tensor(zbuf[:], ybuf[:], gate[:, b, :, c * Q:(c + 1) * Q], ALU.mult
                                            ).then_inc(z_done, 1)
                    nxt = following(b, c, u, more)
                    if nxt:
                        state_terms(*nxt, q + 1)
                    pool.wait_ge(sq_done, q + 1)
                    nc.gpsimd.tensor_tensor(ysq[:, 0:2 * Q], ysq[:, 0:2 * Q], ysq[:, 2 * Q:4 * Q], ALU.add
                                            ).then_inc(ysum_half, 1)
                    pool.wait_ge(ysum_half, q + 1)
                    nc.gpsimd.tensor_tensor(ysq[:, 0:Q], ysq[:, 0:Q], ysq[:, Q:2 * Q], ALU.add).then_inc(ysum, 1)
                    if nxt:
                        skip_term(*nxt, q + 1)
                    pool.wait_ge(z_hi_done, q + 1)
                    wait(pool, op_done, q)
                    nc.gpsimd.tensor_tensor(z_lo[:], zbuf[:], z_hi[:].bitcast(F32), ALU.subtract).then_inc(z_lo_done, 1)
                    if not last_group(g):
                        for n in range(NTILE):
                            if SPLIT_AT[n] == b * NC + c:
                                split_w(g + 1, n)
                    if not more:
                        powers_x2(parts_of(ROUNDS[c]))
                        if c == 1:
                            split_f(0, 0, slice(0, 2 * DM))

            def powers_x2(parts):
                for p, t in parts:
                    if p < 2:
                        power(NT + 2 * t + p)

            def split_f(k, slot_, src):
                w = src.stop - src.start
                pool.wait_ge(f_hi_done, k + 1)
                nc.gpsimd.tensor_tensor(f_lo[:, slot_, 0:w], f_s[:, src], f_hi[:, slot_, 0:w].bitcast(F32), ALU.subtract
                                        ).then_inc(f_lo_done, 1)

            def add_residual(t):
                pool.wait_ge(fin_n, t + 1)
                nc.gpsimd.tensor_tensor(oacc[:, t, :], oacc[:, t, :], f_th[:, 0, :], ALU.add).then_inc(y_out[0], 1)

            groups(pool, body)
            root(NU * NC - 1)
            powers_x2(parts_of(range(ROUND_AFTER, NT + 3), True))
            with pool.Fori(0, FT // 2 - 1) as j:
                for r in range(2):
                    split_f(j * 2 + r + 1, 1 - r, slice(0, 2 * DM))
            split_f(FT - 1, 1, slice(0, 2 * DM))
            for i in range(FT):
                split_f(FT + i, i % 2, half(i))
            for t in range(NT):
                power(3 * NT + t)
                if t % 2 == 1:
                    add_residual(t - 1)

        @block.vector
        def _(dve):
            def moments(k, src):
                nc.vector.bn_stats(ln_st[:, k, :], src).then_inc(stats, 1)
                dve.wait_ge(stats, k + 1)
                nc.vector.bn_aggr(ln_mv[:, k, :], ln_st[:, k, :]).then_inc(aggr, 1)
                dve.wait_ge(aggr, k + 1)
                nc.vector.tensor_scalar(ln_ve[:, k:k + 1], ln_mv[:, k, 1:2], EPS, None, ALU.add).then_inc(var_eps, 1)

            def normalize(k, dst, src):
                dve.wait_ge(rstd, k + 1)
                return nc.vector.tensor_scalar(dst, src, ln_mv[:, k, 0:1], ln_rs[:, k:k + 1], ALU.subtract, ALU.mult)

            for t in range(NT + 1):
                if t < NT:
                    dve.wait_ge(s_x[t], 16)
                    moments(t, oacc[:, t, :])
                if t > 0:
                    normalize(t - 1, oacc[:, t - 1, :], oacc[:, t - 1, :]).then_inc(normed, 1)

            def copy_params(g, b, u):
                if not (isinstance(u, int) and u < 2):
                    q0 = (u - 1) * NC
                    dve.wait_ge(dx_done, q0)
                    dve.wait_ge(e_done, q0)
                    dve.wait_ge(xw_done, (u - 1) * (NC - 1))
                    dve.wait_ge(hd_done, (u - 1) * (NC - 2))
                    if b == 0:
                        dve.wait_ge(wo_hi_done, g * CT)
                if not (isinstance(u, int) and u == 0):
                    nc.vector.tensor_copy(cpar[:, b, :], par[:, g, :]).then_inc(cpar_done, 1)
                nc.vector.tensor_copy(cur[:, b, :, :, :].rearrange("p k c h -> p (k c h)"),
                                      tab[:, u, :, :, :].rearrange("p k c h -> p (k c h)")).then_inc(cur_done, 1)

            for t in range(NT):
                dve.wait_ge(xt_hi_done, t + 1)
                sl = slice(t * P, (t + 1) * P)
                nc.vector.tensor_tensor(xT_lo[:, :, sl], bank[t % 2][:].rearrange("p (k i) -> p k i", k=KT),
                                        xT_hi[:, :, sl].bitcast(F32), ALU.subtract).then_inc(xt_lo_done, 1)
            def first_use(n, b, u):
                conv, k = TILES[n]
                if conv:
                    done = u * NCONV + tiles_up_to(n, True)
                    dve.wait_ge(tap0, done + 1)
                    dve.wait_ge(cpar_done, u + 1)
                    p0 = k * (TAPS + 1)
                    for d in range(1, TAPS):
                        last = nc.vector.scalar_tensor_tensor(
                            out=acc[:, k % 2, d:L], in0=bank[BANKS[n]][:, 0:L - d],
                            scalar=cpar[:, b, p0 + TAPS - 1 - d:p0 + TAPS - d], in1=acc[:, k % 2, d:L],
                            op0=ALU.mult, op1=ALU.add)
                        if d < TAPS - 1:
                            last.then_inc(tap_step, 1)
                            dve.wait_ge(tap_step, done * (TAPS - 2) + d)
                    last.then_inc(taps, 1)
                else:
                    dve.wait_ge(th_done, u * NTILE + n + 1)
                    wait(dve, z_done, (u - 1) * NC)
                    nc.vector.scalar_tensor_tensor(out=gate[:, b, k, :], in0=th[:], scalar=1.0,
                                                   in1=bank[BANKS[n]][:], op0=ALU.add, op1=ALU.mult).then_inc(xc_done, 1)

            def second_use(n, b, u):
                conv, k = TILES[n]
                if conv:
                    dve.wait_ge(th_done, u * NTILE + n + 1)
                    wait(dve, dx_done, (u - 1) * NC)
                    wait(dve, yd_done, (u - 1) * NC)
                    wait(dve, yo_done, (u - 1) * (NC - 1))
                    nc.vector.scalar_tensor_tensor(out=xc[:, b, k, :], in0=th[:], scalar=1.0, in1=acc[:, k % 2, :],
                                                   op0=ALU.add, op1=ALU.mult).then_inc(xc_done, 1)

            def slot(tiles, b, u, before_last=None):
                for n in tiles:
                    if n > 0:
                        second_use(n - 1, b, u)
                    if before_last and n == tiles[-1]:
                        before_last()
                    first_use(n, b, u)

            dve.wait_ge(s_par, 16)
            nc.vector.tensor_scalar(par[:, :, PD:PD + 2 * CT], par[:, :, PD:PD + 2 * CT], 0.5, None, ALU.mult
                                    ).then_inc(pre_dve, 1)
            dve.wait_ge(pre_dve, 1)
            nc.vector.tensor_copy(cpar[:, 0, :], par[:, 0, :]).then_inc(cpar_done, 1)
            dve.wait_ge(s_hp, 16)
            dve.wait_ge(dt_mm, NB)
            for b in range(NB):
                last = nc.vector.tensor_scalar(dt_raw[:, b * L:(b + 1) * L], bank[2 + b][0:NH, :], hp[:, 0:1], None, ALU.add)
            last.then_inc(pre_step, 1)
            dve.wait_ge(pre_step, 1)
            nc.vector.scalar_tensor_tensor(out=dt_abs, in0=dt_raw, scalar=-1.0, in1=dt_raw, op0=ALU.mult, op1=ALU.max
                                           ).then_inc(pre_dve, 1)
            dve.wait_ge(pre_act, 2)
            nc.vector.tensor_scalar(dt_e1, dt_abs, 1.0, None, ALU.add).then_inc(pre_dve, 1)
            dve.wait_ge(pre_dve, 3)
            nc.vector.scalar_tensor_tensor(out=dt_abs, in0=dt_e1, scalar=-1.0, in1=dt_abs, op0=ALU.add, op1=ALU.subtract
                                           ).then_inc(pre_step, 1)
            dve.wait_ge(pre_step, 2)
            dve.wait_ge(pre_act, 3)
            nc.vector.tensor_tensor(dt_ln, dt_ln, dt_abs, ALU.subtract).then_inc(pre_step, 1)
            nc.vector.tensor_scalar(hp[:, 3:4], hp[:, 2:3], -1.0, None, ALU.mult).then_inc(pre_dve, 1)
            dve.wait_ge(pre_step, 3)
            dve.wait_ge(pre_dve, 4)
            nc.vector.scalar_tensor_tensor(out=dt_h, in0=dt_raw, scalar=0.0, in1=dt_ln, op0=ALU.max, op1=ALU.add
                                           ).then_inc(pre_dve, 1)
            dve.wait_ge(pre_dve, 5)
            nc.vector.tensor_scalar(a_h, dt_h, hp[:, 3:4], None, ALU.mult).then_inc(pre_dve, 1)

            def by_unit(table, b):
                return tab[:, b::NB, table, :, :].rearrange("p g c h -> p c g h")

            def by_token(flat, b):
                return flat[:, b * (DM // 2):(b + 1) * (DM // 2)].rearrange("p (c g h) -> p c g h", c=NC, h=HG)

            slot([0], 0, 0)
            dve.wait_ge(pre_pe, 1)
            for b in range(NB):
                last = nc.vector.tensor_scalar(by_unit(DT, b), by_token(bank[4][:], b), 0.5, None, ALU.mult)
            last.then_inc(pre_dve, 1)
            dve.wait_ge(pre_pe, 2)
            nc.vector.tensor_copy(a_tok, bank[5][:]).then_inc(pre_dve, 1)
            slot([1], 0, 0)
            dve.wait_ge(pre_pe, 3)
            nc.vector.tensor_copy(cum_tok, bank[6][:]).then_inc(pre_dve, 1)
            dve.wait_ge(pre_pe, 4)
            dve.wait_ge(pre_dve, 9)
            nc.vector.tensor_tensor(diff_tok, bank[7][:], cum_tok, ALU.subtract).then_inc(pre_dve, 1)
            for b in range(NB):
                last = nc.vector.tensor_copy(by_unit(CUM, b), by_token(cum_tok, b))
            last.then_inc(pre_dve, 1)
            slot([2, 3], 0, 0)
            dve.wait_ge(pre_pe, 5)
            for k in range(2):
                nc.vector.tensor_copy(cum_h[:, k * 4 * P:(k + 1) * 4 * P], bank[4 + k][0:NH, :]).then_inc(pre_dve, 1)
            dve.wait_ge(pre_act, 4)
            for b in range(NB):
                last = nc.vector.tensor_scalar(by_unit(WE, b), by_token(w_tok, b), 0.5, None, ALU.mult)
            last.then_inc(pre_dve, 1)
            slot([4], 0, 0)
            dve.wait_ge(pre_act, 7)
            nc.vector.tensor_scalar(ecum_h, ecum_h, 0.5, None, ALU.mult).then_inc(pre_dve, 1)
            dve.wait_ge(pre_dve, 15)
            copy_params(0, 0, 0)
            nc.vector.memset(oacc[:, NT - 1, :], 0.0).then_inc(pre_step, 1)
            slot(range(5, NTILE), 0, 0)
            dve.wait_ge(pre_step, 4)

            def mean_square(q):
                dve.wait_ge(ssq_done, q + 1)
                wait(dve, r_done, q)
                nc.vector.tensor_scalar(rms[:, 0:1], B_OP[:, 0:1], 1.0 / GW, EPS, ALU.mult, ALU.add
                                        ).then_inc(ms_done, 1)

            def gather_out(g, t, q):
                dve.wait_ge(op_done, q + 1)
                dve.wait_ge(r_done, q + 1)
                if isinstance(g, int) and g == 0:
                    nc.vector.tensor_scalar(oacc[:, t, :], B_OP[:], rms[:, 1:2], None, ALU.mult).then_inc(oacc_done, 1)
                else:
                    nc.vector.scalar_tensor_tensor(out=oacc[:, t, :], in0=B_OP[:], scalar=rms[:, 1:2], in1=oacc[:, t, :],
                                                   op0=ALU.mult, op1=ALU.add).then_inc(oacc_done, 1)

            def matrix(b, c, u, q):
                nd = u * (NC - 1) + c
                dve.wait_ge(st_done, q + 1)
                wait(dve, dh_done, nd)
                nc.vector.tensor_tensor(smask[:], B_S[:, 0:Q], mask4, ALU.mult).then_inc(sm_done, 1)
                nc.vector.tensor_copy(btok[:], B_S[:, Q:2 * Q]).then_inc(bt_done, 1)
                dve.wait_ge(xt_done, q + 1)
                wait(dve, yd_done, q)
                wait(dve, xw_done, nd)
                dve.wait_ge(cur_done, u + 1)
                nc.vector.tensor_tensor(xdt[:], B_XT[:].rearrange("p (h d) -> p h d", h=HG),
                                        cur[:, b, DT, c, :].unsqueeze(2).broadcast_to([P, HG, HD]), ALU.mult
                                        ).then_inc(xdt_done, 1)
                dve.wait_ge(e_done, q + 1)
                dve.wait_ge(sm_done, q + 1)
                nc.vector.tensor_tensor(cumb[:, c % 2, :, :], cumb[:, c % 2, :, :], smask[:].unsqueeze(1).broadcast_to([P, HG, Q]), ALU.mult
                                        ).then_inc(m_done, 1)

            matrix(0, 0, 0, 0)

            def body(g):
                for b, c, u, q, more, gn, bn in steps(g):
                    first = isinstance(q, int) and q == 0
                    nd = u * (NC - 1) + c
                    dve.wait_ge(yd_done, q + 1)
                    dve.wait_ge(dx_done, q + 1)
                    nc.vector.tensor_tensor(ybuf[:], B_YD[:].rearrange("p (k i) -> p k i", k=CT), ybuf[:], ALU.add
                                            ).then_inc(yl_done, 1)
                    if c > 0:
                        dve.wait_ge(yo_done, nd)
                        dve.wait_ge(s_ecum[c % 2], ecum_loads(u, c) * 32)
                        nc.vector.tensor_tensor(ecum[:, c % 2, :, :], B_YO[:].rearrange("p (k i) -> p k i", k=CT),
                                                ecum[:, c % 2, :, :], ALU.mult).then_inc(t1_done, 1)
                        dve.wait_ge(yl_done, q + 1)
                        dve.wait_ge(t1_done, nd)
                        nc.vector.tensor_tensor(ybuf[:], ybuf[:], ecum[:, c % 2, :, :], ALU.add).then_inc(y_done, 1)
                    if c < NC - 1:
                        dve.wait_ge(dh_done, nd + 1)
                        hflat = hst[:].rearrange("p h d -> p (h d)")
                        if c == 0:
                            wait(dve, yo_done, u * (NC - 1))
                            nc.vector.tensor_copy(hflat, B_OP[:]).then_inc(h_done, 1)
                        else:
                            dve.wait_ge(hd_done, u * (NC - 2) + c)
                            nc.vector.tensor_tensor(hflat, B_OP[:], hdec[:].rearrange("p h d -> p (h d)"), ALU.add
                                                    ).then_inc(h_done, 1)
                    if nxt := following(b, c, u, more):
                        matrix(*nxt, q + 1)
                    if c == 0 and more:
                        copy_params(gn, bn, u + 1)
                    slot(SLOTS[c][0] if more else [], bn, u + 1)
                    if not first:
                        gather_out(g if b or c else g - 1, (b * NC + c - 1) % NT, q - 1)
                    if more:
                        slot(SLOTS[c][1], bn, u + 1, lambda: mean_square(q))
                    else:
                        mean_square(q)
                        if c == 1:
                            dequant(0)
                        for p, t in parts_of(ROUNDS[c]):
                            x2_part(p, t)
                    if b == 0 and c == 0:
                        for k in range(CT):
                            dve.wait_ge(wo_hi_done, g * CT + k + 1)
                            nc.vector.scalar_tensor_tensor(out=wo_lo[:, k, :], in0=wo_raw[:, k, :],
                                                           scalar=cpar[:, b, PNW + k:PNW + k + 1],
                                                           in1=wo_hi[:, k, :].bitcast(F32), op0=ALU.mult,
                                                           op1=ALU.subtract).then_inc(wo_lo_done, 1)

            def x2_part(p, t):
                k = NT + 2 * t
                if p == 0:
                    dve.wait_ge(oacc_done, NU * NC - NT + t + 1)
                    moments(k, oacc[:, t, :])
                elif p == 1:
                    normalize(k, oacc[:, t, :], oacc[:, t, :]).then_inc(ln1, 1)
                    dve.wait_ge(ln1, t + 1)
                    dve.wait_ge(s_xin[t % 4], (t // 4 + 1) * 16)
                    nc.vector.tensor_tensor(oacc[:, t, :], oacc[:, t, :], xin[:, t % 4, :], ALU.add).then_inc(x2_done, 1)
                    dve.wait_ge(x2_done, t + 1)
                    moments(k + 1, oacc[:, t, :])
                elif p == 2:
                    normalize(k + 1, xin[:, t % 4, :], oacc[:, t, :]).then_inc(x2n_done, 1)
                else:
                    dve.wait_ge(xt_hi_done, NT + t + 1)
                    sl = slice(t * P, (t + 1) * P)
                    nc.vector.tensor_tensor(xT_lo[:, :, sl], x2_bank(t)[:].rearrange("p (k i) -> p k i", k=KT),
                                            xT_hi[:, :, sl].bitcast(F32), ALU.subtract).then_inc(xt_lo_done, 1)

            def dequant(i):
                dve.wait_ge(s_fq, (i + 1) * 16)
                dve.wait_ge(s_fs, (i + 1) * 16)
                nc.vector.tensor_tensor(f_s[:], f_q[:], f_s[:], ALU.mult).then_inc(f_w, 1)

            def dequant_down(i):
                dve.wait_ge(s_down[i % 2], (i // 2 + 1) * 32)
                nc.vector.scalar_tensor_tensor(out=f_s[:, half(i)], in0=f_q[:, half(i)], scalar=0.5, in1=f_s[:, half(i)],
                                               op0=ALU.mult, op1=ALU.mult).then_inc(f_w, 1)

            groups(dve, body)
            gather_out(NG - 1, NT - 1, NU * NC - 1)
            for p, t in parts_of(range(ROUND_AFTER, NT + 3), True):
                x2_part(p, t)

            def pair(j):
                for r in range(2):
                    i = j * 2 + r
                    if isinstance(i, int) and i == FT - 1:
                        dequant_down(0)
                    else:
                        dequant(i + 1)
                    for b in range(NB):
                        n = i * NB + b
                        hb = f_th[:, 2 + b, :]
                        dve.wait_ge(g_th, n + 1)
                        wait(dve, h_hi_done, (i - 1) * NB + b + 1)
                        wait(dve, h_lo_done, (i - 1) * NB + b + 1)
                        nc.vector.scalar_tensor_tensor(out=hb, in0=f_th[:, b, :], scalar=1.0,
                                                       in1=bank[4 * r + 2 * b][:], op0=ALU.add, op1=ALU.mult
                                                       ).then_inc(g_silu, 1)
                        dve.wait_ge(u_mm, n + 1)
                        dve.wait_ge(g_silu, n + 1)
                        nc.vector.tensor_tensor(hb, bank[4 * r + 2 * b + 1][:], hb, ALU.mult).then_inc(hbuf_done, 1)
                        dve.wait_ge(h_hi_done, n + 1)
                        hs = (slice(None), i, slice(b * L, (b + 1) * L))
                        nc.vector.tensor_tensor(h_lo[hs], hb, h_hi[hs].bitcast(F32), ALU.subtract).then_inc(h_lo_done, 1)

            pairs(dve, pair)
            for i in range(1, FT):
                dequant_down(i)

            def shift(t):
                k = 3 * NT + t
                dve.wait_ge(rstd, k + 1)
                nc.vector.scalar_tensor_tensor(out=ln_sh[:, t:t + 1], in0=ln_mv[:, k, 0:1], scalar=-1.0, in1=ln_rs[:, k:k + 1],
                                               op0=ALU.mult, op1=ALU.mult).then_inc(shift_done, 1)

            def add_residual(t):
                dve.wait_ge(fin_n, t + 1)
                nc.vector.tensor_tensor(oacc[:, t, :], oacc[:, t, :], f_th[:, 1, :], ALU.add).then_inc(y_out[1], 1)

            for t in range(NT):
                dve.wait_ge(dn_mm, FT - 2 + t + 1)
                moments(3 * NT + t, bank[t][:])
                if t > 0:
                    shift(t - 1)
                if t > 2 and t % 2 == 1:
                    add_residual(t - 2)
            shift(NT - 1)
            add_residual(NT - 1)


def lay_out(a):
    import numpy as np

    w = a["L0_attn_in_proj_w"]
    gate_rows, x_rows = w[:NG * GW], w[NG * GW:2 * NG * GW]
    b_rows, c_rows = w[2 * NG * GW:2 * NG * GW + NG * NS], w[2 * NG * GW + NG * NS:2 * NG * (GW + NS)]
    dt_rows = w[-NH:]

    def tiles(rows, n):
        return rows.reshape(NG, n, P, KT, P).transpose(0, 4, 1, 3, 2)

    conv_tiles = np.concatenate([tiles(b_rows, 1), tiles(c_rows, 1), tiles(x_rows, CT)], axis=2)
    gate_tiles = tiles(gate_rows, CT)
    win = np.stack([(conv_tiles if conv else gate_tiles)[:, :, k] for conv, k in TILES], axis=2)
    wdt = np.zeros((P, KT, P), np.float32)
    wdt[:, :, :NH] = dt_rows.reshape(NH, KT, P).transpose(2, 1, 0)
    wo = a["L0_attn_out_proj_w"].reshape(DM, NG, CT, P).transpose(1, 3, 2, 0)

    cw, cb = a["L0_attn_conv_weight"], a["L0_attn_conv_bias"]
    conv = np.concatenate([cw, cb[:, None]], axis=1)
    cx, cB, cC = conv[:NG * GW], conv[NG * GW:NG * (GW + NS)], conv[NG * (GW + NS):]

    def by_partition(v, n):
        return v.reshape(NG, n, P, -1).transpose(2, 0, 1, 3).reshape(P, NG, -1)

    skip = np.repeat(a["L0_attn_D"], HD)
    parg = np.concatenate([by_partition(cB, 1), by_partition(cC, 1), by_partition(cx, CT), by_partition(skip, CT),
                           by_partition(a["L0_attn_norm_weight"], CT)], axis=2)
    hpar = np.stack([a["L0_attn_dt_bias"], a["L0_attn_A_log"]], axis=1)
    i = np.arange(P)
    tri = (i[:, None] <= i[None, :]).astype(np.float32)
    consts = np.stack([np.eye(P, dtype=np.float32), tri, tri * np.float32(0.25), np.ones((P, P), np.float32)], axis=1)

    gq, uq = (a[f"L0_ffn_{n}_q"].reshape(FT, P, KT, P).transpose(0, 3, 2, 1) for n in ("gate", "up"))
    gs, us = (a[f"L0_ffn_{n}_s"].reshape(FT, P, KT).transpose(0, 2, 1) for n in ("gate", "up"))
    return {
        "x": a["L0_attn_hidden_states"].reshape(T, DM),
        "win": win.reshape(NG, P, NTILE, KT * P),
        "wdt": wdt,
        "wo": wo,
        "parg": parg,
        "hpar": hpar,
        "consts": consts,
        "gu_q": np.stack([gq, uq], axis=2).reshape(FT, P, 2 * DM),
        "gu_s": np.stack([gs, us], axis=1).reshape(FT, 2 * DM),
        "dn_q": a["L0_ffn_down_q"].reshape(DM, FT, P).transpose(1, 2, 0),
        "dn_s": a["L0_ffn_down_s"].T,
    }


def kernel(**inputs):
    import numpy as np
    import concourse.bacc as bacc
    from concourse.bass_utils import run_bass_kernel_spmd

    nc = bacc.Bacc("TRN2", target_bir_lowering=False, num_devices=1)
    arrays, args = {}, {}
    for name, v in lay_out({k: np.asarray(v) for k, v in inputs.items()}).items():
        v = np.ascontiguousarray(v)
        arrays[f"in_{name}"] = v
        args[name] = nc.dram_tensor(f"in_{name}", v.shape, mybir.dt.from_np(v.dtype), kind="ExternalInput").ap()
    out = nc.dram_tensor("out_0", (T, DM), F32, kind="ExternalOutput").ap()
    mixer_and_ffn(nc, out=out, **args)
    got = run_bass_kernel_spmd(nc, [arrays], core_ids=[0]).results[0]["out_0"]
    return got.reshape(NB, L, DM)
```

```python
from contextlib import ExitStack

import concourse.bass as bass
from concourse import mybir

F32 = mybir.dt.float32
F32R = mybir.dt.float32r
I32 = mybir.dt.int32
ALU = mybir.AluOpType
ACT = mybir.ActivationFunctionType

P = 128
DM = 512
NB, L = 2, 512
T = NB * L
NH, HD, NS = 64, 64, 128
NG = 8
HG = NH // NG
Q = 128
NC = L // Q
NT = T // Q
KT = DM // P
GW = HG * HD
CT = GW // P
NTILE = 2 + 2 * CT
NCONV = 2 + CT
TAPS = 4
NPAR = NCONV * (TAPS + 1) + 2 * CT
PD, PNW = NCONV * (TAPS + 1), NCONV * (TAPS + 1) + CT
FI = 1792
FT = FI // P
KS = KT - 1
SW = KS * P
EPS = 1e-5
NU = NB * NG
DT, WE, CUM, DEC = range(4)

TILES = [(True, 0), (True, 1), (True, 2), (False, 0), (True, 3), (True, 4), (True, 5), (False, 1), (False, 2), (False, 3)]
BANKS = [0, 1, 2, 0, 1, 2, 0, 1, 2, 1]
ACC_SLOTS = [k % 2 if conv else None for conv, k in TILES]
ALL_CONV = 7
SLOTS = [([0], [1]), ([2, 3], [4]), ([5], [6, 7]), ([8], [9])]
SPLIT_AT = [1, 1, 2, 2, 3, 3, 4, 4, 5, 5]


AFTER = 2 * NC - 1


def tiles_in_part(p, rounds):
    return [r - p for r in rounds if 0 <= r - p < NT]


def tiles_up_to(n, conv):
    return sum(k == conv for k, _ in TILES[:n])


def last_user(n, same):
    back = [m for m in range(n) if same[m] == same[n]]
    return (back[-1], 0) if back else (max(m for m in range(NTILE) if same[m] == same[n]), 1)


def mixer_and_ffn(nc, x, win, wdt, wo, parg, hpar, consts, gu_q, gu_s, gu_last, dn_q, dn_s, out):
    cum_dram = nc.dram_tensor("cum_dram", [NB * NH, L], F32, kind="Internal").ap()
    ecum_dram = nc.dram_tensor("ecum_dram", [NB * NH, L], F32, kind="Internal").ap()
    cum_rows = cum_dram.rearrange("(b g h) (c i) -> g b c h i", b=NB, g=NG, c=NC)
    ecum_rows = ecum_dram.rearrange("(b g k s) (c i) -> g b c s k i", b=NB, g=NG, k=CT, c=NC)

    with ExitStack() as ctx:
        def sem(name):
            return ctx.enter_context(nc.semaphore(name))

        def sb(name, shape, dt, scope=ctx):
            return scope.enter_context(nc.sbuf_tensor(name, shape, dt))

        xT_hi = sb("xT_hi", [P, KT, T], F32R)
        xT_lo = sb("xT_lo", [P, KT, T], F32R)
        oacc = sb("oacc", [P, NT, DM], F32)
        con = sb("con", [P, 4, P], F32)
        ln_st = sb("ln_st", [P, 32, 6], F32)
        ln_mv = sb("ln_mv", [P, 32, 2], F32)
        ln_ve = sb("ln_ve", [P, 32], F32)
        ln_rs = sb("ln_rs", [P, 32], F32)
        ln_sh = sb("ln_sh", [P, 2 * NT], F32)
        mhalf = sb("mhalf", [P, 1], F32)
        ident, tri, mask4, ones = (con[:, i, :] for i in range(4))
        mix = ExitStack()
        wo_raw = sb("wo_raw", [P, CT, DM], F32, mix)
        w_hi = sb("w_hi", [P, NTILE, KT, P], F32R, mix)
        w_lo = sb("w_lo", [P, NTILE, KT, P], F32R, mix)
        wo_hi = sb("wo_hi", [P, CT, DM], F32R, mix)
        wo_lo = sb("wo_lo", [P, CT, DM], F32R, mix)
        w_raw = sb("w_raw", [P, 2, KT * P], F32, mix)
        xc = sb("xc", [P, NB, NCONV, L], F32, mix)
        gate = sb("gate", [P, NB, CT, L], F32, mix)
        acc = sb("acc", [P, 2, L], F32, mix)
        th = sb("th", [P, L], F32, mix)
        cumb = sb("cumb", [P, 2, HG, Q], F32, mix)
        ecum = sb("ecum", [P, 2, CT, Q], F32, mix)
        smask = sb("smask", [P, Q], F32, mix)
        btok = sb("btok", [P, NS], F32, mix)
        xdt = sb("xdt", [P, HG, HD], F32, mix)
        xw = sb("xw", [P, HG, HD], F32, mix)
        ybuf = sb("ybuf", [P, CT, Q], F32, mix)
        ysq = sb("ysq", [P, CT * Q], F32, mix)
        zbuf = sb("zbuf", [P, CT, Q], F32, mix)
        z_hi = sb("z_hi", [P, CT, Q], F32R, mix)
        z_lo = sb("z_lo", [P, CT, Q], F32R, mix)
        hst = sb("hst", [P, HG, HD], F32, mix)
        hdec = sb("hdec", [P, HG, HD], F32, mix)
        tab = sb("tab", [P, NU, 4, NC, HG], F32, mix)
        cur = sb("cur", [P, NB, 4, NC, HG], F32, mix)
        par = sb("par", [P, NG, NPAR], F32, mix)
        cpar = sb("cpar", [P, NB, NPAR], F32, mix)
        hp = sb("hp", [P, 4], F32, mix)
        rms = sb("rms", [P, 2], F32, mix)
        mix.close()
        ffn = ExitStack()
        xin = sb("xin", [P, 4, DM], F32, ffn)
        f_q = sb("f_q", [P, 2 * DM], I32, ffn)
        f_s = sb("f_s", [P, 2 * DM], F32, ffn)
        f_last = sb("f_last", [P, FT // 2, 4], F32, ffn)
        f_pair = sb("f_pair", [P, 2, 2], F32, ffn)
        f_hi = sb("f_hi", [P, 2, 2 * DM], F32R, ffn)
        f_lo = sb("f_lo", [P, 2, 2 * DM], F32R, ffn)
        f_g = sb("f_g", [P, 2, L], F32, ffn)
        f_u = sb("f_u", [P, 2, L], F32, ffn)
        f_th = sb("f_th", [P, L], F32, ffn)
        h_hi = sb("h_hi", [P, FT, T], F32R, ffn)
        h_lo = sb("h_lo", [P, FT, T], F32R, ffn)
        ffn.close()

        bank = [ctx.enter_context(nc.psum_tensor(f"bank{i}", [P, DM], F32)) for i in range(8)]
        B_OP, B_XT, B_S, B_YD, B_YO = bank[3:8]

        s_x = [sem(f"s_x{t}") for t in range(NT)]
        s_con, s_par, s_hp, s_wdt = (sem(n) for n in ("s_con", "s_par", "s_hp", "s_wdt"))
        s_raw = [sem(f"s_raw{i}") for i in range(2)]
        s_first = [sem(f"s_first{n}") for n in range(2, NTILE)]
        s_woraw = sem("s_woraw")
        s_cumb = [sem(f"s_cumb{i}") for i in range(2)]
        s_ecum = [sem(f"s_ecum{i}") for i in range(2)]
        s_scr = sem("s_scr")
        stats, aggr, var_eps, rstd = (sem(n) for n in ("stats", "aggr", "var_eps", "rstd"))
        const_set = sem("const_set")
        normed, xtp, xt_hi_done, xt_lo_done = (sem(n) for n in ("normed", "xtp", "xt_hi_done", "xt_lo_done"))
        wdt_split, dt_mm, pre_pe, pre_act, pre_dve = (
            sem(n) for n in ("wdt_split", "dt_mm", "pre_pe", "pre_act", "pre_dve"))
        ip_done, tap0, taps, th_done, xc_done = (sem(n) for n in ("ip_done", "tap0", "taps", "th_done", "xc_done"))
        tap_step, pre_step = sem("tap_step"), sem("pre_step")
        w_hi_done, w_lo_done, wo_scaled, wo_hi_done, wo_lo_done = (
            sem(n) for n in ("w_hi_done", "w_lo_done", "wo_scaled", "wo_hi_done", "wo_lo_done"))
        cpar_done, cur_done = sem("cpar_done"), sem("cur_done")
        st_done, xt_done, yd_done, yo_done, dh_done, ssq_done, op_done = (
            sem(n) for n in ("st_done", "xt_done", "yd_done", "yo_done", "dh_done", "ssq_done", "op_done"))
        diff_done, e_done, sq_done, z_hi_done = sem("diff_done"), sem("e_done"), sem("sq_done"), sem("z_hi_done")
        sm_done, bt_done, xdt_done, m_done, yl_done, t1_done, y_done, h_done, z_lo_done = (
            sem(n) for n in ("sm_done", "bt_done", "xdt_done", "m_done", "yl_done", "t1_done", "y_done",
                             "h_done", "z_lo_done"))
        ms_done, oacc_done = sem("ms_done"), sem("oacc_done")
        dx_done, xw_done, hd_done, z_done, ysum_half, ysum, r_done = (
            sem(n) for n in ("dx_done", "xw_done", "hd_done", "z_done", "ysum_half", "ysum", "r_done"))
        s_xin = [sem(f"s_xin{i}") for i in range(4)]
        x2_done, x2n_done, x2tp = (sem(n) for n in ("x2_done", "x2n_done", "x2tp"))
        s_fq, s_fs = sem("s_fq"), sem("s_fs")
        s_down = [sem(f"s_down{i}") for i in range(2)]
        s_flast, f_pair_done, f_levels = sem("s_flast"), sem("f_pair_done"), sem("f_levels")
        f_w, f_hi_done, f_lo_done, g_last, u_last, g_sum, u_sum = (
            sem(n) for n in ("f_w", "f_hi_done", "f_lo_done", "g_last", "u_last", "g_sum", "u_sum"))
        g_mm, u_mm, g_th, g_silu, hbuf_done, h_hi_done, h_lo_done, dn_mm, shift_done = (
            sem(n) for n in ("g_mm", "u_mm", "g_th", "g_silu", "hbuf_done", "h_hi_done", "h_lo_done", "dn_mm", "shift_done"))
        y_out = [sem(f"y_out{i}") for i in range(2)]
        fin_n, s_out = sem("fin_n"), sem("s_out")

        def wait(eng, s, n):
            if not isinstance(n, int) or n > 0:
                eng.wait_ge(s, n)

        def groups(eng, body):
            body(0)
            with eng.Fori(1, NG - 1) as g:
                body(g)
            body(NG - 1)

        def pairs(eng, body):
            body(0)
            with eng.Fori(1, FT // 2 - 1) as j:
                body(j)
            body(FT // 2 - 1)

        def hidden_parts(j):
            return [(r, b) for b in range(NB) for r in range(2)] if isinstance(j, int) and j == 0 else [
                (r, b) for r in range(2) for b in range(NB)]

        def part_before(j, n):
            return hidden_parts(j)[n - 1] if n > 0 else (-1, NB - 1)

        def following(b, c, u, more):
            return (b, c + 1, u) if c < NC - 1 else (1 - b, 0, u + 1) if more else None

        def half(i):
            return slice(i % 2 * DM, (i % 2 + 1) * DM)

        def down_slot(buf, i):
            return buf[:, i // 2 % 2, i % 2 * DM:(i % 2 + 1) * DM]

        def in_last_unit(q):
            return isinstance(q, int) and q >= (NU - 1) * NC

        def ssq_bank(q):
            return bank[0] if in_last_unit(q) else B_OP

        def out_bank(q):
            return bank[1] if in_last_unit(q + 1) else B_OP

        def x2_bank(t):
            return bank[2] if t < NC else bank[6 + t % 2]

        def last_group(g):
            return isinstance(g, int) and g == NG - 1

        def steps(g):
            for b in range(NB):
                for c in range(NC):
                    more = not (b == NB - 1 and last_group(g))
                    yield b, c, g * NB + b, (g * NB + b) * NC + c, more, (g + b), 1 - b

        def wait_tile_read(eng, n, u):
            if TILES[n][0]:
                wait(eng, taps, u * NCONV + tiles_up_to(n + 1, True))
            else:
                wait(eng, xc_done, u * NTILE + n + 1)

        def cumb_loads(u, c):
            return u * (NC // 2) + c // 2 + 1

        def ecum_loads(u, c):
            return u + 1 if c == 2 else u * 2 + (c + 1) // 2

        def wait_y(eng, u, q, c):
            if c == 0:
                eng.wait_ge(yl_done, q + 1)
            else:
                eng.wait_ge(y_done, u * (NC - 1) + c)

        def scaled(buf):
            return buf.rearrange("p (m w) -> p m w", m=2)[:, :, 0:SW]

        def levels(buf):
            return buf.rearrange("p (m w) -> p m w", m=2)[:, :, SW:DM]

        cumf = cumb[:].rearrange("p s h i -> p (s h i)")
        dt_raw, dt_abs = cumf[:, 2 * L:3 * L], cumf[:, 3 * L:4 * L]
        dt_e1 = ecum[:, 0, :, :].rearrange("p k i -> p (k i)")
        dt_ln = xc[:, 1, 0, :]
        wdt_raw = xc[:, 1, 1:3, :].rearrange("p k i -> p (k i)")[:, 0:KT * 3 * NH].rearrange("p (k i) -> p k i", k=KT)
        wdt_hi, wdt_lo = wo_hi[:, :, 0:3 * NH], wo_lo[:, :, 0:3 * NH]
        dt_h, a_h, cum_h, ecum_h = dt_e1, dt_abs, dt_raw, dt_ln
        first_raw = ([w_raw[:, n, :] for n in range(2)] + [gate[:, 1, k, :] for k in range(CT)]
                     + [xc[:, 1, k, :] for k in range(3, NCONV)] + [ybuf[:].rearrange("p k i -> p (k i)")])
        a_tok, cum_tok = (v[:].rearrange("p h d -> p (h d)") for v in (xdt, xw))
        diff_tok, w_tok = ysq[:], zbuf[:].rearrange("p k i -> p (k i)")

        block = ctx.enter_context(nc.Block())

        @block.sync
        def _(sp):
            for t in range(4):
                sp.dma_start(oacc[:, t, :], x[t * P:(t + 1) * P, :]).then_inc(s_x[t], 16)
                if t == 1:
                    sp.dma_start(con[:], consts).then_inc(s_con, 16)
                    sp.dma_start(wdt_raw, wdt).then_inc(s_wdt, 16)
            sp.dma_start(hp[:, 0:2], hpar).then_inc(s_hp, 16)
            sp.dma_start(par[:], parg).then_inc(s_par, 16)

            def load_w(g, n):
                wait(sp, w_hi_done, g * NTILE + n - 1)
                wait(sp, w_lo_done, g * NTILE + n - 1)
                sp.dma_start(w_raw[:, n % 2, :], win[g, :, n, :]).then_inc(s_raw[n % 2], 16)

            def load_wo(g):
                wait(sp, wo_lo_done, g)
                sp.dma_start(wo_raw[:], wo[g]).then_inc(s_woraw, 16)

            def load_cum(g, b, c, u, q):
                wait(sp, yd_done, q - 1)
                sp.dma_start(cumb[:, c % 2, :, :], cum_rows[g, b, c].unsqueeze(0).broadcast_to([P, HG, Q])
                             ).then_inc(s_cumb[c % 2], 16)

            def load_ecum(g, b, c, u):
                if c > 0:
                    wait(sp, y_done, u * (NC - 1) + (0, 0, -1, 1)[c])
                    for par_ in range(2):
                        sp.dma_start(ecum[par_ * HD:(par_ + 1) * HD, c % 2, :, :],
                                     ecum_rows[g, b, c, par_].unsqueeze(0).broadcast_to([HD, CT, Q])
                                     ).then_inc(s_ecum[c % 2], 16)

            for n in range(NTILE):
                sp.dma_start(first_raw[n], win[0, :, n, :]).then_inc(s_raw[n] if n < 2 else s_first[n - 2], 16)
                if n < 4:
                    sp.dma_start(oacc[:, n + 4, :], x[(n + 4) * P:(n + 5) * P, :]).then_inc(s_x[n + 4], 16)
            load_wo(0)
            sp.wait_ge(pre_dve, 10)
            sp.dma_start(cum_dram, cum_h).then_inc(s_scr, 16)
            sp.wait_ge(s_scr, 16)
            load_cum(0, 0, 0, 0, 0)
            sp.wait_ge(pre_act, 7)
            load_cum(0, 0, 1, 0, 1)
            sp.wait_ge(pre_dve, 14)
            sp.dma_start(ecum_dram, ecum_h).then_inc(s_scr, 16)
            sp.wait_ge(s_scr, 32)
            load_ecum(0, 0, 1, 0)

            def body(g):
                for b, c, u, q, more, gn, bn in steps(g):
                    if c < NC - 2:
                        load_cum(g, b, c + 2, u, q + 2)
                        load_ecum(g, b, c + 2, u)
                    elif more:
                        load_cum(gn, bn, c + 2 - NC, u + 1, q + 2)
                        load_ecum(gn, bn, c + 2 - NC, u + 1)
                    st = b * NC + c
                    if not last_group(g):
                        for n in range(NTILE):
                            if SPLIT_AT[n] == st + 1:
                                load_w(g + 1, n)
                        if st == 2:
                            load_wo(g + 1)
                    elif st == 1:
                        sp.wait_ge(wo_lo_done, NG)
                        for t in range(4):
                            load_x(t)
                    elif st == NC:
                        sp.wait_ge(ip_done, NU * NTILE)
                        sp.dma_start(f_last[:], gu_last).then_inc(s_flast, 16)
                        load_f(0)

            def load_x(t):
                wait(sp, x2tp, t - 3)
                sp.dma_start(xin[:, t % 4, :], x[t * P:(t + 1) * P, :]).then_inc(s_xin[t % 4], 16)

            def load_f(i):
                wait(sp, f_levels, i)
                sp.dma_start(f_q[:], gu_q[i]).then_inc(s_fq, 16)
                wait(sp, f_lo_done, i)
                sp.dma_start(scaled(f_s[:]), gu_s[i].unsqueeze(0).broadcast_to([P, 2, SW])).then_inc(s_fs, 16)

            def load_down(i):
                wait(sp, f_lo_done, FT + max(i - 1, 0))
                w = half(i)
                if i == 0:
                    sp.wait_ge(f_levels, FT)
                sp.dma_start(f_q[:, w], dn_q[i]).then_inc(s_down[i % 2], 16)
                sp.dma_start(f_s[:, w], dn_s[i].unsqueeze(0).broadcast_to([P, DM])).then_inc(s_down[i % 2], 16)

            groups(sp, body)
            for t in range(4, NT):
                if t == 6:
                    load_f(1)
                load_x(t)
            with sp.Fori(2, FT) as i:
                load_f(i)
            for i in range(FT):
                load_down(i)
            for t in range(NT):
                sp.wait_ge(y_out[t % 2], t // 2 + 1)
                sp.dma_start(out[t * P:(t + 1) * P, :], oacc[:, t, :]).then_inc(s_out, 16)
            sp.wait_ge(s_out, 16 * NT)

        @block.tensor
        def _(pe):
            def split_product(o, l_hi, l_lo, r_hi, r_lo, first, final):
                nc.tensor.matmul(o, l_hi, r_hi, start=first, stop=False)
                nc.tensor.matmul(o, l_hi, r_lo, start=False, stop=False)
                return nc.tensor.matmul(o, l_lo, r_hi, start=False, stop=final)

            def project(g, b, n, u):
                k0 = u * NTILE + n
                wait(pe, w_hi_done, g * NTILE + n + 1)
                wait(pe, w_lo_done, g * NTILE + n + 1)
                m, back = last_user(n, BANKS)
                wait_tile_read(pe, m, u - back)
                s = slice(b * L, (b + 1) * L)
                for k in range(KT):
                    last = split_product(bank[BANKS[n]][:], w_hi[:, n, k, :], w_lo[:, n, k, :],
                                         xT_hi[:, k, s], xT_lo[:, k, s], k == 0, k == KT - 1)
                last.then_inc(ip_done, 1)

            def transpose_x(t):
                pe.wait_ge(normed, t + 1)
                wait(pe, xt_lo_done, t - 3)
                for k in range(KT):
                    last = nc.tensor.transpose(bank[4 + t % 4][:, k * P:(k + 1) * P], oacc[:, t, k * P:(k + 1) * P], ident)
                last.then_inc(xtp, 1)

            def dt_product(b):
                pe.wait_ge(xt_lo_done, (b + 1) * NC)
                s = slice(b * L, (b + 1) * L)
                for k in range(KT):
                    w = slice((1 - b) * NH, (3 - b) * NH)
                    last = split_product(bank[3][:], wdt_hi[:, k, w], wdt_lo[:, k, w], xT_hi[:, k, s], xT_lo[:, k, s],
                                         b == 0 and k == 0, b == NB - 1 and k == KT - 1)
                last.then_inc(dt_mm, 1)

            pe.wait_ge(s_con, 16)
            for t in range(NC + 2):
                transpose_x(t)
            pe.wait_ge(wdt_split, 2)
            dt_product(0)
            transpose_x(NC + 2)
            transpose_x(NC + 3)
            project(0, 0, 0, 0)
            dt_product(1)
            for n in range(1, 4):
                project(0, 0, n, 0)

            def transpose_chunks(o, src):
                for c in range(NC):
                    last = nc.tensor.transpose(o[:, c * P:(c + 1) * P], src[:, c * P:(c + 1) * P], ident)
                last.then_inc(pre_pe, 1)

            pe.wait_ge(pre_dve, 6)
            transpose_chunks(bank[6], a_h)
            pe.wait_ge(pre_dve, 7)
            nc.tensor.matmul(bank[7][:], tri, a_tok, start=True, stop=True).then_inc(pre_pe, 1)
            nc.tensor.matmul(bank[4][:], ones, a_tok, start=True, stop=True).then_inc(pre_pe, 1)
            pe.wait_ge(pre_dve, 8)
            transpose_chunks(bank[5], cum_tok)
            transpose_chunks(bank[3], dt_h)
            for n in range(4, NTILE - 1):
                project(0, 0, n, 0)

            def sum_squares(q, changes):
                pe.wait_ge(ysum, q + 1)
                if in_last_unit(q):
                    pe.wait_ge(ms_done, q)
                else:
                    wait(pe, oacc_done, q)
                    pe.wait_ge(h_done, changes)
                nc.tensor.matmul(ssq_bank(q)[:, 0:1], ysq[:, 0:Q], ones[:, 0:1], start=True, stop=True).then_inc(ssq_done, 1)

            def out_project(g, q, changes):
                pe.wait_ge(z_hi_done, q + 1)
                pe.wait_ge(z_lo_done, q + 1)
                pe.wait_ge(wo_hi_done, g + 1)
                pe.wait_ge(wo_lo_done, g + 1)
                if in_last_unit(q + 1):
                    pe.wait_ge(xc_done, NU * NTILE)
                    pe.wait_ge(oacc_done, q)
                else:
                    pe.wait_ge(h_done, changes)
                for k in range(CT):
                    last = split_product(out_bank(q)[:], z_hi[:, k, :], z_lo[:, k, :], wo_hi[:, k, :], wo_lo[:, k, :],
                                         k == 0, k == CT - 1)
                last.then_inc(op_done, 1)

            def by_token(b, c, u, q):
                s = slice(c * Q, (c + 1) * Q)
                pe.wait_ge(xc_done, u * NTILE + ALL_CONV)
                wait(pe, sm_done, q)
                wait(pe, bt_done, q)
                nc.tensor.matmul(B_S[:, 0:Q], xc[:, b, 0, s], xc[:, b, 1, s], start=True, stop=True)
                nc.tensor.transpose(B_S[:, Q:2 * Q], xc[:, b, 0, s], ident).then_inc(st_done, 1)
                wait(pe, xdt_done, q)
                for k in range(CT):
                    last = nc.tensor.transpose(B_XT[:, k * P:(k + 1) * P], xc[:, b, 2 + k, s], ident)
                last.then_inc(xt_done, 1)

            by_token(0, 0, 0, 0)
            project(0, 0, NTILE - 1, 0)

            def body(g):
                for b, c, u, q, more, gn, bn in steps(g):
                    first = isinstance(q, int) and q == 0
                    if not first:
                        sum_squares(q - 1, u * (NC - 1) + c)
                    pe.wait_ge(m_done, q + 1)
                    pe.wait_ge(xdt_done, q + 1)
                    wait(pe, yl_done, q)
                    for h in range(HG):
                        last = nc.tensor.matmul(B_YD[(h % 2) * HD:(h % 2 + 1) * HD, (h // 2) * Q:(h // 2 + 1) * Q],
                                                xdt[:, h, :], cumb[:, c % 2, h, :], start=True, stop=True)
                    last.then_inc(yd_done, 1)
                    nd = u * (NC - 1) + c
                    if c > 0:
                        pe.wait_ge(h_done, nd)
                        wait(pe, t1_done, nd - 1)
                        for k in range(CT):
                            last = nc.tensor.matmul(B_YO[:, k * Q:(k + 1) * Q],
                                                    hst[:, 2 * k:2 * k + 2, :].rearrange("p h d -> p (h d)"),
                                                    xc[:, b, 1, c * Q:(c + 1) * Q], start=True, stop=True)
                        last.then_inc(yo_done, 1)
                    if c < NC - 1:
                        pe.wait_ge(xw_done, nd + 1)
                        pe.wait_ge(bt_done, q + 1)
                        if not (in_last_unit(q) and c > 0):
                            wait(pe, ms_done, q)
                        nc.tensor.matmul(B_OP[:], btok[:], xw[:].rearrange("p h d -> p (h d)"),
                                         start=True, stop=True).then_inc(dh_done, 1)
                    if nxt := following(b, c, u, more):
                        by_token(*nxt, q + 1)
                    for n in SLOTS[c][0] if more else []:
                        project(gn, bn, n, u + 1)
                    if last_group(g):
                        for t in tiles_in_part(3, [b * NC + c - 1]):
                            transpose_x2(t)
                    if not first:
                        if c == NC - 1 and more:
                            pe.wait_ge(ms_done, q)
                        out_project(g if b or c else g - 1, q - 1, u * (NC - 1) + min(c + 1, NC - 1))
                    for n in SLOTS[c][1] if more else []:
                        project(gn, bn, n, u + 1)

            def transpose_x2(t):
                pe.wait_ge(x2n_done, t + 1)
                pe.wait_ge(xc_done, NU * NTILE)
                wait(pe, xt_lo_done, NT + t - (1 if t > NC else 0))
                for k in range(KT):
                    last = nc.tensor.transpose(x2_bank(t)[:, k * P:(k + 1) * P], xin[:, t % 4, k * P:(k + 1) * P],
                                               ident)
                last.then_inc(x2tp, 1)

            groups(pe, body)
            sum_squares(NU * NC - 1, NU * (NC - 1))
            transpose_x2(NC)
            out_project(NG - 1, NU * NC - 1, NU * (NC - 1))
            transpose_x2(NC + 1)

            pe.wait_ge(xt_lo_done, NT + NC)
            pe.wait_ge(ms_done, NU * NC)

            def pair(j):
                for n, (r, b) in enumerate(hidden_parts(j)):
                    pe.wait_ge(f_hi_done, j * 2 + r + 1)
                    pe.wait_ge(f_lo_done, j * 2 + r + 1)
                    pe.wait_ge(f_levels, j * 2 + r + 1)
                    first = isinstance(j, int) and j == 0
                    if first and n == 2:
                        pe.wait_ge(xt_lo_done, 2 * NT)
                    k0 = j * 2 * NB + n
                    wait(pe, u_sum, k0 - 1)
                    s = slice(b * L, (b + 1) * L)
                    banks = bank[n % 2 * 4:n % 2 * 4 + 4]
                    for m in range(2):
                        if first and (n, m) == (0, 1):
                            pe.wait_ge(oacc_done, NU * NC)
                        if first and (n, m) in ((1, 0), (1, 1)):
                            transpose_x2(NC + 2 + m)
                        for k in range(KS):
                            w = slice(m * DM + k * P, m * DM + (k + 1) * P)
                            split_product(banks[m][:], f_hi[:, r, w], f_lo[:, r, w], xT_hi[:, k, s], xT_lo[:, k, s],
                                          k == 0, k == KS - 1)
                    for m, s_mm in ((0, g_mm), (1, u_mm)):
                        if first and n == 1:
                            pe.wait_ge(xt_lo_done, 2 * NT - 1 + m)
                        w = slice(m * DM + SW, (m + 1) * DM)
                        nc.tensor.matmul(banks[2 + m][:], f_hi[:, r, w], xT_hi[:, KS, s], start=True, stop=False)
                        nc.tensor.matmul(banks[2 + m][:], f_hi[:, r, w], xT_lo[:, KS, s], start=False, stop=True
                                         ).then_inc(s_mm, 1)

            pairs(pe, pair)
            def down(i, t):
                tok = slice(t * P, (t + 1) * P)
                return split_product(bank[t][:], h_hi[:, i, tok], h_lo[:, i, tok], down_slot(f_hi, i),
                                     down_slot(f_lo, i), i == 0, i == FT - 1)

            def wait_down(i):
                pe.wait_ge(h_hi_done, max(i + 1, 2) * NB)
                pe.wait_ge(h_lo_done, max(i + 1, 2) * NB)
                pe.wait_ge(f_hi_done, FT + i + 1)
                pe.wait_ge(f_lo_done, FT + i + 1)

            for i in range(FT - 2):
                wait_down(i)
                for t in range(NT):
                    if i == 0 and t % 4 == 0:
                        pe.wait_ge(u_sum, FT * NB - 1 + t // 4)
                    last = down(i, t)
                last.then_inc(dn_mm, 1)
            wait_down(FT - 2)
            wait_down(FT - 1)
            for t in range(NT):
                down(FT - 2, t)
                down(FT - 1, t).then_inc(dn_mm, 1)

        @block.scalar
        def _(act):
            act.wait_ge(s_wdt, 16)
            nc.scalar.activation(wdt_hi, wdt_raw, ACT.Copy).then_inc(wdt_split, 1)

            def split_w(g, n):
                if isinstance(g, int) and g == 0:
                    act.wait_ge(s_raw[n] if n < 2 else s_first[n - 2], 16)
                    src = first_raw[n]
                else:
                    act.wait_ge(s_raw[n % 2], ((g - 1) * (NTILE // 2) + n // 2 + 2) * 16)
                    src = w_raw[:, n % 2, :]
                wait(act, ip_done, ((g - 1) * NB + 1) * NTILE + n + 1)
                nc.scalar.activation(w_hi[:, n, :, :].rearrange("p k c -> p (k c)"), src, ACT.Copy).then_inc(w_hi_done, 1)

            act.wait_ge(s_hp, 16)
            nc.scalar.activation(hp[:, 2:3], hp[:, 1:2], ACT.Exp).then_inc(pre_act, 1)
            for t in range(NT):
                act.wait_ge(xtp, t + 1)
                nc.scalar.activation(xT_hi[:, :, t * P:(t + 1) * P], bank[4 + t % 4][:].rearrange("p (k i) -> p k i", k=KT),
                                     ACT.Copy).then_inc(xt_hi_done, 1)
                if t > 2:
                    split_w(0, t - 3)

            def first_pass(n, b, u):
                conv, k = TILES[n]
                act.wait_ge(ip_done, u * NTILE + n + 1)
                if conv:
                    act.wait_ge(cpar_done, u + 1)
                    m, back = last_user(n, ACC_SLOTS)
                    wait(act, xc_done, (u - back) * NTILE + m + 1)
                    p0 = k * (TAPS + 1)
                    nc.scalar.activation(acc[:, k % 2, :], bank[BANKS[n]][:], ACT.Identity,
                                         scale=cpar[:, b, p0 + TAPS - 1:p0 + TAPS], bias=cpar[:, b, p0 + TAPS:p0 + TAPS + 1]
                                         ).then_inc(tap0, 1)
                else:
                    wait(act, xc_done, u * NTILE + n)
                    nc.scalar.activation(th[:], bank[BANKS[n]][:], ACT.Tanh, scale=0.5).then_inc(th_done, 1)

            def second_pass(n, u):
                if TILES[n][0]:
                    act.wait_ge(taps, u * NCONV + tiles_up_to(n + 1, True))
                    wait(act, xc_done, u * NTILE + n)
                    nc.scalar.activation(th[:], acc[:, TILES[n][1] % 2, :], ACT.Tanh, scale=0.5).then_inc(th_done, 1)

            def scale_wo(g, tiles=range(CT)):
                act.wait_ge(cpar_done, g * NB + 1)
                act.wait_ge(s_woraw, (g + 1) * 16)
                for k in tiles:
                    nc.scalar.activation(wo_raw[:, k, :], wo_raw[:, k, :], ACT.Copy,
                                         scale=cpar[:, 0, PNW + k:PNW + k + 1]).then_inc(wo_scaled, 1)

            def decays(b, c, u, q):
                differences(b, c, u)
                exponentials(c, q)

            def differences(b, c, u):
                act.wait_ge(s_cumb[c % 2], cumb_loads(u, c) * 16)
                act.wait_ge(cur_done, u + 1)
                for h in range(HG):
                    last = nc.scalar.activation(cumb[:, c % 2, h, :], cumb[:, c % 2, h, :], ACT.Relu, scale=-1.0,
                                                bias=cur[:, b, CUM, c, h:h + 1])
                last.then_inc(diff_done, 1)

            def exponentials(c, q):
                act.wait_ge(diff_done, q + 1)
                nc.scalar.activation(cumb[:, c % 2, :, :], cumb[:, c % 2, :, :], ACT.Exp, scale=-1.0).then_inc(e_done, 1)

            first_pass(0, 0, 0)
            act.wait_ge(pre_dve, 2)
            nc.scalar.activation(dt_abs, dt_abs, ACT.Exp, scale=-1.0).then_inc(pre_act, 1)
            act.wait_ge(pre_dve, 3)
            nc.scalar.activation(dt_ln, dt_e1, ACT.Ln).then_inc(pre_act, 1)
            first_pass(1, 0, 0)
            second_pass(0, 0)
            for n in range(NT - 3, NTILE):
                split_w(0, n)
            scale_wo(0, range(2))

            def slot(tiles, b, u):
                for n in tiles:
                    if n > 0:
                        second_pass(n - 1, u)
                    first_pass(n, b, u)

            def slot_ahead(tiles):
                for n in tiles:
                    if TILES[n][0]:
                        first_pass(n, 0, 0)
                        second_pass(n - 1, 0)
                    else:
                        slot([n], 0, 0)

            slot_ahead([2])
            act.wait_ge(pre_dve, 9)
            nc.scalar.activation(w_tok, diff_tok, ACT.Exp).then_inc(pre_act, 1)
            for b in range(NB):
                o = tab[:, b::NB, DEC, :, :].rearrange("p g c h -> p c g h")
                i_ = bank[4][:].rearrange("p (c b g h) -> p b c g h", c=NC, b=NB, h=HG)[:, b]
                nc.scalar.activation(o, i_, ACT.Exp).then_inc(pre_act, 1)
            act.wait_ge(pre_dve, 10)
            nc.scalar.activation(ecum_h, cum_h, ACT.Exp).then_inc(pre_act, 1)
            scale_wo(0, range(2, CT))
            slot_ahead([3, 4, 5])
            differences(0, 0, 0)
            slot_ahead([6])
            exponentials(0, 0)
            slot_ahead([7])

            slot(range(ALL_CONV + 1, NTILE), 0, 0)

            def body(g):
                for b, c, u, q, more, gn, bn in steps(g):
                    if nxt := following(b, c, u, more):
                        decays(*nxt, q + 1)
                    wait_y(act, u, q, c)
                    wait(act, ssq_done, q)
                    nc.scalar.activation(ysq[:], ybuf[:].rearrange("p k i -> p (k i)"), ACT.Square).then_inc(sq_done, 1)
                    slot(SLOTS[c][0] if more else [], bn, u + 1)
                    if not last_group(g):
                        for n in range(NTILE):
                            if SPLIT_AT[n] == b * NC + c:
                                split_w(g + 1, n)
                        if b == 1 and c == 2:
                            scale_wo(g + 1)
                    if last_group(g):
                        for t in tiles_in_part(3, [b * NC + c - 1]):
                            copy_x2(t)
                    act.wait_ge(z_done, q + 1)
                    wait(act, op_done, q)
                    nc.scalar.activation(z_hi[:], zbuf[:], ACT.Copy).then_inc(z_hi_done, 1)
                    slot(SLOTS[c][1] if more else [], bn, u + 1)
                    if b == 0 and c == 0:
                        wait(act, op_done, q)
                        act.wait_ge(wo_scaled, (g + 1) * CT)
                        nc.scalar.activation(wo_hi[:], wo_raw[:], ACT.Copy).then_inc(wo_hi_done, 1)
                    if not more and c == 2:
                        split_f(0, 0)

            def copy_x2(t):
                act.wait_ge(x2tp, t + 1)
                nc.scalar.activation(xT_hi[:, :, t * P:(t + 1) * P], x2_bank(t)[:].rearrange("p (k i) -> p k i", k=KT),
                                     ACT.Copy).then_inc(xt_hi_done, 1)

            def split_f(i, slot_):
                act.wait_ge(f_w, i + 1)
                wait(act, u_mm, (i - 1) * NB + (1 if isinstance(i, int) and i == 2 else 0))
                nc.scalar.activation(scaled(f_hi[:, slot_, :]), scaled(f_s[:]), ACT.Copy).then_inc(f_hi_done, 1)
                nc.scalar.activation(levels(f_hi[:, slot_, :]), levels(f_q[:]), ACT.Copy).then_inc(f_levels, 1)

            def split_down(i):
                act.wait_ge(f_w, FT + i + 1)
                if i > 3:
                    act.wait_ge(dn_mm, i - 3)
                else:
                    act.wait_ge(u_mm, (FT + i // 2 - 1) * NB)
                nc.scalar.activation(down_slot(f_hi, i), f_s[:, half(i)], ACT.Copy).then_inc(f_hi_done, 1)

            groups(act, body)
            split_f(1, 1)
            for t in range(NC, NT - 1):
                copy_x2(t)

            def scale_last(j, n, r):
                k = j * 2 * NB + n
                banks = bank[n % 2 * 4:n % 2 * 4 + 4]
                act.wait_ge(f_pair_done, j + 1)
                act.wait_ge(g_mm, k + 1)
                wait(act, h_hi_done, k - 1)
                wait(act, h_lo_done, k - 1)
                nc.scalar.activation(f_g[:, n % 2, :], banks[2][:], ACT.Copy, scale=f_pair[:, r, 0:1]
                                     ).then_inc(g_last, 1)
                act.wait_ge(u_mm, k + 1)
                wait(act, hbuf_done, k - 1)
                nc.scalar.activation(f_u[:, n % 2, :], banks[3][:], ACT.Copy, scale=f_pair[:, r, 1:2]
                                     ).then_inc(u_last, 1)

            scale_last(0, 0, 0)
            copy_x2(NT - 1)

            def pair(j):
                for n, (r, b) in enumerate(hidden_parts(j)):
                    k = j * 2 * NB + n
                    first = isinstance(j, int) and j == 0
                    if not (first and n == 0):
                        scale_last(j, n, r)
                    act.wait_ge(g_sum, k + 1)
                    wait(act, g_silu, k)
                    nc.scalar.activation(f_th[:], f_g[:, n % 2, :], ACT.Tanh, scale=0.5).then_inc(g_th, 1)
                    if isinstance(j, int) and j == FT // 2 - 1 and n >= 2:
                        split_down(n - 2)
                    elif n == 2 or (n == 0 and not first):
                        split_f(j * 2 + n // 2 + 1, 1 - n // 2)
                    if not (first and n == 0):
                        pr, pb = part_before(j, n)
                        high_half(k - 1, j * 2 + pr, pb, (n - 1) % 2)

            def high_half(k, i, b, slot_):
                act.wait_ge(hbuf_done, k + 1)
                nc.scalar.activation(h_hi[:, i, b * L:(b + 1) * L], f_g[:, slot_, :], ACT.Copy).then_inc(h_hi_done, 1)

            pairs(act, pair)
            high_half(FT * NB - 1, FT - 1, NB - 1, 1)
            for i in range(2, FT):
                split_down(i)
            for t in range(NT):
                act.wait_ge(shift_done, NT + t + 1)
                wait(act, y_out[t % 2], t // 2)
                nc.scalar.activation(f_g[:, t % 2, :], bank[t][:], ACT.Identity, scale=ln_rs[:, 3 * NT + t:3 * NT + t + 1],
                                     bias=ln_sh[:, NT + t:NT + t + 1]).then_inc(fin_n, 1)

        @block.gpsimd
        def _(pool):
            nc.gpsimd.memset(mhalf[:], -0.5).then_inc(const_set, 1)
            pool.wait_ge(const_set, 1)

            def power(k):
                pool.wait_ge(var_eps, k + 1)
                nc.gpsimd.tensor_tensor(ln_rs[:, k:k + 1], ln_ve[:, k:k + 1], mhalf[:], ALU.pow).then_inc(rstd, 1)

            def split_w(g, n):
                pool.wait_ge(w_hi_done, g * NTILE + n + 1)
                src = first_raw[n] if isinstance(g, int) and g == 0 else w_raw[:, n % 2, :]
                nc.gpsimd.tensor_tensor(w_lo[:, n, :, :].rearrange("p k c -> p (k c)"), src,
                                        w_hi[:, n, :, :].rearrange("p k c -> p (k c)").bitcast(F32), ALU.subtract
                                        ).then_inc(w_lo_done, 1)

            for t in range(NT):
                power(t)
                if t == 1:
                    pool.wait_ge(wdt_split, 1)
                    nc.gpsimd.tensor_tensor(wdt_lo, wdt_raw, wdt_hi.bitcast(F32), ALU.subtract).then_inc(wdt_split, 1)
            for n in range(NTILE):
                split_w(0, n)

            def over(table, b, c):
                return cur[:, b, table, c, :].unsqueeze(2).broadcast_to([P, HG, HD])

            def skip_term(b, c, u, q):
                pool.wait_ge(xc_done, u * NTILE + ALL_CONV)
                pool.wait_ge(cpar_done, u + 1)
                wait(pool, sq_done, q)
                wait(pool, z_done, q)
                nc.gpsimd.tensor_tensor(ybuf[:], xc[:, b, 2:2 + CT, c * Q:(c + 1) * Q],
                                        cpar[:, b, PD:PD + CT].unsqueeze(2).broadcast_to([P, CT, Q]), ALU.mult
                                        ).then_inc(dx_done, 1)

            def state_terms(b, c, u, q):
                nd = u * (NC - 1) + c
                pool.wait_ge(cur_done, u + 1)
                if c < NC - 1:
                    pool.wait_ge(xdt_done, q + 1)
                    wait(pool, dh_done, nd)
                    nc.gpsimd.tensor_tensor(xw[:], xdt[:], over(WE, b, c), ALU.mult).then_inc(xw_done, 1)
                    if c > 0:
                        pool.wait_ge(h_done, nd)
                        nc.gpsimd.tensor_tensor(hdec[:], hst[:], over(DEC, b, c), ALU.mult).then_inc(hd_done, 1)

            def root(q):
                pool.wait_ge(ms_done, q + 1)
                wait(pool, oacc_done, q)
                nc.gpsimd.tensor_tensor(rms[:, 1:2], rms[:, 0:1], mhalf[:], ALU.pow).then_inc(r_done, 1)

            state_terms(0, 0, 0, 0)
            pool.wait_ge(w_lo_done, NTILE)
            skip_term(0, 0, 0, 0)

            def body(g):
                for b, c, u, q, more, gn, bn in steps(g):
                    if not (isinstance(q, int) and q == 0):
                        root(q - 1)
                    wait_y(pool, u, q, c)
                    pool.wait_ge(xc_done, (u + 1) * NTILE)
                    wait(pool, z_hi_done, q)
                    wait(pool, z_lo_done, q)
                    nc.gpsimd.tensor_tensor(zbuf[:], ybuf[:], gate[:, b, :, c * Q:(c + 1) * Q], ALU.mult
                                            ).then_inc(z_done, 1)
                    nxt = following(b, c, u, more)
                    pool.wait_ge(sq_done, q + 1)
                    nc.gpsimd.tensor_tensor(ysq[:, 0:2 * Q], ysq[:, 0:2 * Q], ysq[:, 2 * Q:4 * Q], ALU.add
                                            ).then_inc(ysum_half, 1)
                    pool.wait_ge(ysum_half, q + 1)
                    nc.gpsimd.tensor_tensor(ysq[:, 0:Q], ysq[:, 0:Q], ysq[:, Q:2 * Q], ALU.add).then_inc(ysum, 1)
                    if nxt:
                        state_terms(*nxt, q + 1)
                        skip_term(*nxt, q + 1)
                    pool.wait_ge(z_hi_done, q + 1)
                    wait(pool, op_done, q)
                    nc.gpsimd.tensor_tensor(z_lo[:], zbuf[:], z_hi[:].bitcast(F32), ALU.subtract).then_inc(z_lo_done, 1)
                    if b == 0 and c == 0:
                        pool.wait_ge(wo_hi_done, g + 1)
                        nc.gpsimd.tensor_tensor(wo_lo[:], wo_raw[:], wo_hi[:].bitcast(F32), ALU.subtract
                                                ).then_inc(wo_lo_done, 1)
                    if not last_group(g):
                        for n in range(NTILE):
                            if SPLIT_AT[n] == b * NC + c:
                                split_w(g + 1, n)
                    if not more and c == 2:
                        split_f(0, 0)
                    if last_group(g):
                        powers_x2(b * NC + c - 1)

            def powers_x2(r):
                for p in (1, 0):
                    for t in tiles_in_part(p, [r]):
                        power(NT + 2 * t + p)

            def split_f(i, slot_):
                pool.wait_ge(f_hi_done, i + 1)
                nc.gpsimd.tensor_tensor(scaled(f_lo[:, slot_, :]), scaled(f_s[:]), scaled(f_hi[:, slot_, :]).bitcast(F32),
                                        ALU.subtract).then_inc(f_lo_done, 1)

            def split_down(i):
                pool.wait_ge(f_hi_done, FT + i + 1)
                nc.gpsimd.tensor_tensor(down_slot(f_lo, i), f_s[:, half(i)], down_slot(f_hi, i).bitcast(F32), ALU.subtract
                                        ).then_inc(f_lo_done, 1)

            def add_residual(t):
                pool.wait_ge(fin_n, t + 1)
                pool.wait_ge(x2_done, NT + t + 1)
                nc.gpsimd.tensor_tensor(oacc[:, t, :], oacc[:, t, :], f_g[:, 0, :], ALU.add).then_inc(y_out[0], 1)

            groups(pool, body)
            root(NU * NC - 1)
            split_f(1, 1)
            for r in range(AFTER, NT + 1):
                powers_x2(r)
            with pool.Fori(1, FT // 2) as j:
                for r in range(2):
                    split_f(j * 2 + r, r)
            for i in range(FT):
                split_down(i)
            for t in range(NT):
                power(3 * NT + t)
                if t % 2 == 1:
                    add_residual(t - 1)

        @block.vector
        def _(dve):
            def moments(k, *srcs):
                for n, src in enumerate(srcs):
                    nc.vector.bn_stats(ln_st[:, k + n, :], src).then_inc(stats, 1)
                for n in range(len(srcs)):
                    dve.wait_ge(stats, k + n + 1)
                    nc.vector.bn_aggr(ln_mv[:, k + n, :], ln_st[:, k + n, :]).then_inc(aggr, 1)
                for n in range(len(srcs)):
                    dve.wait_ge(aggr, k + n + 1)
                    nc.vector.tensor_scalar(ln_ve[:, k + n:k + n + 1], ln_mv[:, k + n, 1:2], EPS, None, ALU.add
                                            ).then_inc(var_eps, 1)

            def normalize(k, dst, src):
                dve.wait_ge(rstd, k + 1)
                return nc.vector.tensor_scalar(dst, src, ln_mv[:, k, 0:1], ln_rs[:, k:k + 1], ALU.subtract, ALU.mult)

            for t in range(NT + 3):
                if t < NT:
                    dve.wait_ge(s_x[t], 16)
                    moments(t, oacc[:, t, :])
                if 0 < t <= NT:
                    normalize(t - 1, oacc[:, t - 1, :], oacc[:, t - 1, :]).then_inc(normed, 1)
                if t > 2:
                    dve.wait_ge(xt_hi_done, t - 2)
                    sl = slice((t - 3) * P, (t - 2) * P)
                    nc.vector.tensor_tensor(xT_lo[:, :, sl], bank[4 + (t - 3) % 4][:].rearrange("p (k i) -> p k i", k=KT),
                                            xT_hi[:, :, sl].bitcast(F32), ALU.subtract).then_inc(xt_lo_done, 1)

            def copy_params(g, b, u):
                if not (isinstance(u, int) and u < 2):
                    q0 = (u - 1) * NC
                    dve.wait_ge(dx_done, q0)
                    dve.wait_ge(e_done, q0)
                    dve.wait_ge(xw_done, (u - 1) * (NC - 1))
                    dve.wait_ge(hd_done, (u - 1) * (NC - 2))
                    if b == 0:
                        dve.wait_ge(wo_scaled, g * CT)
                if not (isinstance(u, int) and u == 0):
                    nc.vector.tensor_copy(cpar[:, b, :], par[:, g, :]).then_inc(cpar_done, 1)
                nc.vector.tensor_copy(cur[:, b, :, :, :].rearrange("p k c h -> p (k c h)"),
                                      tab[:, u, :, :, :].rearrange("p k c h -> p (k c h)")).then_inc(cur_done, 1)

            def first_use(n, b, u):
                conv, k = TILES[n]
                if conv:
                    done = u * NCONV + tiles_up_to(n, True)
                    dve.wait_ge(tap0, done + 1)
                    dve.wait_ge(cpar_done, u + 1)
                    p0 = k * (TAPS + 1)
                    for d in range(1, TAPS):
                        last = nc.vector.scalar_tensor_tensor(
                            out=acc[:, k % 2, d:L], in0=bank[BANKS[n]][:, 0:L - d],
                            scalar=cpar[:, b, p0 + TAPS - 1 - d:p0 + TAPS - d], in1=acc[:, k % 2, d:L],
                            op0=ALU.mult, op1=ALU.add)
                        if d < TAPS - 1:
                            last.then_inc(tap_step, 1)
                            dve.wait_ge(tap_step, done * (TAPS - 2) + d)
                    last.then_inc(taps, 1)
                else:
                    dve.wait_ge(th_done, u * NTILE + n + 1)
                    wait(dve, z_done, (u - 1) * NC)
                    nc.vector.scalar_tensor_tensor(out=gate[:, b, k, :], in0=th[:], scalar=1.0,
                                                   in1=bank[BANKS[n]][:], op0=ALU.add, op1=ALU.mult).then_inc(xc_done, 1)

            def second_use(n, b, u):
                conv, k = TILES[n]
                if conv:
                    dve.wait_ge(th_done, u * NTILE + n + 1)
                    wait(dve, dx_done, (u - 1) * NC)
                    wait(dve, yd_done, (u - 1) * NC)
                    wait(dve, yo_done, (u - 1) * (NC - 1))
                    nc.vector.scalar_tensor_tensor(out=xc[:, b, k, :], in0=th[:], scalar=1.0, in1=acc[:, k % 2, :],
                                                   op0=ALU.add, op1=ALU.mult).then_inc(xc_done, 1)

            def slot(tiles, b, u, before_last=None):
                for n in tiles:
                    if n > 0:
                        second_use(n - 1, b, u)
                    if before_last and n == tiles[-1]:
                        before_last()
                    first_use(n, b, u)

            def slot_ahead(tiles):
                for n in tiles:
                    if TILES[n][0]:
                        first_use(n, 0, 0)
                        second_use(n - 1, 0, 0)
                    else:
                        slot([n], 0, 0)

            dve.wait_ge(s_par, 16)
            nc.vector.tensor_scalar(par[:, :, PD:PD + 2 * CT], par[:, :, PD:PD + 2 * CT], 0.5, None, ALU.mult
                                    ).then_inc(pre_dve, 1)
            dve.wait_ge(pre_dve, 1)
            nc.vector.tensor_copy(cpar[:, 0, :], par[:, 0, :]).then_inc(cpar_done, 1)
            first_use(0, 0, 0)
            dve.wait_ge(s_hp, 16)
            dve.wait_ge(dt_mm, NB)
            nc.vector.tensor_scalar(dt_raw, bank[3][:], hp[:, 0:1], None, ALU.add).then_inc(pre_step, 1)
            dve.wait_ge(pre_step, 1)
            nc.vector.scalar_tensor_tensor(out=dt_abs, in0=dt_raw, scalar=-1.0, in1=dt_raw, op0=ALU.mult, op1=ALU.max
                                           ).then_inc(pre_dve, 1)
            dve.wait_ge(pre_act, 2)
            nc.vector.tensor_scalar(dt_e1, dt_abs, 1.0, None, ALU.add).then_inc(pre_dve, 1)
            dve.wait_ge(pre_dve, 3)
            nc.vector.scalar_tensor_tensor(out=dt_abs, in0=dt_e1, scalar=-1.0, in1=dt_abs, op0=ALU.add, op1=ALU.subtract
                                           ).then_inc(pre_step, 1)
            dve.wait_ge(pre_step, 2)
            dve.wait_ge(pre_act, 3)
            nc.vector.tensor_tensor(dt_ln, dt_ln, dt_abs, ALU.subtract).then_inc(pre_step, 1)
            nc.vector.tensor_scalar(hp[:, 3:4], hp[:, 2:3], -1.0, None, ALU.mult).then_inc(pre_dve, 1)
            dve.wait_ge(pre_step, 3)
            dve.wait_ge(pre_dve, 4)
            nc.vector.scalar_tensor_tensor(out=dt_h, in0=dt_raw, scalar=0.0, in1=dt_ln, op0=ALU.max, op1=ALU.add
                                           ).then_inc(pre_dve, 1)
            dve.wait_ge(pre_dve, 5)
            nc.vector.tensor_scalar(a_h, dt_h, hp[:, 3:4], None, ALU.mult).then_inc(pre_dve, 1)

            def by_unit(table, b):
                return tab[:, b::NB, table, :, :].rearrange("p g c h -> p c g h")

            def by_token(flat, b):
                return flat.rearrange("p (c b g h) -> p b c g h", c=NC, b=NB, h=HG)[:, b]

            second_use(0, 0, 0)
            dve.wait_ge(pre_pe, 1)
            nc.vector.tensor_copy(a_tok, bank[6][:]).then_inc(pre_dve, 1)
            first_use(1, 0, 0)
            dve.wait_ge(pre_pe, 2)
            nc.vector.tensor_copy(cum_tok, bank[7][:]).then_inc(pre_dve, 1)
            dve.wait_ge(pre_pe, 3)
            dve.wait_ge(pre_dve, 8)
            nc.vector.tensor_tensor(diff_tok, bank[4][:], cum_tok, ALU.subtract).then_inc(pre_dve, 1)
            dve.wait_ge(pre_pe, 4)
            nc.vector.tensor_copy(cum_h, bank[5][:]).then_inc(pre_dve, 1)
            slot_ahead([2])
            for b in range(NB):
                last = nc.vector.tensor_copy(by_unit(CUM, b), by_token(cum_tok, b))
            last.then_inc(pre_dve, 1)
            dve.wait_ge(pre_pe, 5)
            for b in range(NB):
                last = nc.vector.tensor_scalar(by_unit(DT, b), by_token(bank[3][:], b), 0.5, None, ALU.mult)
            last.then_inc(pre_dve, 1)
            dve.wait_ge(pre_act, 4)
            for b in range(NB):
                last = nc.vector.tensor_scalar(by_unit(WE, b), by_token(w_tok, b), 0.5, None, ALU.mult)
            last.then_inc(pre_dve, 1)
            dve.wait_ge(pre_act, 7)
            nc.vector.tensor_scalar(ecum_h, ecum_h, 0.5, None, ALU.mult).then_inc(pre_dve, 1)
            slot_ahead([3, 4])
            dve.wait_ge(pre_dve, 14)
            copy_params(0, 0, 0)
            nc.vector.memset(oacc[:, NT - 1, :], 0.0).then_inc(pre_step, 1)
            slot_ahead(range(5, ALL_CONV + 1))
            dve.wait_ge(pre_step, 4)

            def mean_square(q):
                dve.wait_ge(ssq_done, q + 1)
                wait(dve, r_done, q)
                nc.vector.tensor_scalar(rms[:, 0:1], ssq_bank(q)[:, 0:1], 1.0 / GW, EPS, ALU.mult, ALU.add
                                        ).then_inc(ms_done, 1)

            def gather_out(g, t, q):
                dve.wait_ge(op_done, q + 1)
                dve.wait_ge(r_done, q + 1)
                if isinstance(g, int) and g == 0:
                    nc.vector.tensor_scalar(oacc[:, t, :], out_bank(q)[:], rms[:, 1:2], None, ALU.mult).then_inc(oacc_done, 1)
                else:
                    nc.vector.scalar_tensor_tensor(out=oacc[:, t, :], in0=out_bank(q)[:], scalar=rms[:, 1:2], in1=oacc[:, t, :],
                                                   op0=ALU.mult, op1=ALU.add).then_inc(oacc_done, 1)

            def matrix(b, c, u, q):
                nd = u * (NC - 1) + c
                dve.wait_ge(st_done, q + 1)
                wait(dve, dh_done, nd)
                nc.vector.tensor_tensor(smask[:], B_S[:, 0:Q], mask4, ALU.mult).then_inc(sm_done, 1)
                nc.vector.tensor_copy(btok[:], B_S[:, Q:2 * Q]).then_inc(bt_done, 1)
                dve.wait_ge(xt_done, q + 1)
                wait(dve, yd_done, q)
                wait(dve, xw_done, nd)
                dve.wait_ge(cur_done, u + 1)
                nc.vector.tensor_tensor(xdt[:], B_XT[:].rearrange("p (h d) -> p h d", h=HG),
                                        cur[:, b, DT, c, :].unsqueeze(2).broadcast_to([P, HG, HD]), ALU.mult
                                        ).then_inc(xdt_done, 1)
                dve.wait_ge(e_done, q + 1)
                dve.wait_ge(sm_done, q + 1)
                nc.vector.tensor_tensor(cumb[:, c % 2, :, :], cumb[:, c % 2, :, :], smask[:].unsqueeze(1).broadcast_to([P, HG, Q]), ALU.mult
                                        ).then_inc(m_done, 1)

            matrix(0, 0, 0, 0)
            slot(range(ALL_CONV + 1, NTILE), 0, 0)

            def body(g):
                for b, c, u, q, more, gn, bn in steps(g):
                    first = isinstance(q, int) and q == 0
                    nd = u * (NC - 1) + c
                    dve.wait_ge(yd_done, q + 1)
                    dve.wait_ge(dx_done, q + 1)
                    nc.vector.tensor_tensor(ybuf[:], B_YD[:].rearrange("p (k i) -> p k i", k=CT), ybuf[:], ALU.add
                                            ).then_inc(yl_done, 1)
                    if c > 0:
                        dve.wait_ge(yo_done, nd)
                        dve.wait_ge(s_ecum[c % 2], ecum_loads(u, c) * 32)
                        nc.vector.tensor_tensor(ecum[:, c % 2, :, :], B_YO[:].rearrange("p (k i) -> p k i", k=CT),
                                                ecum[:, c % 2, :, :], ALU.mult).then_inc(t1_done, 1)
                        dve.wait_ge(yl_done, q + 1)
                        dve.wait_ge(t1_done, nd)
                        nc.vector.tensor_tensor(ybuf[:], ybuf[:], ecum[:, c % 2, :, :], ALU.add).then_inc(y_done, 1)
                    if c < NC - 1:
                        dve.wait_ge(dh_done, nd + 1)
                        hflat = hst[:].rearrange("p h d -> p (h d)")
                        if c == 0:
                            wait(dve, yo_done, u * (NC - 1))
                            nc.vector.tensor_copy(hflat, B_OP[:]).then_inc(h_done, 1)
                        else:
                            dve.wait_ge(hd_done, u * (NC - 2) + c)
                            nc.vector.tensor_tensor(hflat, B_OP[:], hdec[:].rearrange("p h d -> p (h d)"), ALU.add
                                                    ).then_inc(h_done, 1)
                    if nxt := following(b, c, u, more):
                        matrix(*nxt, q + 1)
                    if c == 0 and more:
                        copy_params(gn, bn, u + 1)
                    if first:
                        dve.wait_ge(s_scr, 32)
                    slot(SLOTS[c][0] if more else [], bn, u + 1)
                    if last_group(g):
                        for p in (3, 2):
                            for t in tiles_in_part(p, [b * NC + c - 1]):
                                x2_part(p, t)
                    if not first:
                        gather_out(g if b or c else g - 1, (b * NC + c - 1) % NT, q - 1)
                    if more:
                        slot(SLOTS[c][1], bn, u + 1, lambda: mean_square(q))
                    if last_group(g):
                        for t in tiles_in_part(1, [b * NC + c - 1]):
                            add_input(t)
                        if not more:
                            mean_square(q)
                        moments_x2(b * NC + c - 1)
                    if not more and c == 1:
                        dequant(0)

            def add_input(t):
                k = NT + 2 * t
                dve.wait_ge(rstd, k + 1)
                dve.wait_ge(s_xin[t % 4], (t // 4 + 1) * 16)
                nc.vector.scalar_tensor_tensor(out=oacc[:, t, :], in0=oacc[:, t, :], scalar=ln_rs[:, k:k + 1],
                                               in1=xin[:, t % 4, :], op0=ALU.mult, op1=ALU.add).then_inc(x2_done, 1)

            def moments_x2(r):
                if r < 0:
                    return
                if r < NT:
                    dve.wait_ge(oacc_done, NU * NC - NT + r + 1)
                if r > 0:
                    dve.wait_ge(x2_done, r)
                moments(NT + 2 * r - (r > 0), *(oacc[:, t, :] for p in (1, 0) for t in tiles_in_part(p, [r])))

            def x2_part(p, t):
                if p == 2:
                    normalize(NT + 2 * t + 1, xin[:, t % 4, :], oacc[:, t, :]).then_inc(x2n_done, 1)
                else:
                    dve.wait_ge(xt_hi_done, NT + t + 1)
                    sl = slice(t * P, (t + 1) * P)
                    nc.vector.tensor_tensor(xT_lo[:, :, sl], x2_bank(t)[:].rearrange("p (k i) -> p k i", k=KT),
                                            xT_hi[:, :, sl].bitcast(F32), ALU.subtract).then_inc(xt_lo_done, 1)

            def dequant(i):
                dve.wait_ge(s_fq, (i + 1) * 16)
                dve.wait_ge(s_fs, (i + 1) * 16)
                nc.vector.tensor_tensor(scaled(f_s[:]), scaled(f_q[:]), scaled(f_s[:]), ALU.mult).then_inc(f_w, 1)

            def dequant_down(i):
                dve.wait_ge(s_down[i % 2], (i // 2 + 1) * 32)
                nc.vector.scalar_tensor_tensor(out=f_s[:, half(i)], in0=f_q[:, half(i)], scalar=0.5, in1=f_s[:, half(i)],
                                               op0=ALU.mult, op1=ALU.mult).then_inc(f_w, 1)

            def copy_last_scales(j):
                nc.vector.tensor_copy(f_pair[:].rearrange("p r m -> p (r m)"),
                                      f_last[:, j, :]).then_inc(f_pair_done, 1)

            groups(dve, body)
            dequant(1)
            dve.wait_ge(s_flast, 16)
            copy_last_scales(0)
            x2_part(2, NT - 3)
            add_input(NT - 2)
            gather_out(NG - 1, NT - 1, NU * NC - 1)
            moments_x2(NT - 1)
            x2_part(3, NT - 4)
            x2_part(2, NT - 2)
            add_input(NT - 1)
            moments_x2(NT)
            x2_part(3, NT - 3)
            x2_part(2, NT - 1)
            x2_part(3, NT - 2)

            def whole_sums(j, n):
                k = j * 2 * NB + n
                g, up, banks = f_g[:, n % 2, :], f_u[:, n % 2, :], bank[n % 2 * 4:n % 2 * 4 + 4]
                dve.wait_ge(g_last, k + 1)
                nc.vector.tensor_tensor(g, banks[0][:], g, ALU.add).then_inc(g_sum, 1)
                dve.wait_ge(u_last, k + 1)
                nc.vector.tensor_tensor(up, banks[1][:], up, ALU.add).then_inc(u_sum, 1)

            whole_sums(0, 0)
            x2_part(3, NT - 1)

            def pair(j):
                for n, (r, b) in enumerate(hidden_parts(j)):
                    k = j * 2 * NB + n
                    if isinstance(j, int) and j == FT // 2 - 1 and n >= 2:
                        dequant_down(n - 2)
                    elif n == 2 or (n == 0 and not (isinstance(j, int) and j == 0)):
                        dequant(j * 2 + n // 2 + 1)
                    g, up = f_g[:, n % 2, :], f_u[:, n % 2, :]
                    if not (isinstance(j, int) and j == 0 and n == 0):
                        whole_sums(j, n)
                    dve.wait_ge(g_th, k + 1)
                    dve.wait_ge(g_sum, k + 1)
                    nc.vector.scalar_tensor_tensor(out=g, in0=f_th[:], scalar=1.0, in1=g, op0=ALU.add, op1=ALU.mult
                                                   ).then_inc(g_silu, 1)
                    if not (isinstance(j, int) and j == 0 and n == 0):
                        pr, pb = part_before(j, n)
                        low_half(k - 1, j * 2 + pr, pb, (n - 1) % 2)
                    dve.wait_ge(g_silu, k + 1)
                    dve.wait_ge(u_sum, k + 1)
                    nc.vector.tensor_tensor(g, up, g, ALU.mult).then_inc(hbuf_done, 1)
                    if n == 2 * NB - 1 and not (isinstance(j, int) and j == FT // 2 - 1):
                        copy_last_scales(j + 1)

            def low_half(k, i, b, slot_):
                dve.wait_ge(h_hi_done, k + 1)
                hs = (slice(None), i, slice(b * L, (b + 1) * L))
                nc.vector.tensor_tensor(h_lo[hs], f_g[:, slot_, :], h_hi[hs].bitcast(F32), ALU.subtract
                                        ).then_inc(h_lo_done, 1)

            pairs(dve, pair)
            low_half(FT * NB - 1, FT - 1, NB - 1, 1)
            def finish_x2(t):
                k = NT + 2 * t
                nc.vector.scalar_tensor_tensor(out=ln_sh[:, t:t + 1], in0=ln_mv[:, k, 0:1], scalar=-1.0, in1=ln_rs[:, k:k + 1],
                                               op0=ALU.mult, op1=ALU.mult).then_inc(shift_done, 1)
                dve.wait_ge(shift_done, t + 1)
                nc.vector.tensor_scalar(oacc[:, t, :], oacc[:, t, :], ln_sh[:, t:t + 1], None, ALU.add).then_inc(x2_done, 1)

            for i in range(2, FT):
                dequant_down(i)
                if i <= NT + 1:
                    finish_x2(i - 2)

            def shift(t):
                k = 3 * NT + t
                dve.wait_ge(rstd, k + 1)
                nc.vector.scalar_tensor_tensor(out=ln_sh[:, NT + t:NT + t + 1], in0=ln_mv[:, k, 0:1], scalar=-1.0,
                                               in1=ln_rs[:, k:k + 1], op0=ALU.mult, op1=ALU.mult).then_inc(shift_done, 1)

            def add_residual(t):
                dve.wait_ge(fin_n, t + 1)
                nc.vector.tensor_tensor(oacc[:, t, :], oacc[:, t, :], f_g[:, 1, :], ALU.add).then_inc(y_out[1], 1)

            for t in range(NT):
                dve.wait_ge(dn_mm, FT - 2 + t + 1)
                moments(3 * NT + t, bank[t][:])
                if t > 0:
                    shift(t - 1)
                if t > 2 and t % 2 == 1:
                    add_residual(t - 2)
            shift(NT - 1)
            add_residual(NT - 1)


def lay_out(a):
    import numpy as np

    w = a["L0_attn_in_proj_w"]
    gate_rows, x_rows = w[:NG * GW], w[NG * GW:2 * NG * GW]
    b_rows, c_rows = w[2 * NG * GW:2 * NG * GW + NG * NS], w[2 * NG * GW + NG * NS:2 * NG * (GW + NS)]
    dt_rows = w[-NH:]

    def tiles(rows, n):
        return rows.reshape(NG, n, P, KT, P).transpose(0, 4, 1, 3, 2)

    conv_tiles = np.concatenate([tiles(b_rows, 1), tiles(c_rows, 1), tiles(x_rows, CT)], axis=2)
    gate_tiles = tiles(gate_rows, CT)
    win = np.stack([(conv_tiles if conv else gate_tiles)[:, :, k] for conv, k in TILES], axis=2)
    wdt = np.zeros((P, KT, 3 * NH), np.float32)
    wdt[:, :, NH:2 * NH] = dt_rows.reshape(NH, KT, P).transpose(2, 1, 0)
    wo = a["L0_attn_out_proj_w"].reshape(DM, NG, CT, P).transpose(1, 3, 2, 0)

    cw, cb = a["L0_attn_conv_weight"], a["L0_attn_conv_bias"]
    conv = np.concatenate([cw, cb[:, None]], axis=1)
    cx, cB, cC = conv[:NG * GW], conv[NG * GW:NG * (GW + NS)], conv[NG * (GW + NS):]

    def by_partition(v, n):
        return v.reshape(NG, n, P, -1).transpose(2, 0, 1, 3).reshape(P, NG, -1)

    skip = np.repeat(a["L0_attn_D"], HD)
    parg = np.concatenate([by_partition(cB, 1), by_partition(cC, 1), by_partition(cx, CT), by_partition(skip, CT),
                           by_partition(a["L0_attn_norm_weight"], CT)], axis=2)
    hpar = np.tile(np.stack([a["L0_attn_dt_bias"], a["L0_attn_A_log"]], axis=1), (NB, 1))
    i = np.arange(P)
    tri = (i[:, None] <= i[None, :]).astype(np.float32)
    consts = np.stack([np.eye(P, dtype=np.float32), tri, tri * np.float32(0.25), np.ones((P, P), np.float32)], axis=1)

    gq, uq = (a[f"L0_ffn_{n}_q"].reshape(FT, P, KT, P).transpose(0, 3, 2, 1) for n in ("gate", "up"))
    gs, us = (a[f"L0_ffn_{n}_s"].reshape(FT, P, KT).transpose(0, 2, 1) for n in ("gate", "up"))
    return {
        "x": a["L0_attn_hidden_states"].reshape(T, DM),
        "win": win.reshape(NG, P, NTILE, KT * P),
        "wdt": wdt,
        "wo": wo,
        "parg": parg,
        "hpar": hpar,
        "consts": consts,
        "gu_q": np.stack([gq, uq], axis=2).reshape(FT, P, 2 * DM),
        "gu_s": np.stack([gs[:, :KS], us[:, :KS]], axis=1).reshape(FT, 2, SW),
        "gu_last": np.stack([gs[:, KS], us[:, KS]], axis=1).transpose(2, 0, 1).reshape(P, FT // 2, 4),
        "dn_q": a["L0_ffn_down_q"].reshape(DM, FT, P).transpose(1, 2, 0),
        "dn_s": a["L0_ffn_down_s"].T,
    }


def kernel(**inputs):
    import numpy as np
    import concourse.bacc as bacc
    from concourse.bass_utils import run_bass_kernel_spmd

    nc = bacc.Bacc("TRN2", target_bir_lowering=False, num_devices=1)
    arrays, args = {}, {}
    for name, v in lay_out({k: np.asarray(v) for k, v in inputs.items()}).items():
        v = np.ascontiguousarray(v)
        arrays[f"in_{name}"] = v
        args[name] = nc.dram_tensor(f"in_{name}", v.shape, mybir.dt.from_np(v.dtype), kind="ExternalInput").ap()
    out = nc.dram_tensor("out_0", (T, DM), F32, kind="ExternalOutput").ap()
    mixer_and_ffn(nc, out=out, **args)
    got = run_bass_kernel_spmd(nc, [arrays], core_ids=[0]).results[0]["out_0"]
    return got.reshape(NB, L, DM)
```
